# Optimizing a Trainium2 kernel written in Bass

```python
import numpy as np
import jax
import jax.numpy as jnp

def _softmax(x, axis=-1):
    return jax.nn.softmax(x, axis=axis)

def _gelu(x):
    return jax.nn.gelu(x, approximate=True)

def _silu(x):
    return jax.nn.silu(x)

def _sigmoid(x):
    return jax.nn.sigmoid(x)

def _layernorm(x, axis=-1, eps=1e-05):
    m = jnp.mean(x, axis=axis, keepdims=True)
    v = jnp.var(x, axis=axis, keepdims=True)
    return (x - m) / jnp.sqrt(v + eps)

def _scatter_add(tgt, idx, src, axis=0):
    return tgt.at[idx].add(src)

def _segment_sum(src, seg, n):
    return jax.ops.segment_sum(src, seg, n)
kernel_name = 'mk_early_fusion_embed_d2_tok_img768_r4_c01d93'

def setup_inputs(seed: int=0):
    np.random.seed(seed)
    _w = jnp.asarray

    def _rec_inputs():
        import jax
        import jax.numpy as jnp
        _rk = jax.random.key(seed)
        x = -0.000348323 + 0.999952 * jax.random.normal(jax.random.fold_in(_rk, 1), (16, 3, 112, 112), jnp.float32)
        x_txt = jax.random.randint(jax.random.fold_in(_rk, 51), (16, 77), 0, 30521, jnp.int32)
        mask_BS_i1_0 = jnp.where(jnp.ones((16, 77), dtype=bool), 1, 0).astype(jnp.int32)
        return (x, x_txt, mask_BS_i1_0)
    x, x_txt, mask_BS_i1_0 = _rec_inputs()

    def _L0_tok_setup():
        import jax, jax.numpy as jnp
        import numpy as np
        PATCH = 16

        def _patchify(x, p):
            B, C, H, W = x.shape
            nH, nW = (H // p, W // p)
            t = x.reshape(B, C, nH, p, nW, p)
            t = t.transpose(0, 2, 4, 3, 5, 1)
            return t.reshape(B, nH * nW, p * p * C)
        key = jax.random.key(seed)
        kx, kw = jax.random.split(key)
        B, C, H, W = (32, 3, 96, 96)
        embed_dim = 192
        in_feat = PATCH * PATCH * C * 5
        x = jax.random.normal(kx, (B, C, H, W), dtype=jnp.float32)
        Wm = jax.random.normal(kw, (embed_dim, in_feat), dtype=jnp.float32) * 0.02
        b = jnp.zeros((embed_dim,), dtype=jnp.float32)
        gamma = jnp.ones((embed_dim,), dtype=jnp.float32)
        beta = jnp.zeros((embed_dim,), dtype=jnp.float32)
        return {'x': x, 'W': Wm, 'b': b, 'gamma': gamma, 'beta': beta}
    _L0_tok_all = _L0_tok_setup()
    _L0_tok_in = {k: v for k, v in _L0_tok_all.items() if k in ('W', 'b', 'gamma', 'beta')}
    del _L0_tok_all

    def _L0_txt_setup():
        import jax, jax.numpy as jnp
        import numpy as np
        LN_EPS = 1e-12

        def _layernorm(x, gamma, beta):
            mu = jnp.mean(x, axis=-1, keepdims=True)
            var = jnp.mean(jnp.square(x - mu), axis=-1, keepdims=True)
            return (x - mu) * jax.lax.rsqrt(var + LN_EPS) * gamma + beta
        key = jax.random.key(seed)
        ks = jax.random.split(key, 6)
        B, S, V, H, P, T = (16, 128, 30522, 192, 128, 2)
        return {'input_ids': jax.random.randint(ks[0], (B, S), 0, V, dtype=jnp.int64) if jax.config.jax_enable_x64 else jax.random.randint(ks[0], (B, S), 0, V).astype(jnp.int32), 'token_type_ids': jax.random.randint(ks[1], (B, S), 0, T).astype(jnp.int32), 'word_emb': jax.random.normal(ks[2], (V, H), dtype=jnp.float32) * 0.02, 'pos_emb': jax.random.normal(ks[3], (P, H), dtype=jnp.float32) * 0.02, 'type_emb': jax.random.normal(ks[4], (T, H), dtype=jnp.float32) * 0.02, 'ln_gamma': jnp.ones((H,), dtype=jnp.float32), 'ln_beta': jnp.zeros((H,), dtype=jnp.float32)}
    _L0_txt_all = _L0_txt_setup()
    _L0_txt_in = {k: v for k, v in _L0_txt_all.items() if k in ('word_emb', 'pos_emb', 'type_emb', 'ln_gamma', 'ln_beta')}
    del _L0_txt_all

    def _L0_attn_setup():
        import jax, jax.numpy as jnp
        import numpy as np
        EPS = 0.0001
        LN_EPS = 1e-05

        def _layernorm(x, g, b):
            m = jnp.mean(x, axis=-1, keepdims=True)
            v = jnp.mean(jnp.square(x - m), axis=-1, keepdims=True)
            return (x - m) * jax.lax.rsqrt(v + LN_EPS) * g + b

        def _softmax_features(x, proj, is_query):
            d = x.shape[-1]
            xn = x * d ** (-0.25)
            u = jnp.einsum('bhnd,md->bhnm', xn, proj)
            diag = 0.5 * jnp.sum(jnp.square(xn), axis=-1, keepdims=True)
            if is_query:
                stab = jnp.max(u, axis=-1, keepdims=True)
            else:
                stab = jnp.max(u, axis=(-2, -1), keepdims=True)
            ratio = proj.shape[0] ** (-0.5)
            return ratio * (jnp.exp(u - diag - stab) + EPS)
        B, N, E, H, M, F = (4, 512, 192, 12, 64, 768)
        Dh = E // H
        key = jax.random.key(seed)
        ks = jax.random.split(key, 4)
        return {'x': jax.random.normal(ks[0], (B, N, E), jnp.float32), 'proj': jax.random.normal(ks[1], (M, Dh), jnp.float32), 'ln1_g': jnp.ones((E,), jnp.float32), 'ln1_b': jnp.zeros((E,), jnp.float32), 'ln2_g': jnp.ones((E,), jnp.float32), 'ln2_b': jnp.zeros((E,), jnp.float32), 'W1': jax.random.normal(ks[2], (E, F), jnp.float32) * 0.02, 'b1': jnp.zeros((F,), jnp.float32), 'W2': jax.random.normal(ks[3], (F, E), jnp.float32) * 0.02, 'b2': jnp.zeros((E,), jnp.float32)}
    _L0_attn_all = _L0_attn_setup()
    _L0_attn_in = {k: v for k, v in _L0_attn_all.items() if k in ('proj', 'ln1_g', 'ln1_b', 'ln2_g', 'ln2_b', 'W1', 'b1', 'W2', 'b2')}
    del _L0_attn_all

    def _L0_ffn_setup():
        import jax, jax.numpy as jnp
        import numpy as np
        H = 192
        R = 64
        E = 8
        B, S = (8, 512)
        key = jax.random.key(seed)
        ks = jax.random.split(key, 10)
        s_in = 1.0 / np.sqrt(H)
        s_r = 1.0 / np.sqrt(R)
        return {'x': jax.random.normal(ks[0], (B, S, H), dtype=jnp.float32), 'enc_w': jax.random.uniform(ks[1], (H, R), jnp.float32, -s_in, s_in), 'enc_b': jax.random.uniform(ks[2], (R,), jnp.float32, -s_in, s_in), 'sw_w': jax.random.uniform(ks[3], (R, E), jnp.float32, -s_r, s_r), 'sw_b': jax.random.uniform(ks[4], (E,), jnp.float32, -s_r, s_r), 'w1': jax.random.uniform(ks[5], (E, H, R), jnp.float32, -s_in, s_in), 'b1': jax.random.uniform(ks[6], (E, R), jnp.float32, -s_in, s_in), 'w2': jax.random.uniform(ks[7], (E, R, H), jnp.float32, -s_r, s_r), 'b2': jax.random.uniform(ks[8], (E, H), jnp.float32, -s_r, s_r)}
    _L0_ffn_all = _L0_ffn_setup()
    _L0_ffn_in = {k: v for k, v in _L0_ffn_all.items() if k in ('enc_w', 'enc_b', 'sw_w', 'sw_b', 'w1', 'b1', 'w2', 'b2')}
    del _L0_ffn_all

    def _L1_attn_setup():
        import jax, jax.numpy as jnp
        import numpy as np
        MODEL_DIM = 192
        HEADS = 12
        HEAD_DIM = MODEL_DIM // HEADS
        SEQ = 512

        def _rope_tables(seq_len, d):
            i = np.arange(d // 2, dtype=np.float64)
            theta = 10000.0 ** (-2.0 * i / d)
            m = np.arange(1, seq_len + 1, dtype=np.float64)[:, None]
            m_theta = np.repeat(m * theta[None, :], 2, axis=-1)
            return (jnp.asarray(np.cos(m_theta), jnp.float32), jnp.asarray(np.sin(m_theta), jnp.float32))

        def _shuffle(x):
            b, t, d = x.shape
            xp = x.reshape(b, t, d // 2, 2)
            xp = jnp.stack([-xp[..., 1], xp[..., 0]], axis=-1)
            return xp.reshape(b, t, d)

        def _rope(x, cos, sin):
            t = x.shape[-2]
            return x * cos[:t][None] + _shuffle(x) * sin[:t][None]
        key = jax.random.key(seed)
        kx, kq, kk, kv, ko = jax.random.split(key, 5)
        x = jax.random.normal(kx, (4, SEQ, MODEL_DIM), jnp.float32)
        std = 0.02
        W_q = jax.random.normal(kq, (MODEL_DIM, MODEL_DIM), jnp.float32) * std
        W_k = jax.random.normal(kk, (MODEL_DIM, MODEL_DIM), jnp.float32) * std
        W_v = jax.random.normal(kv, (MODEL_DIM, MODEL_DIM), jnp.float32) * std
        W_o = jax.random.normal(ko, (MODEL_DIM, MODEL_DIM), jnp.float32) * std
        return {'x': x, 'W_q': W_q, 'W_k': W_k, 'W_v': W_v, 'W_o': W_o}
    _L1_attn_all = _L1_attn_setup()
    _L1_attn_in = {k: v for k, v in _L1_attn_all.items() if k in ('W_q', 'W_k', 'W_v', 'W_o')}
    del _L1_attn_all

    def _L1_ffn_setup():
        import jax, jax.numpy as jnp
        import numpy as np
        NHEAD = 12
        EPS_Z = 1e-05
        EPS_LN = 1e-05

        def _zscore_last(t, n):
            m = t.mean(axis=-1, keepdims=True)
            var = ((t - m) ** 2).sum(axis=-1, keepdims=True) / (n - 1)
            return (t - m) / (jnp.sqrt(var) + EPS_Z)

        def _layernorm(x, g, b):
            m = x.mean(axis=-1, keepdims=True)
            v = ((x - m) ** 2).mean(axis=-1, keepdims=True)
            return (x - m) * jax.lax.rsqrt(v + EPS_LN) * g + b
        key = jax.random.key(seed)
        ks = jax.random.split(key, 20)
        B, T, D, FF, E = (2, 256, 192, 768, 4)
        p = lambda k, shape: jax.random.normal(k, shape, jnp.float32) * 0.02
        return {'src': jax.random.normal(ks[0], (B, T, D), jnp.float32), 'frac': jax.random.uniform(ks[1], (B, T), jnp.float32), 'Wq': p(ks[2], (D, D)), 'bq': jnp.zeros((D,), jnp.float32), 'Wk': p(ks[3], (D, D)), 'bk': jnp.zeros((D,), jnp.float32), 'Wv': p(ks[4], (D, D)), 'bv': jnp.zeros((D,), jnp.float32), 'Wo': p(ks[5], (D, D)), 'bo': jnp.zeros((D,), jnp.float32), 'gamma': jnp.float32(1.0), 'ln1_g': jnp.ones((D,), jnp.float32), 'ln1_b': jnp.zeros((D,), jnp.float32), 'ln2_g': jnp.ones((D,), jnp.float32), 'ln2_b': jnp.zeros((D,), jnp.float32), 'Wg': p(ks[6], (E, D)), 'bg': jnp.zeros((E,), jnp.float32), 'W1': p(ks[7], (E, D, FF)), 'b1': jnp.zeros((E, FF), jnp.float32), 'W2': p(ks[8], (E, FF, D)), 'b2': jnp.zeros((E, D), jnp.float32)}
    _L1_ffn_all = _L1_ffn_setup()
    _L1_ffn_in = {k: v for k, v in _L1_ffn_all.items() if k in ('frac', 'Wq', 'bq', 'Wk', 'bk', 'Wv', 'bv', 'Wo', 'bo', 'gamma', 'ln1_g', 'ln1_b', 'ln2_g', 'ln2_b', 'Wg', 'bg', 'W1', 'b1', 'W2', 'b2')}
    del _L1_ffn_all
    return {'x': x, 'x_txt': x_txt, 'mask_BS_i1_0': mask_BS_i1_0, 'L0_tok_W': _L0_tok_in['W'], 'L0_tok_b': _L0_tok_in['b'], 'L0_tok_gamma': _L0_tok_in['gamma'], 'L0_tok_beta': _L0_tok_in['beta'], 'L0_txt_word_emb': _L0_txt_in['word_emb'], 'L0_txt_pos_emb': _L0_txt_in['pos_emb'], 'L0_txt_type_emb': _L0_txt_in['type_emb'], 'L0_txt_ln_gamma': _L0_txt_in['ln_gamma'], 'L0_txt_ln_beta': _L0_txt_in['ln_beta'], 'L0_attn_proj': _L0_attn_in['proj'], 'L0_attn_ln1_g': _L0_attn_in['ln1_g'], 'L0_attn_ln1_b': _L0_attn_in['ln1_b'], 'L0_attn_ln2_g': _L0_attn_in['ln2_g'], 'L0_attn_ln2_b': _L0_attn_in['ln2_b'], 'L0_attn_W1': _L0_attn_in['W1'], 'L0_attn_b1': _L0_attn_in['b1'], 'L0_attn_W2': _L0_attn_in['W2'], 'L0_attn_b2': _L0_attn_in['b2'], 'L0_ffn_enc_w': _L0_ffn_in['enc_w'], 'L0_ffn_enc_b': _L0_ffn_in['enc_b'], 'L0_ffn_sw_w': _L0_ffn_in['sw_w'], 'L0_ffn_sw_b': _L0_ffn_in['sw_b'], 'L0_ffn_w1': _L0_ffn_in['w1'], 'L0_ffn_b1': _L0_ffn_in['b1'], 'L0_ffn_w2': _L0_ffn_in['w2'], 'L0_ffn_b2': _L0_ffn_in['b2'], 'L1_attn_W_q': _L1_attn_in['W_q'], 'L1_attn_W_k': _L1_attn_in['W_k'], 'L1_attn_W_v': _L1_attn_in['W_v'], 'L1_attn_W_o': _L1_attn_in['W_o'], 'L1_ffn_frac': _L1_ffn_in['frac'], 'L1_ffn_Wq': _L1_ffn_in['Wq'], 'L1_ffn_bq': _L1_ffn_in['bq'], 'L1_ffn_Wk': _L1_ffn_in['Wk'], 'L1_ffn_bk': _L1_ffn_in['bk'], 'L1_ffn_Wv': _L1_ffn_in['Wv'], 'L1_ffn_bv': _L1_ffn_in['bv'], 'L1_ffn_Wo': _L1_ffn_in['Wo'], 'L1_ffn_bo': _L1_ffn_in['bo'], 'L1_ffn_gamma': _L1_ffn_in['gamma'], 'L1_ffn_ln1_g': _L1_ffn_in['ln1_g'], 'L1_ffn_ln1_b': _L1_ffn_in['ln1_b'], 'L1_ffn_ln2_g': _L1_ffn_in['ln2_g'], 'L1_ffn_ln2_b': _L1_ffn_in['ln2_b'], 'L1_ffn_Wg': _L1_ffn_in['Wg'], 'L1_ffn_bg': _L1_ffn_in['bg'], 'L1_ffn_W1': _L1_ffn_in['W1'], 'L1_ffn_b1': _L1_ffn_in['b1'], 'L1_ffn_W2': _L1_ffn_in['W2'], 'L1_ffn_b2': _L1_ffn_in['b2']}

def reference(x, x_txt, mask_BS_i1_0, L0_tok_W, L0_tok_b, L0_tok_gamma, L0_tok_beta, L0_txt_word_emb, L0_txt_pos_emb, L0_txt_type_emb, L0_txt_ln_gamma, L0_txt_ln_beta, L0_attn_proj, L0_attn_ln1_g, L0_attn_ln1_b, L0_attn_ln2_g, L0_attn_ln2_b, L0_attn_W1, L0_attn_b1, L0_attn_W2, L0_attn_b2, L0_ffn_enc_w, L0_ffn_enc_b, L0_ffn_sw_w, L0_ffn_sw_b, L0_ffn_w1, L0_ffn_b1, L0_ffn_w2, L0_ffn_b2, L1_attn_W_q, L1_attn_W_k, L1_attn_W_v, L1_attn_W_o, L1_ffn_frac, L1_ffn_Wq, L1_ffn_bq, L1_ffn_Wk, L1_ffn_bk, L1_ffn_Wv, L1_ffn_bv, L1_ffn_Wo, L1_ffn_bo, L1_ffn_gamma, L1_ffn_ln1_g, L1_ffn_ln1_b, L1_ffn_ln2_g, L1_ffn_ln2_b, L1_ffn_Wg, L1_ffn_bg, L1_ffn_W1, L1_ffn_b1, L1_ffn_W2, L1_ffn_b2):
    import jax
    import jax.numpy as jnp

    def _L0_tok_ref(x, W, b, gamma, beta):
        import jax, jax.numpy as jnp
        import numpy as np
        PATCH = 16

        def _patchify(x, p):
            B, C, H, W = x.shape
            nH, nW = (H // p, W // p)
            t = x.reshape(B, C, nH, p, nW, p)
            t = t.transpose(0, 2, 4, 3, 5, 1)
            return t.reshape(B, nH * nW, p * p * C)
        p = PATCH
        s = p // 2
        shifts = [(0, 0), (-s, -s), (-s, s), (s, -s), (s, s)]
        pats = [_patchify(jnp.roll(x, (dx, dy), axis=(2, 3)), p) for dx, dy in shifts]
        tokens = jnp.concatenate(pats, axis=-1)
        tokens = jnp.einsum('bnf,ef->bne', tokens, W) + b
        mean = jnp.mean(tokens, axis=-1, keepdims=True)
        var = jnp.var(tokens, axis=-1, keepdims=True)
        tokens = (tokens - mean) * jax.lax.rsqrt(var + 1e-05) * gamma + beta
        return tokens

    def _L0_txt_ref(input_ids, token_type_ids, word_emb, pos_emb, type_emb, ln_gamma, ln_beta):
        import jax, jax.numpy as jnp
        import numpy as np
        LN_EPS = 1e-12

        def _layernorm(x, gamma, beta):
            mu = jnp.mean(x, axis=-1, keepdims=True)
            var = jnp.mean(jnp.square(x - mu), axis=-1, keepdims=True)
            return (x - mu) * jax.lax.rsqrt(var + LN_EPS) * gamma + beta
        B, S = input_ids.shape
        words = jnp.take(word_emb, input_ids, axis=0)
        position_ids = jnp.arange(S)
        positions = jnp.take(pos_emb, position_ids, axis=0)[None]
        types = jnp.take(type_emb, token_type_ids, axis=0)
        emb = words + positions + types
        return _layernorm(emb, ln_gamma, ln_beta)

    def _L0_attn_ref(x, proj, ln1_g, ln1_b, ln2_g, ln2_b, W1, b1, W2, b2):
        import jax, jax.numpy as jnp
        import numpy as np
        EPS = 0.0001
        LN_EPS = 1e-05

        def _layernorm(x, g, b):
            m = jnp.mean(x, axis=-1, keepdims=True)
            v = jnp.mean(jnp.square(x - m), axis=-1, keepdims=True)
            return (x - m) * jax.lax.rsqrt(v + LN_EPS) * g + b

        def _softmax_features(x, proj, is_query):
            d = x.shape[-1]
            xn = x * d ** (-0.25)
            u = jnp.einsum('bhnd,md->bhnm', xn, proj)
            diag = 0.5 * jnp.sum(jnp.square(xn), axis=-1, keepdims=True)
            if is_query:
                stab = jnp.max(u, axis=-1, keepdims=True)
            else:
                stab = jnp.max(u, axis=(-2, -1), keepdims=True)
            ratio = proj.shape[0] ** (-0.5)
            return ratio * (jnp.exp(u - diag - stab) + EPS)
        B, N, E = x.shape
        M, Dh = proj.shape
        H = E // Dh
        h = _layernorm(x, ln1_g, ln1_b)
        qkv = h.reshape(B, N, H, Dh).transpose(0, 2, 1, 3)
        q_p = _softmax_features(qkv, proj, is_query=True)
        k_p = _softmax_features(qkv, proj, is_query=False)
        k_sum = jnp.sum(k_p, axis=-2)
        d_inv = 1.0 / jnp.einsum('bhnm,bhm->bhn', q_p, k_sum)
        ctx = jnp.einsum('bhnm,bhnd->bhmd', k_p, qkv)
        attn = jnp.einsum('bhnm,bhmd,bhn->bhnd', q_p, ctx, d_inv)
        attn = attn.transpose(0, 2, 1, 3).reshape(B, N, E)
        x = x + attn
        h2 = _layernorm(x, ln2_g, ln2_b)
        h2 = jax.nn.gelu(h2 @ W1 + b1, approximate=False) @ W2 + b2
        return x + h2

    def _L0_ffn_ref(x, enc_w, enc_b, sw_w, sw_b, w1, b1, w2, b2):
        import jax, jax.numpy as jnp
        import numpy as np
        H = 192
        R = 64
        E = 8
        B, S = (8, 512)
        b, s, d = x.shape
        xt = x.reshape(-1, d)
        x_enc = xt @ enc_w + enc_b
        route_prob = jax.nn.softmax(x_enc @ sw_w + sw_b, axis=-1)
        route_prob_max = jnp.max(route_prob, axis=-1)
        routes = jnp.argmax(route_prob, axis=-1)
        onehot = jax.nn.one_hot(routes, E, dtype=xt.dtype)
        h = jnp.einsum('td,edr->ter', xt, w1) + b1[None]
        h = jax.nn.gelu(h, approximate=False)
        h = h * onehot[..., None]
        out = jnp.einsum('ter,erd->td', h, w2) + onehot @ b2
        out = out * route_prob_max[:, None]
        return out.reshape(b, s, d)

    def _L1_attn_ref(x, W_q, W_k, W_v, W_o):
        import jax, jax.numpy as jnp
        import numpy as np
        MODEL_DIM = 192
        HEADS = 12
        HEAD_DIM = MODEL_DIM // HEADS
        SEQ = 512

        def _rope_tables(seq_len, d):
            i = np.arange(d // 2, dtype=np.float64)
            theta = 10000.0 ** (-2.0 * i / d)
            m = np.arange(1, seq_len + 1, dtype=np.float64)[:, None]
            m_theta = np.repeat(m * theta[None, :], 2, axis=-1)
            return (jnp.asarray(np.cos(m_theta), jnp.float32), jnp.asarray(np.sin(m_theta), jnp.float32))

        def _shuffle(x):
            b, t, d = x.shape
            xp = x.reshape(b, t, d // 2, 2)
            xp = jnp.stack([-xp[..., 1], xp[..., 0]], axis=-1)
            return xp.reshape(b, t, d)

        def _rope(x, cos, sin):
            t = x.shape[-2]
            return x * cos[:t][None] + _shuffle(x) * sin[:t][None]
        b, t, d = x.shape
        cos, sin = _rope_tables(t, d)
        Q = _rope(x @ W_q.T, cos, sin)
        K = _rope(x @ W_k.T, cos, sin)
        V = x @ W_v.T
        Qh = Q.reshape(b, t, HEADS, HEAD_DIM)
        Kh = K.reshape(b, t, HEADS, HEAD_DIM)
        Vh = V.reshape(b, t, HEADS, HEAD_DIM)
        scores = jnp.einsum('bthd,bshd->bhts', Qh, Kh) / jnp.sqrt(jnp.float32(HEAD_DIM))
        mask = jnp.triu(jnp.ones((t, t), bool), k=1)
        scores = jnp.where(mask[None, None], -jnp.inf, scores)
        attn = jax.nn.softmax(scores, axis=-1)
        out = jnp.einsum('bhts,bshd->bthd', attn, Vh).reshape(b, t, d)
        return out @ W_o.T

    def _L1_ffn_ref(src, frac, Wq, bq, Wk, bk, Wv, bv, Wo, bo, gamma, ln1_g, ln1_b, ln2_g, ln2_b, Wg, bg, W1, b1, W2, b2):
        import jax, jax.numpy as jnp
        import numpy as np
        NHEAD = 12
        EPS_Z = 1e-05
        EPS_LN = 1e-05

        def _zscore_last(t, n):
            m = t.mean(axis=-1, keepdims=True)
            var = ((t - m) ** 2).sum(axis=-1, keepdims=True) / (n - 1)
            return (t - m) / (jnp.sqrt(var) + EPS_Z)

        def _layernorm(x, g, b):
            m = x.mean(axis=-1, keepdims=True)
            v = ((x - m) ** 2).mean(axis=-1, keepdims=True)
            return (x - m) * jax.lax.rsqrt(v + EPS_LN) * g + b
        B, T, D = src.shape
        H = NHEAD
        hd = D // H
        scale = hd ** (-0.5)
        Q = (src @ Wq.T + bq).reshape(B, T, H, hd)
        K = (src @ Wk.T + bk).reshape(B, T, H, hd)
        V = (src @ Wv.T + bv).reshape(B, T, H, hd)
        logits = jnp.einsum('bqhd,bkhd->bhqk', Q, K) * scale
        logits = gamma * _zscore_last(logits, T)
        probs = jax.nn.softmax(logits, axis=-1)
        attn = jnp.einsum('bhqk,bkhd->bqhd', probs, V).reshape(B, T, D)
        attn = attn @ Wo.T + bo
        x = _layernorm(src + attn, ln1_g, ln1_b)
        E = Wg.shape[0]
        gate_scores = jax.nn.softmax(x @ Wg.T + bg, axis=-1)
        top2_val, top2_idx = jax.lax.top_k(gate_scores, 2)
        combine = (jax.nn.one_hot(top2_idx, E, dtype=x.dtype) * top2_val[..., None]).sum(axis=-2)
        h = jax.nn.relu(jnp.einsum('btd,edf->ebtf', x, W1) + b1[:, None, None, :])
        y = jnp.einsum('ebtf,efd->ebtd', h, W2) + b2[:, None, None, :]
        ff = jnp.einsum('ebtd,bte->btd', y, combine)
        return _layernorm(x + ff, ln2_g, ln2_b)
    h = _L0_tok_ref(x, L0_tok_W, L0_tok_b, L0_tok_gamma, L0_tok_beta)
    h = jnp.concatenate([h, _L0_txt_ref(x_txt, mask_BS_i1_0, L0_txt_word_emb, L0_txt_pos_emb, L0_txt_type_emb, L0_txt_ln_gamma, L0_txt_ln_beta)], axis=1)
    h = h + _L0_attn_ref(_layernorm(h, axis=-1), L0_attn_proj, L0_attn_ln1_g, L0_attn_ln1_b, L0_attn_ln2_g, L0_attn_ln2_b, L0_attn_W1, L0_attn_b1, L0_attn_W2, L0_attn_b2)
    h = h + _L0_ffn_ref(_layernorm(h, axis=-1), L0_ffn_enc_w, L0_ffn_enc_b, L0_ffn_sw_w, L0_ffn_sw_b, L0_ffn_w1, L0_ffn_b1, L0_ffn_w2, L0_ffn_b2)
    h = h + _L1_attn_ref(_layernorm(h, axis=-1), L1_attn_W_q, L1_attn_W_k, L1_attn_W_v, L1_attn_W_o)
    h = h + _L1_ffn_ref(_layernorm(h, axis=-1), L1_ffn_frac, L1_ffn_Wq, L1_ffn_bq, L1_ffn_Wk, L1_ffn_bk, L1_ffn_Wv, L1_ffn_bv, L1_ffn_Wo, L1_ffn_bo, L1_ffn_gamma, L1_ffn_ln1_g, L1_ffn_ln1_b, L1_ffn_ln2_g, L1_ffn_ln2_b, L1_ffn_Wg, L1_ffn_bg, L1_ffn_W1, L1_ffn_b1, L1_ffn_W2, L1_ffn_b2)
    return h

_drawn_inputs = setup_inputs


def setup_inputs(seed=0):
    import zlib

    import numpy as np

    out = dict(_drawn_inputs(seed))
    spreads = {'L0_tok_b': (0.0, 0.1),
     'L0_tok_gamma': (1.0, 0.2),
     'L0_tok_beta': (0.0, 0.1),
     'L0_txt_ln_gamma': (1.0, 0.2),
     'L0_txt_ln_beta': (0.0, 0.1),
     'L0_attn_ln1_g': (1.0, 0.2),
     'L0_attn_ln1_b': (0.0, 0.1),
     'L0_attn_ln2_g': (1.0, 0.6),
     'L0_attn_ln2_b': (0.0, 0.8),
     'L0_attn_b1': (0.0, 0.606),
     'L0_attn_b2': (0.0, 0.1),
     'L1_ffn_bq': (0.0, 2.0),
     'L1_ffn_bk': (0.0, 2.0),
     'L1_ffn_bv': (0.0, 0.8),
     'L1_ffn_bo': (0.0, 0.288),
     'L1_ffn_ln1_g': (1.0, 0.2),
     'L1_ffn_ln1_b': (0.0, 0.276),
     'L1_ffn_ln2_g': (1.0, 0.2),
     'L1_ffn_ln2_b': (0.0, 0.306),
     'L1_ffn_bg': (0.0, 0.8),
     'L1_ffn_b1': (0.0, 0.8),
     'L1_ffn_b2': (0.0, 0.577)}
    factors = {'L0_ffn_enc_w': 3.403,
     'L0_ffn_enc_b': 8.0,
     'L0_ffn_sw_w': 3.429,
     'L0_ffn_sw_b': 6.687,
     'L0_ffn_w1': 3.568,
     'L0_ffn_b1': 8.0,
     'L0_ffn_w2': 3.347,
     'L0_ffn_b2': 8.0,
     'L1_attn_W_q': 8.0,
     'L1_attn_W_k': 8.0,
     'L1_attn_W_v': 4.757,
     'L1_attn_W_o': 4.42,
     'L1_ffn_Wq': 8.0,
     'L1_ffn_Wk': 8.0,
     'L1_ffn_Wv': 4.305,
     'L1_ffn_Wo': 3.125,
     'L1_ffn_Wg': 3.927,
     'L1_ffn_W1': 4.563,
     'L1_ffn_W2': 3.533}
    for name, (base, spread) in spreads.items():
        noise = np.random.default_rng([zlib.crc32(name.encode()), seed]).standard_normal(out[name].shape)
        drawn = base * np.exp(spread * noise) if base else spread * noise
        out[name] = jnp.asarray(drawn.astype(out[name].dtype))
    for name, factor in factors.items():
        out[name] = (out[name] * factor).astype(out[name].dtype)
    return out
```

```python
from contextlib import ExitStack

import concourse.bass as bass
from concourse import mybir

F32 = mybir.dt.float32
BF16 = mybir.dt.bfloat16
I32 = mybir.dt.int32
ALU = mybir.AluOpType
ACT = mybir.ActivationFunctionType
AX = mybir.AxisListType

B = 16
TI = 49
TW = 64 + 55
TT = 77
T = TI + TT
D = 192
KC = 96
NK = D // KC
HEADS = 12
HD = D // HEADS
HPC = KC // HD
M = 64
F = 768
FC = F // 128
G = 4
GT = G * T
NG = B // G
E0 = 8
R0 = 64
C0 = E0 * R0 // 128
E1 = 4
PF = 6

(V_TOKB, V_TOKG, V_TOKBETA, V_TXTG, V_TXTB, V_L1G, V_L1B, V_L2G, V_L2B, V_FB2,
 V_N1G, V_N1B, V_N2G, V_N2B) = range(14)


def program(nc, p1, tokw, ids, types, word_emb, pos_emb, type_emb, vecs, favor_bd, f_w1, f_b1, f_w2,
            enc_w, sw_w, x_w1, x_b1, x_w2, x_b2, a_w, g_w, gate_w, m_w1, m_b1, m_w2, m_b2, gamma,
            rope, ident_in, causal_in, headmask_in, expand_in, iota_in, out):
    with ExitStack() as ctx:
        def sb(name, shape, dt=F32):
            return ctx.enter_context(nc.sbuf_tensor(name, shape, dt))

        def sem(name):
            return ctx.enter_context(nc.semaphore(name))

        bank = ctx.enter_context(nc.psum_tensor("bank", [128, 8, 512], F32))

        stream = sb("stream", [T, B, D])
        x1 = sb("x1", [T, B, D])
        vec = sb("vec", [T, 14, D])
        ident = sb("ident", [128, 128])
        identb = sb("identb", [128, 128], BF16)
        causal = sb("causal", [T, 3 * T], BF16)
        headmask = sb("headmask", [KC, HPC, T])
        ropes = sb("ropes", [T, 2, D])
        iota8 = sb("iota8", [T, E0])
        expand = sb("expand", [E0, E0 * R0], BF16)
        ones = sb("ones", [HEADS, T])
        halves = sb("halves", [T, 2, B])
        xs = sb("xs", [T, G, D])
        xt = sb("xt", [KC + 1, 2, NK, T])
        ot = sb("ot", [KC + 1, 2, NK, T])
        xtg = sb("xtg", [KC + 1, NK, GT])
        gamma_sb = sb("gamma_sb", [T, 1])
        gsign = sb("gsign", [T, 1])
        gabs = sb("gabs", [T, 1])
        gneg = sb("gneg", [T, 1])
        w_bd = sb("w_bd", [KC, HPC * M])
        w_f1 = sb("w_f1", [KC, NK, F])
        w_fb1 = sb("w_fb1", [128, FC])
        w_f2 = sb("w_f2", [128, FC, D])
        w_enc = sb("w_enc", [KC + 1, NK, R0])
        w_sw = sb("w_sw", [R0 + 1, E0])
        w_x1 = sb("w_x1", [KC, NK, E0 * R0])
        w_xb1 = sb("w_xb1", [128, C0])
        w_x2 = sb("w_x2", [128, C0, D])
        w_xb2 = sb("w_xb2", [E0, D])
        w_a = sb("w_a", [KC, NK, 4 * D])
        w_g = sb("w_g", [KC + 1, NK, 4 * D])
        w_gate = sb("w_gate", [KC + 1, NK, E1])
        w_mb1 = sb("w_mb1", [128, E1, FC])
        w_mb2 = sb("w_mb2", [E1, D])
        w_m1 = sb("w_m1", [KC, E1, NK, F])
        w_m2 = sb("w_m2", [128, E1, FC, D])
        work = sb("work", [128, PF * 5 * D])
        tokw_sb = work[:].rearrange("p (c s d) -> p c s d", c=PF, s=5)
        p1_sb = sb("p1_sb", [128, 2, PF * 128])
        txt = sb("txt", [TT, B, D])
        ids_sb = sb("ids_sb", [TT, B], I32)
        types_sb = sb("types_sb", [TT, B], I32)
        pos = sb("pos", [TT, D])
        hid = work[:, 0:FC * GT].rearrange("p (f t) -> p f t", f=FC)
        acc = work[0:T, FC * GT:FC * GT + G * D].rearrange("p (t d) -> p t d", t=G)

        st = sb("st", [T, B, 6])
        mean = sb("mean", [T, B])
        rstd = sb("rstd", [T, B])
        var = sb("var", [T, B])
        msum = sb("msum", [T, B])
        mdif = sb("mdif", [T, B])

        sq = sb("sq", [T, 2, D])
        ssum = sb("ssum", [T, 2, HEADS])
        mq = sb("mq", [T, 2, HEADS])
        qsub = sb("qsub", [T, 2, HEADS])
        ksub = sb("ksub", [T, 2, HEADS])
        kmax = sb("kmax", [HEADS, 2])
        kdiag = sb("kdiag", [HEADS, 2, HEADS])
        eq = work[0:T, 0:2 * F].rearrange("p (u m) -> p u m", u=2)
        ek = work[0:T, 2 * F:4 * F].rearrange("p (u m) -> p u m", u=2)
        va = sb("va", [T, 2, HEADS, HD + 1])
        cb = sb("cb", [128, 2, HEADS // 2, 2 * (HD + 1)])
        qt_f = work[:, 4 * F:4 * F + 2 * 6 * T].rearrange("p (u n) -> p u n", u=2)
        rden = sb("rden", [T, 2, HEADS])
        at = sb("at", [T, 2, D])

        qk = work[0:T, 0:2 * 2 * D].rearrange("p (u n) -> p u n", u=2)
        qk2 = work[0:T, 768:768 + 2 * 2 * D].rearrange("p (u n) -> p u n", u=2)
        qt = sb("qt", [KC, 2, NK * T])
        kbd = xtg_big = sb("kbd", [KC, 2, HPC * T])
        pr = work[0:T, 1536:1536 + 2 * HPC * T].rearrange("p (u n) -> p u n", u=2)
        pt = work[0:T, 3072:3072 + 2 * HPC * T].rearrange("p (u n) -> p u n", u=2)
        st6 = sb("st6", [T, 2, HPC, 6])
        smax = sb("smax", [T, 2, HPC])
        nbias = sb("nbias", [T, 2, HPC])
        zscale = sb("zscale", [T, 2, HPC])
        zvar = sb("zvar", [T, 2, HPC])
        zdif = sb("zdif", [T, 2, HPC])
        zstd = sb("zstd", [T, 2, HPC])
        psums = sb("psums", [T, 2, HEADS])

        enct = sb("enct", [R0 + 1, GT])
        lg = sb("lg", [T, G, E0])
        pe_ = sb("pe_", [T, G, E0])
        hit = sb("hit", [T, G, E0])
        onehot = sb("onehot", [T, G, E0])
        one2 = sb("one2", [T, G, E0])
        gstat = sb("gstat", [T, 4, G])
        pmax = sb("pmax", [T, G])
        oht = sb("oht", [E0, GT])
        ohtb = sb("ohtb", [E0, GT], BF16)

        feps = sb("feps", [T, 1])
        mark = sb("mark", [1, 32])
        sems = {}

        def S(name):
            if name not in sems:
                sems[name] = sem(name)
            return sems[name]

        weights = [(vec[:], vecs.partition_broadcast(T)), (w_bd[:], favor_bd), (w_f1[:], f_w1), (w_fb1[:], f_b1),
                   (w_f2[:], f_w2), (w_enc[:], enc_w), (w_sw[:], sw_w), (w_x1[:], x_w1), (w_xb1[:], x_b1),
                   (w_x2[:], x_w2), (w_xb2[:], x_b2), (w_a[:], a_w), (w_g[:], g_w), (w_gate[:], gate_w),
                   (w_mb1[:], m_b1), (w_mb2[:], m_b2), (w_m1[:], m_w1), (w_m2[:], m_w2),
                   (gamma_sb[:], gamma.partition_broadcast(T)), (ropes[:], rope), (ident[:], ident_in[0]),
                   (headmask[:], headmask_in), (iota8[:], iota_in), (pos[:], pos_emb)]
        NW = len(weights)

        block = ctx.enter_context(nc.Block())

        def pair(i, u):
            return 2 * i + (u + 1)

        @block.sync
        def _(sp):
            sp.dma_start(ids_sb[:], ids).then_inc(S("ids_in"), 16)
            sp.dma_start(types_sb[:], types).then_inc(S("ids_in"), 16)
            sp.dma_start(tokw_sb, tokw).then_inc(S("tokw_in"), 16)
            for u in range(2):
                sp.dma_start(p1_sb[:, u, :], p1[u]).then_inc(S(f"p1_in{u}"), 16)
            for dst, src in weights:
                sp.dma_start(dst, src).then_inc(S("weights_in"), 16)
            with sp.Fori(0, B // 4 - 1) as i:
                for u in range(2):
                    sp.wait_ge(S("tok_mm"), pair(i, u))
                    sp.dma_start(p1_sb[:, u, :], p1[2 * i + (u + 2)]).then_inc(S(f"p1_in{u}"), 16)
            sp.wait_ge(S("tok_ready"), 8)
            for j in range(2):
                for y in range(7):
                    row = 64 * j + 8 * y
                    sp.dma_start(stream[7 * y:7 * y + 7, :, :].rearrange("p (n j) d -> p n j d", j=2)[:, :, j, :],
                                 x1[row:row + 7, 0:B // 2, :]).then_inc(S("stream_in"), 16)
            sp.wait_ge(S("txt_ready"), B)
            sp.dma_start(stream[TI:T, :, :], txt[:]).then_inc(S("stream_in"), 16)
            sp.wait_ge(S("final"), B)
            sp.dma_start(out.rearrange("b t d -> t b d"), stream[:]).then_inc(S("out_done"), 16)
            sp.wait_ge(S("out_done"), 16)

        @block.gpsimd
        def _(pool):
            nc.gpsimd.memset(ones[:], 1.0).then_inc(S("pool_const"), 1)
            nc.gpsimd.memset(feps[:], 1e-4).then_inc(S("pool_const"), 1)
            nc.gpsimd.memset(halves[:, 0, :], -0.5).then_inc(S("pool_const"), 1)
            nc.gpsimd.memset(halves[:, 1, :], 0.5).then_inc(S("pool_const"), 1)
            pool.dma_start(identb[:], ident_in[0]).then_inc(S("cast_in"), 16)
            pool.dma_start(causal[:], causal_in).then_inc(S("cast_in"), 16)
            pool.dma_start(expand[:], expand_in).then_inc(S("cast_in"), 16)
            pool.wait_ge(S("ids_in"), 32)
            for b in range(B):
                pool.indirect_dma_start(txt[:, b, :], None, word_emb, bass.IndirectOffsetOnAxis(ids_sb[:, b:b + 1], 0)).then_inc(S("words_in"), 16)
                pool.indirect_dma_start(stream[0:TT, b, :], None, type_emb, bass.IndirectOffsetOnAxis(types_sb[:, b:b + 1], 0)).then_inc(S("words_in"), 16)
            pool.wait_ge(S("pool_const"), 4)
            rs = [0]

            def inverse_deviation(P, n):
                rs[0] += 1
                pool.wait_ge(S("var_ready"), rs[0])
                nc.gpsimd.tensor_tensor(rstd[0:P, 0:n], var[0:P, 0:n], halves[0:P, 0, 0:n], ALU.pow).then_inc(S("rstd_ready"), 1)

            inverse_deviation(TT, B)
            inverse_deviation(TW, B // 2)
            inverse_deviation(T, B)
            inverse_deviation(T, B)
            with pool.Fori(0, B // 2) as i:
                for u in range(2):
                    pool.wait_ge(S("f_xs"), pair(i, u))
                    nc.gpsimd.tensor_tensor(sq[:, u, :], xs[:, u, :], xs[:, u, :], ALU.mult).then_inc(S("f_sq"), 1)
                for u in range(2):
                    pool.wait_ge(S("f_ekexp"), pair(i, u))
                    nc.gpsimd.tensor_tensor(ek[:, u, :], ek[:, u, :], feps[:].to_broadcast([T, F]), ALU.add).then_inc(S("f_ek"), 1)
            inverse_deviation(T, B)
            inverse_deviation(T, B)
            inverse_deviation(T, B)
            inverse_deviation(T, B)
            with pool.Fori(0, B // 2) as i:
                for c in range(NK):
                    for u in range(2):
                        pool.wait_ge(S("g_var"), 4 * i + (2 * c + u + 1))
                        nc.gpsimd.tensor_tensor(zstd[:, u, :], zvar[:, u, :], halves[:, 1, 0:HPC], ALU.pow).then_inc(S("g_std"), 1)
            inverse_deviation(T, B)
            with pool.Fori(0, NG) as g:
                pool.wait_ge(S("m_var"), g + 1)
                nc.gpsimd.tensor_tensor(rstd[:, 0:G], var[:, 0:G], halves[:, 0, 0:G], ALU.pow).then_inc(S("m_rstd"), 1)

        def scores(u):
            return bank[0:T, 4 * u + 1:4 * u + 3, 0:3 * T].rearrange("p k (h t) -> p k h t", t=T)

        def chunk_keys(dve, n, i, c, u):
            dve.wait_ge(S(n + "_qt"), pair(i, u))
            nc.vector.tensor_tensor(kbd[:, u, :].rearrange("p (h t) -> p h t", t=T),
                                    bank[0:KC, 4 * u, (2 + c) * T:(3 + c) * T].unsqueeze(1).to_broadcast([KC, HPC, T]),
                                    headmask[:], ALU.mult).then_inc(S(n + "_kbd"), 1)

        def copy_probs(dve, n, i, c, u):
            dve.wait_ge(S(n + "_pt"), 4 * i + (2 * c + u + 1))
            nc.vector.tensor_copy(pt[:, u, :].rearrange("p (k x) -> p k x", k=2),
                                  bank[0:T, 4 * u + 1:4 * u + 3, 0:3 * T]).then_inc(S(n + "_pts"), 1)

        def attended(dve, done, n, i, u):
            dve.wait_ge(S(n + "_pv"), pair(i, u))
            done(nc.vector.reciprocal(rden[:, u, :], psums[:, u, :]))
            nc.vector.tensor_tensor(at[:, u, :].rearrange("p (h d) -> p h d", h=HEADS),
                                    bank[0:T, 4 * u + 3, 0:D].rearrange("p (h d) -> p h d", h=HEADS),
                                    rden[:, u, :].unsqueeze(2).to_broadcast([T, HEADS, HD]), ALU.mult).then_inc(S(n + "_at"), 1)

        @block.vector
        def _(dve):
            count = {"n": 0, "i": None, "per": 0, "c": 0}

            def enter(i, per):
                count.update(i=i, per=per, c=0)

            def leave(trips):
                assert count["c"] == count["per"], count
                count.update(n=count["n"] + trips * count["per"], i=None, c=0)

            def done(ins):
                ins.then_inc(S("dve_step"), 1)
                if count["i"] is None:
                    count["n"] += 1
                    dve.wait_ge(S("dve_step"), count["n"])
                else:
                    count["c"] += 1
                    dve.wait_ge(S("dve_step"), count["i"] * count["per"] + (count["n"] + count["c"]))

            stats = [0]
            norms = [0]

            def moments(P, n, eps, chain):
                chain(nc.vector.tensor_tensor(msum[0:P, 0:n], st[0:P, 0:n, 1], st[0:P, 0:n, 4], ALU.add))
                chain(nc.vector.tensor_tensor(mdif[0:P, 0:n], st[0:P, 0:n, 1], st[0:P, 0:n, 4], ALU.subtract))
                chain(nc.vector.tensor_tensor(var[0:P, 0:n], st[0:P, 0:n, 2], st[0:P, 0:n, 5], ALU.add))
                chain(nc.vector.tensor_scalar(mean[0:P, 0:n], msum[0:P, 0:n], 0.5, None, ALU.mult))
                chain(nc.vector.scalar_tensor_tensor(mdif[0:P, 0:n], mdif[0:P, 0:n], 0.25, mdif[0:P, 0:n], ALU.mult, ALU.mult))
                chain(nc.vector.scalar_tensor_tensor(var[0:P, 0:n], var[0:P, 0:n], 1.0 / D, mdif[0:P, 0:n], ALU.mult, ALU.add))
                return nc.vector.tensor_scalar(var[0:P, 0:n], var[0:P, 0:n], eps, None, ALU.add)

            def norm_stats(P, n, src, eps):
                with dve.Fori(0, n) as b:
                    nc.vector.bn_stats(st[0:P, b, :], src[0:P, b, :]).then_inc(S("stats"), 1)
                stats[0] += n
                norms[0] += 1
                dve.wait_ge(S("stats"), stats[0])
                moments(P, n, eps, done).then_inc(S("var_ready"), 1)
                dve.wait_ge(S("rstd_ready"), norms[0])

            def normalise(dst, src, P, b):
                return nc.vector.tensor_scalar(dst, src, mean[0:P, bass.ts(b, 1)], rstd[0:P, bass.ts(b, 1)],
                                               ALU.subtract, ALU.mult)

            nc.vector.memset(xt[KC:KC + 1], 1.0).then_inc(S("dve_const"), 1)
            nc.vector.memset(ot[KC:KC + 1], 1.0).then_inc(S("dve_const"), 1)
            nc.vector.memset(xtg[KC:KC + 1], 1.0).then_inc(S("dve_const"), 1)
            nc.vector.memset(enct[R0:R0 + 1], 1.0).then_inc(S("dve_const"), 1)
            nc.vector.memset(va[:], 1.0).then_inc(S("dve_const"), 1)
            nc.vector.memset(cb[:], 0.0).then_inc(S("dve_const"), 1)
            nc.vector.memset(onehot[:], 0.0).then_inc(S("dve_const"), 1)
            for u in range(2):
                nc.vector.memset(mark[:, u:u + 1], 0.0).then_inc(S("tok_bank_free"), 1)
            dve.wait_ge(S("tokw_in"), 16)
            for shift, (c, lo, hi) in ((1, (0, 0, 128)), (1, (1, 0, 64)), (2, (1, 64, 128)), (2, (2, 0, 128)),
                                       (3, (3, 0, 128)), (3, (4, 0, 64)), (4, (4, 64, 128)), (4, (5, 0, 128))):
                w = tokw_sb[lo:hi, c, shift, :]
                nc.vector.tensor_tensor(w, w, tokw_sb[lo:hi, c, 0, :], ALU.add).then_inc(S("tokw_ready"), 1)
            dve.wait_ge(S("weights_in"), 16 * NW)
            nc.vector.tensor_scalar(w_bd[:], w_bd[:], HD ** -0.25, None, ALU.mult).then_inc(S("bd_ready"), 1)
            done(nc.vector.tensor_scalar(gneg[:], gamma_sb[:], -1.0, None, ALU.mult))
            done(nc.vector.tensor_tensor(gabs[:], gamma_sb[:], gneg[:], ALU.max))
            done(nc.vector.tensor_scalar(gsign[:], gamma_sb[:], 0.0, None, ALU.is_ge))
            done(nc.vector.tensor_scalar(gsign[:], gsign[:], 2.0, -1.0, ALU.mult, ALU.add))

            dve.wait_ge(S("words_in"), 16 * 2 * B)
            with dve.Fori(0, B) as b:
                enter(b, 2)
                done(nc.vector.tensor_tensor(txt[:, b, :], txt[:, b, :], pos[:], ALU.add))
                done(nc.vector.tensor_tensor(txt[:, b, :], txt[:, b, :], stream[0:TT, b, :], ALU.add))
                leave(B)
            norm_stats(TT, B, txt, 1e-12)
            with dve.Fori(0, B) as b:
                enter(b, 2)
                done(normalise(txt[:, b, :], txt[:, b, :], TT, b))
                done(nc.vector.tensor_tensor(txt[:, b, :], txt[:, b, :], vec[0:TT, V_TXTG, :], ALU.mult))
                nc.vector.tensor_tensor(txt[:, b, :], txt[:, b, :], vec[0:TT, V_TXTB, :], ALU.add).then_inc(S("txt_ready"), 1)
                leave(B)

            with dve.Fori(0, B // 4) as i:
                for u in range(2):
                    dve.wait_ge(S("tok_mm"), pair(i, u))
                    nc.vector.tensor_tensor(x1[0:TW, 2 * i + u, :], bank[0:TW, u, 0:D], vec[0:TW, V_TOKB, :],
                                            ALU.add).then_inc(S("tok_bank_free"), 1)
            dve.wait_ge(S("tok_bank_free"), 2 + B // 2)
            norm_stats(TW, B // 2, x1, 1e-5)
            with dve.Fori(0, B // 2) as b:
                enter(b, 2)
                done(normalise(x1[0:TW, b, :], x1[0:TW, b, :], TW, b))
                done(nc.vector.tensor_tensor(x1[0:TW, b, :], x1[0:TW, b, :], vec[0:TW, V_TOKG, :], ALU.mult))
                nc.vector.tensor_tensor(x1[0:TW, b, :], x1[0:TW, b, :], vec[0:TW, V_TOKBETA, :],
                                        ALU.add).then_inc(S("tok_ready"), 1)
                leave(B // 2)
            dve.wait_ge(S("stream_in"), 16 * 15)

            norm_stats(T, B, stream, 1e-5)
            with dve.Fori(0, B) as b:
                normalise(x1[:, b, :], stream[:, b, :], T, b).then_inc(S("f_x1"), 1)
            dve.wait_ge(S("f_x1"), B)
            norm_stats(T, B, x1, 1e-5)
            with dve.Fori(0, B // 2) as i:
                enter(i, 2 * 10)
                for u in range(2):
                    b = 2 * i + u
                    done(normalise(xs[:, u, :], x1[:, b, :], T, b))
                    done(nc.vector.tensor_tensor(xs[:, u, :], xs[:, u, :], vec[:, V_L1G, :], ALU.mult))
                    nc.vector.tensor_tensor(xs[:, u, :], xs[:, u, :], vec[:, V_L1B, :], ALU.add).then_inc(S("f_xs"), 1)
                for u in range(2):
                    dve.wait_ge(S("f_sq"), pair(i, u))
                    done(nc.vector.tensor_reduce(ssum[:, u, :], sq[:, u, :].rearrange("p (h d) -> p h d", h=HEADS), AX.X, ALU.add))
                for u in range(2):
                    feats = bank[0:T, 4 * u + 1:4 * u + 3, 0:HPC * M].rearrange("p k (h m) -> p k h m", m=M)
                    dve.wait_ge(S("f_u"), pair(i, u))
                    nc.vector.tensor_reduce(mq[:, u, :].rearrange("p (k h) -> p k h", k=2), feats, AX.X, ALU.max).then_inc(S("f_mq"), 1)
                    dve.wait_ge(S("f_mq"), pair(i, u))
                    done(nc.vector.scalar_tensor_tensor(qsub[:, u, :], ssum[:, u, :], 0.125, mq[:, u, :], ALU.mult, ALU.add))
                    nc.vector.tensor_tensor(eq[:, u, :].rearrange("p (k h m) -> p k h m", k=2, m=M), feats,
                                            qsub[:, u, :].rearrange("p (k h) -> p k h", k=2).unsqueeze(3).to_broadcast([T, 2, HPC, M]),
                                            ALU.subtract).then_inc(S("f_eq"), 1)
                for u in range(2):
                    dve.wait_ge(S("f_mqt"), pair(i, u))
                    done(nc.vector.tensor_reduce(kmax[:, u:u + 1], bank[0:HEADS, 4 * u, 256:256 + T], AX.X, ALU.max))
                    nc.vector.tensor_scalar(kdiag[:, u, :], ident[0:HEADS, 0:HEADS], kmax[:, u:u + 1], None, ALU.mult).then_inc(S("f_kd"), 1)
                for u in range(2):
                    feats = bank[0:T, 4 * u + 1:4 * u + 3, 0:HPC * M].rearrange("p k (h m) -> p k h m", m=M)
                    dve.wait_ge(S("f_kb"), pair(i, u))
                    done(nc.vector.scalar_tensor_tensor(ksub[:, u, :], ssum[:, u, :], 0.125, bank[0:T, 4 * u, 384:384 + HEADS], ALU.mult, ALU.add))
                    nc.vector.tensor_tensor(ek[:, u, :].rearrange("p (k h m) -> p k h m", k=2, m=M), feats,
                                            ksub[:, u, :].rearrange("p (k h) -> p k h", k=2).unsqueeze(3).to_broadcast([T, 2, HPC, M]),
                                            ALU.subtract).then_inc(S("f_eksub"), 1)
                for u in range(2):
                    dve.wait_ge(S("f_ctx"), pair(i, u))
                    ctxs = bank[:, 4 * u + 3, 0:6 * 34].rearrange("p (j n) -> p j n", n=34)
                    nc.vector.tensor_copy(cb[0:64, u, :, 0:17], ctxs[0:64, :, 0:17])
                    nc.vector.tensor_copy(cb[64:128, u, :, 17:34], ctxs[64:128, :, 17:34]).then_inc(S("f_cb"), 1)
                for u in range(2):
                    dve.wait_ge(S("f_qt"), pair(i, u))
                    nc.vector.tensor_scalar(qt_f[:, u, :].rearrange("p (k n) -> p k n", k=2), bank[:, 4 * u + 1:4 * u + 3, 0:3 * T],
                                            1e-4, None, ALU.add).then_inc(S("f_qts"), 1)
                for u in range(2):
                    b = 2 * i + u
                    dve.wait_ge(S("f_att"), pair(i, u))
                    att = bank[0:T, 4 * u + 3, 256:256 + 6 * 34].rearrange("p (h n) -> p h n", n=17)
                    done(nc.vector.reciprocal(rden[:, u, :], att[:, :, HD]))
                    done(nc.vector.tensor_tensor(at[:, u, :].rearrange("p (h d) -> p h d", h=HEADS), att[:, :, 0:HD],
                                                 rden[:, u, :].unsqueeze(2).to_broadcast([T, HEADS, HD]), ALU.mult))
                    done(nc.vector.tensor_tensor(x1[:, b, :], x1[:, b, :], at[:, u, :], ALU.add))
                    done(nc.vector.tensor_tensor(stream[:, b, :], stream[:, b, :], x1[:, b, :], ALU.add))
                leave(B // 2)

            norm_stats(T, B, x1, 1e-5)

            def group_vec(k):
                return vec[:, k, :].unsqueeze(1).to_broadcast([T, G, D])

            with dve.Fori(0, NG) as g:
                enter(g, 4 + 1 + 8)
                for t in range(G):
                    b = 4 * g + t
                    done(normalise(xs[:, t, :], x1[:, b, :], T, b))
                done(nc.vector.tensor_tensor(xs[:], xs[:], group_vec(V_L2G), ALU.mult))
                nc.vector.tensor_tensor(xs[:], xs[:], group_vec(V_L2B), ALU.add).then_inc(S("g_xs"), 1)
                for t in range(G):
                    b = 4 * g + t
                    dve.wait_ge(S("n_y"), 4 * g + (t + 1))
                    done(nc.vector.tensor_tensor(at[:, t % 2, :], bank[0:T, 4 + t, 0:D], vec[:, V_FB2, :], ALU.add))
                    done(nc.vector.tensor_tensor(stream[:, b, :], stream[:, b, :], at[:, t % 2, :], ALU.add))
                leave(NG)

            def first_of(dst, values, top):
                n = values.shape[2]
                dve_top = gstat[:, top, :].unsqueeze(2).to_broadcast([T, G, n])
                done(nc.vector.tensor_reduce(gstat[:, top, :], values, AX.X, ALU.max))
                done(nc.vector.tensor_tensor(hit[:, :, 0:n], values, dve_top, ALU.is_ge))
                done(nc.vector.tensor_tensor(hit[:, :, 0:n], hit[:, :, 0:n], iota8[:, 0:n].unsqueeze(1).to_broadcast([T, G, n]), ALU.mult))
                done(nc.vector.tensor_reduce(gstat[:, 3, :], hit[:, :, 0:n], AX.X, ALU.min))
                return nc.vector.tensor_tensor(dst, hit[:, :, 0:n], gstat[:, 3, :].unsqueeze(2).to_broadcast([T, G, n]), ALU.is_equal)

            def softmax(n, logits, name, k):
                done(nc.vector.tensor_reduce(gstat[:, 0, :], logits, AX.X, ALU.max))
                nc.vector.tensor_tensor(lg[:, :, 0:n], logits, gstat[:, 0, :].unsqueeze(2).to_broadcast([T, G, n]),
                                        ALU.subtract).then_inc(S(name + "_lg"), 1)
                dve.wait_ge(S(name + "_exp"), k)
                done(nc.vector.tensor_reduce(gstat[:, 1, :], lg[:, :, 0:n], AX.X, ALU.add))
                done(nc.vector.reciprocal(gstat[:, 1, :], gstat[:, 1, :]))
                done(nc.vector.tensor_tensor(pe_[:, :, 0:n], lg[:, :, 0:n], gstat[:, 1, :].unsqueeze(2).to_broadcast([T, G, n]), ALU.mult))

            norm_stats(T, B, stream, 1e-5)
            with dve.Fori(0, NG) as g:
                enter(g, 4 + 4 + 4 + 1 + 4)
                for t in range(G):
                    b = 4 * g + t
                    ins = normalise(xs[:, t, :], stream[:, b, :], T, b)
                    if t < G - 1:
                        done(ins)
                ins.then_inc(S("x_xs"), 1)
                dve.wait_ge(S("x_logits"), g + 1)
                softmax(E0, bank[0:T, 3, 0:G * E0].rearrange("p (t e) -> p t e", e=E0), "x", g + 1)
                first_of(onehot[:], pe_[:], 2).then_inc(S("x_onehot"), 1)
                done(nc.vector.tensor_copy(pmax[:], gstat[:, 2, :]))
                dve.wait_ge(S("x_oht"), g + 1)
                done(nc.vector.tensor_copy(oht[:], bank[0:E0, 3, 0:GT]))
                nc.vector.tensor_copy(ohtb[:], bank[0:E0, 3, 0:GT]).then_inc(S("x_ohts"), 1)
                for c in range(C0):
                    dve.wait_ge(S("x_hid"), C0 * g + (c + 1))
                    dve.wait_ge(S("x_mask"), C0 * g + (c + 1))
                    nc.vector.tensor_tensor(hid[:, c, :], hid[:, c, :], bank[:, c % 2, 0:GT], ALU.mult).then_inc(S("x_masked"), 1)
                for t in range(G):
                    b = 4 * g + t
                    dve.wait_ge(S("x_y"), 4 * g + (t + 1))
                    done(nc.vector.scalar_tensor_tensor(stream[:, b, :], bank[0:T, 4 + t, 0:D], pmax[:, t:t + 1], stream[:, b, :], ALU.mult, ALU.add))
                leave(NG)

            norm_stats(T, B, stream, 1e-5)
            with dve.Fori(0, B // 2) as i:
                enter(i, 2 * (3 + 2 * 1 + 1 + 1))
                for u in range(2):
                    b = 2 * i + u
                    normalise(xs[:, u, :], stream[:, b, :], T, b).then_inc(S("a_xs"), 1)
                for u in range(2):
                    dve.wait_ge(S("a_qkv"), pair(i, u))
                    raw = bank[0:T, 4 * u + 1, 0:2 * D].rearrange("p (a d) -> p a d", a=2)
                    raw2 = bank[0:T, 4 * u + 1, 0:2 * D].rearrange("p (n r) -> p n r", r=2)
                    sw = qk2[:, u, :].rearrange("p (n r) -> p n r", r=2)
                    sine = ropes[:, 1, :]
                    done(nc.vector.tensor_tensor(qk[:, u, :].rearrange("p (a d) -> p a d", a=2), raw,
                                                 ropes[:, 0, :].unsqueeze(1).to_broadcast([T, 2, D]), ALU.mult))
                    done(nc.vector.tensor_copy(sw[:, :, 0], raw2[:, :, 1]))
                    nc.vector.tensor_copy(sw[:, :, 1], raw2[:, :, 0]).then_inc(S("a_swap"), 1)
                    dve.wait_ge(S("a_swap"), pair(i, u))
                    done(nc.vector.tensor_tensor(qk2[:, u, :].rearrange("p (a d) -> p a d", a=2), qk2[:, u, :].rearrange("p (a d) -> p a d", a=2),
                                                 sine.unsqueeze(1).to_broadcast([T, 2, D]), ALU.mult))
                    nc.vector.tensor_tensor(qk[:, u, :], qk[:, u, :], qk2[:, u, :], ALU.add).then_inc(S("a_qk"), 1)
                for c in range(NK):
                    for u in range(2):
                        chunk_keys(dve, "a", i, c, u)
                    for u in range(2):
                        v = 4 * i + (2 * c + u + 1)
                        dve.wait_ge(S("a_s"), v)
                        done(nc.vector.tensor_reduce(smax[:, u, :].rearrange("p (k h) -> p k h", k=2), scores(u), AX.X, ALU.max))
                        nc.vector.tensor_scalar(nbias[:, u, :], smax[:, u, :], -0.25, None, ALU.mult).then_inc(S("a_bias"), 1)
                    for u in range(2):
                        copy_probs(dve, "a", i, c, u)
                for u in range(2):
                    attended(dve, done, "a", i, u)
                for u in range(2):
                    b = 2 * i + u
                    dve.wait_ge(S("a_o"), pair(i, u))
                    done(nc.vector.tensor_tensor(stream[:, b, :], stream[:, b, :], bank[0:T, 4 * u + 3, 256:256 + D], ALU.add))
                leave(B // 2)

            norm_stats(T, B, stream, 1e-5)
            with dve.Fori(0, B // 2) as i:
                enter(i, 2 * (1 + 2 * 8 + 1))
                for u in range(2):
                    b = 2 * i + u
                    normalise(xs[:, u, :], stream[:, b, :], T, b).then_inc(S("g_xs2"), 1)
                for u in range(2):
                    dve.wait_ge(S("g_qkv"), pair(i, u))
                    nc.vector.tensor_scalar(qk[:, u, 0:D], bank[0:T, 4 * u + 1, 0:D], gsign[:, 0:1], None, ALU.mult)
                    nc.vector.tensor_copy(qk[:, u, D:2 * D], bank[0:T, 4 * u + 1, D:2 * D]).then_inc(S("g_qk"), 1)
                for c in range(NK):
                    for u in range(2):
                        chunk_keys(dve, "g", i, c, u)
                    for u in range(2):
                        v = 4 * i + (2 * c + u + 1)
                        dve.wait_ge(S("g_s"), v)
                        for h in range(HPC):
                            nc.vector.bn_stats(st6[:, u, h, :], bank[0:T, 4 * u + 1 + h // 3, (h % 3) * T:(h % 3 + 1) * T])
                        done(nc.vector.tensor_reduce(smax[:, u, :].rearrange("p (k h) -> p k h", k=2), scores(u), AX.X, ALU.max))
                        done(nc.vector.tensor_tensor(zdif[:, u, :], st6[:, u, :, 1], st6[:, u, :, 4], ALU.subtract))
                        done(nc.vector.tensor_tensor(zvar[:, u, :], st6[:, u, :, 2], st6[:, u, :, 5], ALU.add))
                        done(nc.vector.scalar_tensor_tensor(zdif[:, u, :], zdif[:, u, :], T / 4.0, zdif[:, u, :], ALU.mult, ALU.mult))
                        done(nc.vector.tensor_tensor(zvar[:, u, :], zvar[:, u, :], zdif[:, u, :], ALU.add))
                        nc.vector.tensor_scalar(zvar[:, u, :], zvar[:, u, :], 1.0 / (HD * (T - 1)), None, ALU.mult).then_inc(S("g_var"), 1)
                    for u in range(2):
                        v = 4 * i + (2 * c + u + 1)
                        dve.wait_ge(S("g_std"), v)
                        done(nc.vector.tensor_scalar(zstd[:, u, :], zstd[:, u, :], 1e-5, None, ALU.add))
                        done(nc.vector.reciprocal(zscale[:, u, :], zstd[:, u, :]))
                        done(nc.vector.tensor_scalar(zscale[:, u, :], zscale[:, u, :], gabs[:, 0:1], HD ** -0.5, ALU.mult, ALU.mult))
                        nc.vector.scalar_tensor_tensor(nbias[:, u, :], smax[:, u, :], -1.0, zscale[:, u, :], ALU.mult, ALU.mult).then_inc(S("g_bias"), 1)
                    for u in range(2):
                        copy_probs(dve, "g", i, c, u)
                for u in range(2):
                    attended(dve, done, "g", i, u)
                for u in range(2):
                    b = 2 * i + u
                    dve.wait_ge(S("g_o"), pair(i, u))
                    done(nc.vector.tensor_tensor(x1[:, b, :], xs[:, u, :], bank[0:T, 4 * u + 3, 256:256 + D], ALU.add))
                leave(B // 2)

            norm_stats(T, B, x1, 1e-5)
            with dve.Fori(0, NG) as g:
                enter(g, 4 + 1 + 4 + 5 + 1 + 5 + 1 + 1 + 6 + 4 + 1 + 1)
                for t in range(G):
                    b = 4 * g + t
                    done(normalise(xs[:, t, :], x1[:, b, :], T, b))
                done(nc.vector.tensor_tensor(xs[:], xs[:], group_vec(V_N1G), ALU.mult))
                nc.vector.tensor_tensor(xs[:], xs[:], group_vec(V_N1B), ALU.add).then_inc(S("m_xs"), 1)
                dve.wait_ge(S("m_logits"), g + 1)
                softmax(E1, bank[0:T, 1, 0:G * E1].rearrange("p (t e) -> p t e", e=E1), "m", g + 1)
                p4, o1, o2 = pe_[:, :, 0:E1], onehot[:, :, 0:E1], one2[:, :, 0:E1]
                done(first_of(o1, p4, 2))
                done(nc.vector.scalar_tensor_tensor(lg[:, :, 0:E1], o1, -2.0, p4, ALU.mult, ALU.add))
                done(first_of(o2, lg[:, :, 0:E1], 2))
                done(nc.vector.tensor_tensor(o1, o1, o2, ALU.add))
                nc.vector.tensor_tensor(pe_[:, :, E1:2 * E1], o1, p4, ALU.mult).then_inc(S("m_comb"), 1)
                dve.wait_ge(S("m_combt"), g + 1)
                nc.vector.tensor_copy(oht[0:E1, :], bank[0:E1, 1, 0:GT]).then_inc(S("m_combts"), 1)
                for t in range(G):
                    dve.wait_ge(S("m_b2"), 4 * g + (t + 1))
                    nc.vector.tensor_tensor(acc[:, t, :], xs[:, t, :], bank[0:T, 4 + t, 256:256 + D], ALU.add).then_inc(S("m_acc"), 1)
                for e in range(E1):
                    for t in range(G):
                        dve.wait_ge(S("m_y"), 16 * g + (4 * e + t + 1))
                        dve.wait_ge(S("m_acc"), 20 * g + (4 * e + t + 1))
                        nc.vector.scalar_tensor_tensor(acc[:, t, :], bank[0:T, 4 + t, 0:D], pe_[:, t, E1 + e:E1 + e + 1],
                                                       acc[:, t, :], ALU.mult, ALU.add).then_inc(S("m_acc"), 1)
                dve.wait_ge(S("m_acc"), 20 * g + 20)
                for t in range(G):
                    ins = nc.vector.bn_stats(st[:, t, :], acc[:, t, :])
                done(ins)
                moments(T, G, 1e-5, done).then_inc(S("m_var"), 1)
                dve.wait_ge(S("m_rstd"), g + 1)
                for t in range(G):
                    done(nc.vector.tensor_scalar(xs[:, t, :], acc[:, t, :], mean[:, t:t + 1], rstd[:, t:t + 1], ALU.subtract, ALU.mult))
                done(nc.vector.tensor_tensor(xs[:], xs[:], group_vec(V_N2G), ALU.mult))
                done(nc.vector.tensor_tensor(xs[:], xs[:], group_vec(V_N2B), ALU.add))
                for t in range(G):
                    nc.vector.tensor_tensor(stream[:, 4 * g + t, :], stream[:, 4 * g + t, :], xs[:, t, :], ALU.add).then_inc(S("final"), 1)
                dve.wait_ge(S("final"), G * g + G)
                leave(NG)


        @block.scalar
        def _(act):
            act.wait_ge(S("weights_in"), 16 * NW)
            act.wait_ge(S("dve_const"), 7)

            def pair_tokens(xs_ready, xt_mm, xt_ready, i):
                for u in range(2):
                    act.wait_ge(S(xt_mm), pair(i, u))
                    nc.scalar.copy(xt[0:KC, u, :, :], bank[0:KC, 4 * u, 0:NK * T].rearrange("p (c t) -> p c t", c=NK)).then_inc(S(xt_ready), 1)

            def group_tokens(name, g):
                act.wait_ge(S(name + "_xtmm"), g + 1)
                nc.scalar.copy(xtg[0:KC, :, :], bank[0:KC, 0:2, 0:GT]).then_inc(S(name + "_xt"), 1)

            with act.Fori(0, B // 2) as i:
                for u in range(2):
                    act.wait_ge(S("f_xtmm"), pair(i, u))
                    nc.scalar.copy(xt[0:KC, u, :, :], bank[0:KC, 4 * u, 0:NK * T].rearrange("p (c t) -> p c t", c=NK)).then_inc(S("f_xt"), 1)
                for u in range(2):
                    act.wait_ge(S("f_xs"), pair(i, u))
                    nc.scalar.copy(va[:, u, :, 0:HD], xs[:, u, :].rearrange("p (h d) -> p h d", h=HEADS)).then_inc(S("f_va"), 1)
                for u in range(2):
                    act.wait_ge(S("f_eq"), pair(i, u))
                    nc.scalar.activation(eq[:, u, :], eq[:, u, :], ACT.Exp).then_inc(S("f_eqexp"), 1)
                for u in range(2):
                    act.wait_ge(S("f_eksub"), pair(i, u))
                    nc.scalar.activation(ek[:, u, :], ek[:, u, :], ACT.Exp).then_inc(S("f_ekexp"), 1)

            with act.Fori(0, NG) as g:
                group_tokens("n", g)
                for f in range(FC):
                    act.wait_ge(S("n_hmm"), FC * g + (f + 1))
                    nc.scalar.activation(hid[:, f, :], bank[:, 2 + f % 2, 0:GT], ACT.Gelu, bias=w_fb1[:, f:f + 1]).then_inc(S("n_hid"), 1)

            with act.Fori(0, NG) as g:
                group_tokens("x", g)
                act.wait_ge(S("x_encmm"), g + 1)
                nc.scalar.copy(enct[0:R0, :], bank[0:R0, 2, 0:GT]).then_inc(S("x_enc"), 1)
                act.wait_ge(S("x_lg"), g + 1)
                nc.scalar.activation(lg[:], lg[:], ACT.Exp).then_inc(S("x_exp"), 1)
                for c in range(C0):
                    act.wait_ge(S("x_hmm"), C0 * g + (c + 1))
                    nc.scalar.activation(hid[:, c, :], bank[:, 2, 0:GT], ACT.Gelu, bias=w_xb1[:, c:c + 1]).then_inc(S("x_hid"), 1)

            def attention(n, i):
                for u in range(2):
                    act.wait_ge(S(n + "_xtmm"), pair(i, u))
                    nc.scalar.copy(xt[0:KC, u, :, :], bank[0:KC, 4 * u, 0:NK * T].rearrange("p (c t) -> p c t", c=NK)).then_inc(S(n + "_xt"), 1)
                for u in range(2):
                    act.wait_ge(S(n + "_qkv"), pair(i, u))
                    nc.scalar.copy(sq[:, u, :], bank[0:T, 4 * u + 2, 0:D]).then_inc(S(n + "_v"), 1)
                for u in range(2):
                    act.wait_ge(S(n + "_qkt"), pair(i, u))
                    nc.scalar.copy(qt[:, u, :], bank[0:KC, 4 * u, 0:NK * T]).then_inc(S(n + "_qt"), 1)
                for c in range(NK):
                    for u in range(2):
                        act.wait_ge(S(n + "_bias"), 4 * i + (2 * c + u + 1))
                        for h in range(HPC):
                            scale = 0.25 if n == "a" else zscale[:, u, h:h + 1]
                            ins = nc.scalar.activation(pr[:, u, h * T:(h + 1) * T], bank[0:T, 4 * u + 1 + h // 3, (h % 3) * T:(h % 3 + 1) * T],
                                                       ACT.Exp, bias=nbias[:, u, h:h + 1], scale=scale,
                                                       accum_out=psums[:, u, HPC * c + h:HPC * c + h + 1])
                        ins.then_inc(S(n + "_p"), 1)
                for u in range(2):
                    act.wait_ge(S(n + "_otmm"), pair(i, u))
                    nc.scalar.copy(ot[0:KC, u, :, :], bank[0:KC, 4 * u, 0:NK * T].rearrange("p (c t) -> p c t", c=NK)).then_inc(S(n + "_ot"), 1)

            with act.Fori(0, B // 2) as i:
                attention("a", i)
            with act.Fori(0, B // 2) as i:
                attention("g", i)

            with act.Fori(0, NG) as g:
                group_tokens("m", g)
                act.wait_ge(S("m_lg"), g + 1)
                nc.scalar.activation(lg[:, :, 0:E1], lg[:, :, 0:E1], ACT.Exp).then_inc(S("m_exp"), 1)
                for e in range(E1):
                    for f in range(FC):
                        act.wait_ge(S("m_hmm"), E1 * FC * g + (FC * e + f + 1))
                        nc.scalar.activation(hid[:, f, :], bank[:, 2 + f % 2, 0:GT], ACT.Relu, bias=w_mb1[:, e, f:f + 1]).then_inc(S("m_hid"), 1)

        @block.tensor
        def _(pe):
            mm = nc.tensor.matmul
            pe.wait_ge(S("weights_in"), 16 * NW)
            pe.wait_ge(S("tokw_ready"), 8)
            pe.wait_ge(S("dve_const"), 7)
            pe.wait_ge(S("pool_const"), 4)
            pe.wait_ge(S("cast_in"), 48)

            with pe.Fori(0, B // 4) as i:
                for u in range(2):
                    pe.wait_ge(S(f"p1_in{u}"), 16 * i + 16)
                    pe.wait_ge(S("tok_bank_free"), pair(i, u))
                    grid = p1_sb[:, u, :].rearrange("p (c n) -> p c n", c=PF)
                    n = 0
                    for c in range(PF):
                        for shift, (dy, dx) in enumerate(((1, 1), (1, 0), (0, 1), (0, 0))):
                            at_ = 8 * dy + dx
                            ins = mm(bank[0:TW, u, 0:D], grid[:, c, at_:at_ + TW], tokw_sb[:, c, 1 + shift, :],
                                     start=(n == 0), stop=(n == PF * 4 - 1))
                            n += 1
                    ins.then_inc(S("tok_mm"), 1)

            def transpose_pair(name, ready, i, src):
                for u in range(2):
                    pe.wait_ge(S(ready), pair(i, u))
                    for c in range(NK):
                        ins = nc.tensor.transpose(bank[0:KC, 4 * u, c * T:(c + 1) * T], src[:, u, c * KC:(c + 1) * KC], ident[0:T, 0:T])
                    ins.then_inc(S(name), 1)

            def transpose_group(name, g):
                pe.wait_ge(S(name + "_xs" if name != "n" else "g_xs"), g + 1)
                for c in range(NK):
                    for t in range(G):
                        ins = nc.tensor.transpose(bank[0:KC, c, t * T:(t + 1) * T], xs[:, t, c * KC:(c + 1) * KC], ident[0:T, 0:T])
                ins.then_inc(S(name + "_xtmm"), 1)
                pe.wait_ge(S(name + "_xt"), g + 1)

            pe.wait_ge(S("bd_ready"), 1)
            with pe.Fori(0, B // 2) as i:
                transpose_pair("f_xtmm", "f_xs", i, xs)
                for u in range(2):
                    pe.wait_ge(S("f_xt"), pair(i, u))
                    for c in range(NK):
                        ins = mm(bank[0:T, 4 * u + 1 + c, 0:HPC * M], xt[0:KC, u, c, :], w_bd[:], start=True, stop=True)
                    ins.then_inc(S("f_u"), 1)
                for u in range(2):
                    pe.wait_ge(S("f_mq"), pair(i, u))
                    nc.tensor.transpose(bank[0:HEADS, 4 * u, 256:256 + T], mq[:, u, :], ident[0:T, 0:T]).then_inc(S("f_mqt"), 1)
                for u in range(2):
                    pe.wait_ge(S("f_kd"), pair(i, u))
                    mm(bank[0:T, 4 * u, 384:384 + HEADS], ones[:], kdiag[:, u, :], start=True, stop=True).then_inc(S("f_kb"), 1)
                for u in range(2):
                    pe.wait_ge(S("f_ek"), pair(i, u))
                    pe.wait_ge(S("f_va"), pair(i, u))
                    for j in range(6):
                        ins = mm(bank[:, 4 * u + 3, j * 34:(j + 1) * 34], ek[:, u, j * 128:(j + 1) * 128],
                                 va[:, u, 2 * j:2 * j + 2, :].rearrange("p a b -> p (a b)"), start=True, stop=True)
                    ins.then_inc(S("f_ctx"), 1)
                for u in range(2):
                    pe.wait_ge(S("f_eqexp"), pair(i, u))
                    for j in range(6):
                        ins = nc.tensor.transpose(bank[:, 4 * u + 1 + j // 3, (j % 3) * T:(j % 3 + 1) * T], eq[:, u, j * 128:(j + 1) * 128], ident[0:T, 0:T])
                    ins.then_inc(S("f_qt"), 1)
                for u in range(2):
                    pe.wait_ge(S("f_cb"), pair(i, u))
                    pe.wait_ge(S("f_qts"), pair(i, u))
                    for j in range(6):
                        ins = mm(bank[0:T, 4 * u + 3, 256 + j * 34:256 + (j + 1) * 34], qt_f[:, u, j * T:(j + 1) * T], cb[:, u, j, :], start=True, stop=True)
                    ins.then_inc(S("f_att"), 1)

            with pe.Fori(0, NG) as g:
                transpose_group("n", g)
                for f in range(FC):
                    if f >= 2:
                        pe.wait_ge(S("n_hid"), FC * g + (f - 1))
                    for c in range(NK):
                        ins = mm(bank[:, 2 + f % 2, 0:GT], w_f1[:, c, f * 128:(f + 1) * 128], xtg[0:KC, c, :], start=(c == 0), stop=(c == NK - 1))
                    ins.then_inc(S("n_hmm"), 1)
                pe.wait_ge(S("n_hid"), FC * g + FC)
                for t in range(G):
                    for f in range(FC):
                        ins = mm(bank[0:T, 4 + t, 0:D], hid[:, f, t * T:(t + 1) * T], w_f2[:, f, :], start=(f == 0), stop=(f == FC - 1))
                    ins.then_inc(S("n_y"), 1)

            with pe.Fori(0, NG) as g:
                transpose_group("x", g)
                for c in range(NK):
                    kc = KC + (c == NK - 1)
                    ins = mm(bank[0:R0, 2, 0:GT], w_enc[0:kc, c, :], xtg[0:kc, c, :], start=(c == 0), stop=(c == NK - 1))
                ins.then_inc(S("x_encmm"), 1)
                pe.wait_ge(S("x_enc"), g + 1)
                for t in range(G):
                    ins = mm(bank[0:T, 3, t * E0:(t + 1) * E0], enct[:, t * T:(t + 1) * T], w_sw[:], start=True, stop=True)
                ins.then_inc(S("x_logits"), 1)
                pe.wait_ge(S("x_onehot"), g + 1)
                for t in range(G):
                    ins = nc.tensor.transpose(bank[0:E0, 3, t * T:(t + 1) * T], onehot[:, t, :], ident[0:T, 0:T])
                ins.then_inc(S("x_oht"), 1)
                pe.wait_ge(S("x_ohts"), g + 1)
                for k in range(C0):
                    if k >= 1:
                        pe.wait_ge(S("x_hid"), C0 * g + k)
                    for c in range(NK):
                        ins = mm(bank[:, 2, 0:GT], w_x1[:, c, k * 128:(k + 1) * 128], xtg[0:KC, c, :], start=(c == 0), stop=(c == NK - 1))
                    ins.then_inc(S("x_hmm"), 1)
                    if k >= 2:
                        pe.wait_ge(S("x_masked"), C0 * g + (k - 1))
                    mm(bank[:, k % 2, 0:GT], expand[:, k * 128:(k + 1) * 128], ohtb[:], start=True, stop=True).then_inc(S("x_mask"), 1)
                pe.wait_ge(S("x_masked"), C0 * g + C0)
                for t in range(G):
                    for k in range(C0):
                        mm(bank[0:T, 4 + t, 0:D], hid[:, k, t * T:(t + 1) * T], w_x2[:, k, :], start=(k == 0), stop=False)
                    mm(bank[0:T, 4 + t, 0:D], oht[:, t * T:(t + 1) * T], w_xb2[:], start=False, stop=True).then_inc(S("x_y"), 1)

            def attention(n, w, i):
                transpose_pair(n + "_xtmm", "a_xs" if n == "a" else "g_xs2", i, xs)
                for u in range(2):
                    pe.wait_ge(S(n + "_xt"), pair(i, u))
                    for col, width, k in ((0, 2 * D, 1), (2 * D, D, 2)):
                        for c in range(NK):
                            kc = KC + (c == NK - 1 and n == "g")
                            ins = mm(bank[0:T, 4 * u + k, 0:width], xt[0:kc, u, c, :], w[0:kc, c, col:col + width], start=(c == 0), stop=(c == NK - 1))
                    ins.then_inc(S(n + "_qkv"), 1)
                for u in range(2):
                    pe.wait_ge(S(n + "_qk"), pair(i, u))
                    for j in range(2 * NK):
                        ins = nc.tensor.transpose(bank[0:KC, 4 * u, j * T:(j + 1) * T], qk[:, u, j * KC:(j + 1) * KC], ident[0:T, 0:T])
                    ins.then_inc(S(n + "_qkt"), 1)
                for c in range(NK):
                    for u in range(2):
                        v = 4 * i + (2 * c + u + 1)
                        pe.wait_ge(S(n + "_kbd"), v)
                        if c == 0:
                            pe.wait_ge(S(n + "_qt"), pair(i, u))
                            pe.wait_ge(S(n + "_v"), pair(i, u))
                        for k in range(2):
                            ins = mm(bank[0:T, 4 * u + 1 + k, 0:3 * T], qt[:, u, c * T:(c + 1) * T], kbd[:, u, k * 3 * T:(k + 1) * 3 * T],
                                     start=True, stop=(n == "g"))
                            if n == "a":
                                ins = mm(bank[0:T, 4 * u + 1 + k, 0:3 * T], identb[0:T, 0:T], causal[:], start=False, stop=True)
                        ins.then_inc(S(n + "_s"), 1)
                    for u in range(2):
                        pe.wait_ge(S(n + "_p"), 4 * i + (2 * c + u + 1))
                        for h in range(HPC):
                            ins = nc.tensor.transpose(bank[0:T, 4 * u + 1 + h // 3, (h % 3) * T:(h % 3 + 1) * T], pr[:, u, h * T:(h + 1) * T], ident[0:T, 0:T])
                        ins.then_inc(S(n + "_pt"), 1)
                    for u in range(2):
                        pe.wait_ge(S(n + "_pts"), 4 * i + (2 * c + u + 1))
                        for h in range(HPC):
                            col = (HPC * c + h) * HD
                            ins = mm(bank[0:T, 4 * u + 3, col:col + HD], pt[:, u, h * T:(h + 1) * T], sq[:, u, col:col + HD], start=True, stop=True)
                        if c == NK - 1:
                            ins.then_inc(S(n + "_pv"), 1)
                transpose_pair(n + "_otmm", n + "_at", i, at)
                for u in range(2):
                    pe.wait_ge(S(n + "_ot"), pair(i, u))
                    for c in range(NK):
                        kc = KC + (c == NK - 1 and n == "g")
                        ins = mm(bank[0:T, 4 * u + 3, 256:256 + D], ot[0:kc, u, c, :], w[0:kc, c, 3 * D:4 * D], start=(c == 0), stop=(c == NK - 1))
                    ins.then_inc(S(n + "_o"), 1)

            with pe.Fori(0, B // 2) as i:
                attention("a", w_a, i)
            with pe.Fori(0, B // 2) as i:
                attention("g", w_g, i)

            with pe.Fori(0, NG) as g:
                transpose_group("m", g)
                for t in range(G):
                    for c in range(NK):
                        kc = KC + (c == NK - 1)
                        ins = mm(bank[0:T, 1, t * E1:(t + 1) * E1], xtg[0:kc, c, t * T:(t + 1) * T], w_gate[0:kc, c, :],
                                 start=(c == 0), stop=(c == NK - 1))
                ins.then_inc(S("m_logits"), 1)
                pe.wait_ge(S("m_comb"), g + 1)
                for t in range(G):
                    ins = nc.tensor.transpose(bank[0:E1, 1, t * T:(t + 1) * T], pe_[:, t, E1:2 * E1], ident[0:T, 0:T])
                ins.then_inc(S("m_combt"), 1)
                pe.wait_ge(S("m_combts"), g + 1)
                for t in range(G):
                    mm(bank[0:T, 4 + t, 256:256 + D], oht[0:E1, t * T:(t + 1) * T], w_mb2[:], start=True, stop=True).then_inc(S("m_b2"), 1)
                pe.wait_ge(S("m_acc"), 20 * g + 4)
                for e in range(E1):
                    for f in range(FC):
                        if f >= 2:
                            pe.wait_ge(S("m_hid"), E1 * FC * g + (FC * e + f - 1))
                        for c in range(NK):
                            ins = mm(bank[:, 2 + f % 2, 0:GT], w_m1[:, e, c, f * 128:(f + 1) * 128], xtg[0:KC, c, :], start=(c == 0), stop=(c == NK - 1))
                        ins.then_inc(S("m_hmm"), 1)
                    pe.wait_ge(S("m_hid"), E1 * FC * g + (FC * e + FC))
                    for t in range(G):
                        if e > 0:
                            pe.wait_ge(S("m_acc"), 20 * g + (4 * e + t + 1))
                        for f in range(FC):
                            ins = mm(bank[0:T, 4 + t, 0:D], hid[:, f, t * T:(t + 1) * T], w_m2[:, e, f, :], start=(f == 0), stop=(f == FC - 1))
                        ins.then_inc(S("m_y"), 1)


def kernel(**inputs):
    import numpy as np
    import concourse.bacc as bacc
    from concourse.bass_utils import run_bass_kernel_spmd

    a = {k: np.asarray(x) for k, x in inputs.items()}
    nc = bacc.Bacc("TRN2", target_bir_lowering=False, num_devices=1)
    half = 8

    def quadrant_rows(w):
        n = w.shape[0]
        w = w.reshape(n, 2, half, 2, half, 3).transpose(0, 1, 3, 2, 4, 5)
        return w.reshape(n, 2, 2, half * half * 3)

    x = a["x"].reshape(B, 3, 14, half, 14, half)
    blocks = np.arange(-1, 15) % 14
    x = x[:, :, blocks][:, :, :, :, blocks]
    x = x.reshape(B, 3, 8, 2, half, 8, 2, half).transpose(3, 6, 4, 7, 1, 0, 2, 5)
    p1 = x.reshape(PF, 128, B // 2, 2, 8, 8).transpose(2, 1, 0, 3, 4, 5).reshape(B // 2, 128, PF * 128)
    wt = quadrant_rows(a["L0_tok_W"].reshape(D * 5, 16, 16, 3)).reshape(D, 5, 2, 2, D)
    wt = np.stack([wt[:, 0, ::-1, ::-1]] + [wt[:, k] for k in range(1, 5)])
    tokw = wt.reshape(5, D, PF, 128).transpose(3, 2, 0, 1)

    def chunks(w, k=KC):
        return w.reshape(w.shape[0] // k, k, w.shape[1]).transpose(1, 0, 2)

    def with_bias(w, b):
        row = np.zeros((1, NK, w.shape[1]), w.dtype)
        row[0, NK - 1] = b
        return np.concatenate([chunks(w), row])

    vecs = np.stack([a[k] for k in (
        "L0_tok_b", "L0_tok_gamma", "L0_tok_beta", "L0_txt_ln_gamma", "L0_txt_ln_beta", "L0_attn_ln1_g",
        "L0_attn_ln1_b", "L0_attn_ln2_g", "L0_attn_ln2_b", "L0_attn_b2", "L1_ffn_ln1_g", "L1_ffn_ln1_b",
        "L1_ffn_ln2_g", "L1_ffn_ln2_b")])
    bd = np.zeros((KC, HPC * M), np.float32)
    for h in range(HPC):
        bd[h * HD:(h + 1) * HD, h * M:(h + 1) * M] = a["L0_attn_proj"].T
    angle = np.repeat(np.arange(1, T + 1)[:, None] * 10000.0 ** (-2.0 * np.arange(D // 2) / D), 2, axis=-1)
    sign = np.tile([-1.0, 1.0], D // 2)
    rope = np.stack([np.cos(angle), np.sin(angle) * sign], axis=1).astype(np.float32)
    eye = np.eye(128, dtype=np.float32)[None]
    above = np.triu(np.ones((T, T)), k=1) * -1e30
    causal = np.tile(above, (1, 3)).astype(np.float32)
    headmask = np.repeat((np.arange(KC)[:, None] // HD == np.arange(HPC))[:, :, None], T, axis=2).astype(np.float32)
    expand = np.repeat(np.eye(E0, dtype=np.float32), R0, axis=1)
    iota = np.tile(np.arange(E0, dtype=np.float32) - E0, (T, 1))
    qkvo = np.concatenate([a[f"L1_attn_W_{k}"].T for k in "qkvo"], axis=1)
    qkvo_g = np.concatenate([a[f"L1_ffn_W{k}"].T for k in "qkvo"], axis=1)
    bias_g = np.concatenate([a[f"L1_ffn_b{k}"] for k in "qkvo"])
    arrays = {
        "p1": p1, "tokw": tokw, "ids": a["x_txt"].T, "types": a["mask_BS_i1_0"].T,
        "word_emb": a["L0_txt_word_emb"], "pos_emb": a["L0_txt_pos_emb"][:TT], "type_emb": a["L0_txt_type_emb"],
        "vecs": vecs, "favor_bd": bd, "f_w1": chunks(a["L0_attn_W1"]), "f_b1": a["L0_attn_b1"].reshape(FC, 128).T,
        "f_w2": chunks(a["L0_attn_W2"], 128), "enc_w": with_bias(a["L0_ffn_enc_w"], a["L0_ffn_enc_b"]),
        "sw_w": np.concatenate([a["L0_ffn_sw_w"], a["L0_ffn_sw_b"][None]]),
        "x_w1": chunks(a["L0_ffn_w1"].transpose(1, 0, 2).reshape(D, E0 * R0)),
        "x_b1": a["L0_ffn_b1"].reshape(C0, 128).T, "x_w2": chunks(a["L0_ffn_w2"].reshape(E0 * R0, D), 128),
        "x_b2": a["L0_ffn_b2"], "a_w": chunks(qkvo), "g_w": with_bias(qkvo_g, bias_g),
        "gate_w": with_bias(a["L1_ffn_Wg"].T, a["L1_ffn_bg"]),
        "m_w1": a["L1_ffn_W1"].reshape(E1, NK, KC, F).transpose(2, 0, 1, 3),
        "m_b1": a["L1_ffn_b1"].reshape(E1, FC, 128).transpose(2, 0, 1),
        "m_w2": a["L1_ffn_W2"].reshape(E1, FC, 128, D).transpose(2, 0, 1, 3), "m_b2": a["L1_ffn_b2"],
        "gamma": a["L1_ffn_gamma"].reshape(1), "rope": rope, "ident_in": eye, "causal_in": causal,
        "headmask_in": headmask, "expand_in": expand, "iota_in": iota,
    }
    arrays = {k: np.ascontiguousarray(x) for k, x in arrays.items()}
    handles = {k: nc.dram_tensor(k, x.shape, mybir.dt.from_np(x.dtype), kind="ExternalInput").ap()
               for k, x in arrays.items()}
    out = nc.dram_tensor("out", (B, T, D), F32, kind="ExternalOutput").ap()
    program(nc, out=out, **handles)
    result = run_bass_kernel_spmd(nc, [arrays], core_ids=[0])
    return result.results[0]["out"]
```

```python
from contextlib import ExitStack

import concourse.bass as bass
from concourse import mybir

F32 = mybir.dt.float32
BF16 = mybir.dt.bfloat16
I32 = mybir.dt.int32
ALU = mybir.AluOpType
ACT = mybir.ActivationFunctionType
AX = mybir.AxisListType

B = 16
TI = 49
TW = 64 + 55
TT = 77
T = TI + TT
D = 192
KC = 96
NK = D // KC
HEADS = 12
HD = D // HEADS
HPC = KC // HD
M = 64
F = 768
FC = F // 128
G = 4
GT = G * T
NG = B // G
E0 = 8
R0 = 64
UNITS = 4
C0 = E0 * R0 // 128
E1 = 4
PF = 6

(V_TOKB, V_TOKG, V_TOKBETA, V_TXTG, V_TXTB, V_L1G, V_L1B, V_L2G, V_L2B, V_FB2,
 V_N1G, V_N1B, V_N2G, V_N2B) = range(14)


def program(nc, p1, tokw, ids, types, word_emb, pos_emb, type_emb, vecs, favor_bd, f_w1, f_b1, f_w2,
            enc_w, sw_w, x_w1, x_b1, x_w2, x_b2, a_w, g_w, gate_w, m_w1, m_b1, m_w2, m_b2, gamma,
            rope, ident_in, causal_in, headmask_in, expand_in, iota_in, out):
    with ExitStack() as ctx:
        def sb(name, shape, dt=F32):
            return ctx.enter_context(nc.sbuf_tensor(name, shape, dt))

        def sem(name):
            return ctx.enter_context(nc.semaphore(name))

        bank = ctx.enter_context(nc.psum_tensor("bank", [128, 8, 512], F32))

        stream = sb("stream", [T, B, D])
        x1 = sb("x1", [T, B, D])
        vec = sb("vec", [T, 14, D])
        ident = sb("ident", [128, 128])
        identb = sb("identb", [128, 128], BF16)
        causal = sb("causal", [T, 3 * T], BF16)
        headmask = sb("headmask", [KC, HPC, T])
        ropes = sb("ropes", [T, 2, D])
        iota8 = sb("iota8", [T, E0])
        expand = sb("expand", [E0, E0 * R0], BF16)
        ones = sb("ones", [HEADS, T])
        halves = sb("halves", [T, 2, B])
        xs = sb("xs", [T, G, D])
        xt = sb("xt", [KC + 1, 2, NK, T])
        ot = sb("ot", [KC + 1, 2, NK, T])
        xtg = sb("xtg", [KC + 1, NK, GT])
        xtn = sb("xtn", [KC + 1, NK, GT])
        gamma_sb = sb("gamma_sb", [T, 1])
        gsign = sb("gsign", [T, 1])
        gabs = sb("gabs", [T, 1])
        gneg = sb("gneg", [T, 1])
        w_bd = sb("w_bd", [KC, HPC * M])
        w_f1 = sb("w_f1", [KC, NK, F])
        w_fb1 = sb("w_fb1", [128, FC])
        w_f2 = sb("w_f2", [128, FC, D])
        w_enc = sb("w_enc", [KC + 1, NK, R0])
        w_sw = sb("w_sw", [R0 + 1, E0])
        w_x1 = sb("w_x1", [KC, NK, E0 * R0])
        w_xb1 = sb("w_xb1", [128, C0])
        w_x2 = sb("w_x2", [128, C0, D])
        w_xb2 = sb("w_xb2", [E0, D])
        w_a = sb("w_a", [KC, NK, 4 * D])
        w_g = sb("w_g", [KC + 1, NK, 4 * D])
        w_gate = sb("w_gate", [KC + 1, NK, E1])
        w_mb1 = sb("w_mb1", [128, E1, FC])
        w_mb2 = sb("w_mb2", [E1, D])
        w_m1 = sb("w_m1", [KC, E1, NK, F])
        w_m2 = sb("w_m2", [128, E1, FC, D])
        work = sb("work", [128, PF * 5 * D])
        tokw_sb = work[:].rearrange("p (c s d) -> p c s d", c=PF, s=5)
        p1_sb = sb("p1_sb", [128, 2, PF * 128])
        txt = sb("txt", [TT, B, D])
        ids_sb = sb("ids_sb", [TT, B], I32)
        types_sb = sb("types_sb", [TT, B], I32)
        pos = sb("pos", [TT, D])
        hid = work[:, 0:FC * GT].rearrange("p (f t) -> p f t", f=FC)
        acc = work[0:T, FC * GT:FC * GT + G * D].rearrange("p (t d) -> p t d", t=G)

        st = sb("st", [T, B, 6])
        mean = sb("mean", [T, B])
        rstd = sb("rstd", [T, B])
        var = sb("var", [T, B])
        msum = sb("msum", [T, B])
        mdif = sb("mdif", [T, B])

        sq = sb("sq", [T, 2, D])
        ssum = sb("ssum", [T, 2, HEADS])
        mq = sb("mq", [T, 2, HEADS])
        qsub = sb("qsub", [T, 2, HEADS])
        ksub = sb("ksub", [T, 2, HEADS])
        kmax = sb("kmax", [HEADS, 2])
        kdiag = sb("kdiag", [HEADS, 2, HEADS])
        eq = work[0:T, 0:2 * F].rearrange("p (u m) -> p u m", u=2)
        ek = work[0:T, 2 * F:4 * F].rearrange("p (u m) -> p u m", u=2)
        va = sb("va", [T, 2, HEADS, HD + 1])
        cb = sb("cb", [128, 2, HEADS // 2, 2 * (HD + 1)])
        qt_f = work[:, 4 * F:4 * F + 2 * 6 * T].rearrange("p (u n) -> p u n", u=2)
        rden = sb("rden", [T, 2, HEADS])
        at = sb("at", [T, 2, D])

        qk = work[0:T, 0:2 * D]
        qk2 = work[0:T, 2 * D:4 * D]
        qkt = sb("qkt", [KC, 2 * NK * T])
        kbd = sb("kbd", [KC, UNITS, 3 * T])
        vals = sb("vals", [T, D])
        pr = work[0:T, 1536:1536 + UNITS * 3 * T].rearrange("p (q n) -> p q n", q=UNITS)
        pt = work[0:T, 3072:3072 + UNITS * 3 * T].rearrange("p (q n) -> p q n", q=UNITS)
        st6 = sb("st6", [T, HPC, 6])
        smax = sb("smax", [T, HEADS])
        nbias = sb("nbias", [T, HEADS])
        zscales = sb("zscales", [T, NK, HPC])
        zvar = sb("zvar", [T, HPC])
        zdif = sb("zdif", [T, HPC])
        zstd = sb("zstd", [T, HPC])
        psums = sb("psums", [T, HEADS])

        enct = sb("enct", [R0 + 1, GT])
        lg = sb("lg", [T, G, E0])
        pe_ = sb("pe_", [T, G, E0])
        hit = sb("hit", [T, G, E0])
        onehot = sb("onehot", [T, G, E0])
        one2 = sb("one2", [T, G, E0])
        gstat = sb("gstat", [T, 4, G])
        pmax = sb("pmax", [T, G])
        oht = sb("oht", [E0, GT])
        ohtb = sb("ohtb", [E0, GT], BF16)

        feps = sb("feps", [T, 1])
        mark = sb("mark", [1, 32])
        sems = {}

        def S(name):
            if name not in sems:
                sems[name] = sem(name)
            return sems[name]

        early = [(pos[:], pos_emb), (vec[:], vecs.partition_broadcast(T))]
        weights = [(ident[:], ident_in[0]), (w_bd[:], favor_bd), (w_f1[:], f_w1), (w_fb1[:], f_b1),
                   (w_f2[:], f_w2), (w_enc[:], enc_w), (w_sw[:], sw_w), (w_x1[:], x_w1), (w_xb1[:], x_b1),
                   (w_x2[:], x_w2), (w_xb2[:], x_b2), (iota8[:], iota_in), (w_a[:], a_w), (ropes[:], rope),
                   (headmask[:], headmask_in), (w_g[:], g_w), (gamma_sb[:], gamma.partition_broadcast(T)),
                   (w_gate[:], gate_w), (w_mb1[:], m_b1), (w_mb2[:], m_b2), (w_m1[:], m_w1), (w_m2[:], m_w2)]
        NW = len(weights)

        block = ctx.enter_context(nc.Block())

        def pair(i, u):
            return 2 * i + (u + 1)

        @block.sync
        def _(sp):
            sp.dma_start(ids_sb[:], ids).then_inc(S("ids_in"), 16)
            sp.dma_start(types_sb[:], types).then_inc(S("ids_in"), 16)
            sp.dma_start(tokw_sb, tokw).then_inc(S("tokw_in"), 16)
            for u in range(2):
                sp.dma_start(p1_sb[:, u, :], p1[u]).then_inc(S(f"p1_in{u}"), 16)
            for dst, src in early:
                sp.dma_start(dst, src).then_inc(S("early_in"), 16)
            with sp.Fori(0, B // 4 - 1) as i:
                for u in range(2):
                    sp.wait_ge(S("tok_mm"), pair(i, u))
                    sp.dma_start(p1_sb[:, u, :], p1[2 * i + (u + 2)]).then_inc(S(f"p1_in{u}"), 16)
            sp.wait_ge(S("txt_ready"), 1)
            sp.dma_start(stream[TI:T, :, :], txt[:]).then_inc(S("stream_in"), 16)
            sp.wait_ge(S("tok_ready"), 1)
            for j in range(2):
                for y in range(7):
                    row = 64 * j + 8 * y
                    sp.dma_start(stream[7 * y:7 * y + 7, :, :].rearrange("p (n j) d -> p n j d", j=2)[:, :, j, :],
                                 x1[row:row + 7, 0:B // 2, :]).then_inc(S("stream_in"), 16)
            sp.wait_ge(S("final"), B)
            sp.dma_start(out.rearrange("b t d -> t b d"), stream[:]).then_inc(S("out_done"), 16)
            sp.wait_ge(S("out_done"), 16)

        def group_loop(eng, front, slot, n):
            front(n, 0)
            with eng.Fori(0, NG - 1) as g:
                slot(g, True)
            slot(NG - 1, False)

        def attention_loop(eng, front, slot, n):
            front(n, 0)
            with eng.Fori(0, B - 1) as b:
                slot(b, True)
            slot(B - 1, False)

        @block.gpsimd
        def _(pool):
            nc.gpsimd.memset(ones[:], 1.0).then_inc(S("pool_const"), 1)
            nc.gpsimd.memset(feps[:], 1e-4).then_inc(S("pool_const"), 1)
            nc.gpsimd.memset(halves[:, 0, :], -0.5).then_inc(S("pool_const"), 1)
            nc.gpsimd.memset(halves[:, 1, :], 0.5).then_inc(S("pool_const"), 1)
            pool.wait_ge(S("ids_in"), 32)
            for b in range(B):
                pool.indirect_dma_start(txt[:, b, :], None, word_emb, bass.IndirectOffsetOnAxis(ids_sb[:, b:b + 1], 0)).then_inc(S("words_in"), 16)
                pool.indirect_dma_start(stream[0:TT, b, :], None, type_emb, bass.IndirectOffsetOnAxis(types_sb[:, b:b + 1], 0)).then_inc(S("words_in"), 16)
            pool.dma_start(identb[:], ident_in[0]).then_inc(S("cast_in"), 16)
            pool.dma_start(causal[:], causal_in).then_inc(S("cast_in"), 16)
            pool.dma_start(expand[:], expand_in).then_inc(S("cast_in"), 16)
            pool.wait_ge(S("pool_const"), 4)
            rs = [0]

            def inverse_deviation(P, n):
                rs[0] += 1
                pool.wait_ge(S("var_ready"), rs[0])
                nc.gpsimd.tensor_tensor(rstd[0:P, 0:n], var[0:P, 0:n], halves[0:P, 0, 0:n], ALU.pow).then_inc(S("rstd_ready"), 1)

            def pool_keys(n, k):
                pool.wait_ge(S(n + "_qkt"), k + 1)
                for q in range(UNITS):
                    c, half = q // 2, q % 2
                    nc.gpsimd.tensor_tensor(kbd[:, q, :].rearrange("p (h t) -> p h t", t=T),
                                            qkt[:, (2 + c) * T:(3 + c) * T].unsqueeze(1).to_broadcast([KC, 3, T]),
                                            headmask[:, 3 * half:3 * half + 3, :], ALU.mult).then_inc(S(n + "_kbd"), 1)

            def pool_deviations(b):
                for c in range(NK):
                    pool.wait_ge(S("g_var"), 2 * b + (c + 1))
                    nc.gpsimd.tensor_tensor(zstd[:], zvar[:], halves[:, 1, 0:HPC], ALU.pow).then_inc(S("g_std"), 1)

            inverse_deviation(TT, B)
            inverse_deviation(TW, B // 2)
            inverse_deviation(T, B)
            inverse_deviation(T, B)
            with pool.Fori(0, B // 2) as i:
                for u in range(2):
                    pool.wait_ge(S("f_xs"), pair(i, u))
                    nc.gpsimd.tensor_tensor(sq[:, u, :], xs[:, u, :], xs[:, u, :], ALU.mult).then_inc(S("f_sq"), 1)
                for u in range(2):
                    pool.wait_ge(S("f_ekexp"), pair(i, u))
                    nc.gpsimd.tensor_tensor(ek[:, u, :], ek[:, u, :], feps[:].to_broadcast([T, F]), ALU.add).then_inc(S("f_ek"), 1)
            inverse_deviation(T, B)
            inverse_deviation(T, B)
            inverse_deviation(T, B)
            attention_loop(pool, pool_keys, lambda b, more: more and pool_keys("a", b + 1), "a")
            inverse_deviation(T, B)
            attention_loop(pool, pool_keys, lambda b, more: (pool_deviations(b), more and pool_keys("g", b + 1)), "g")
            inverse_deviation(T, B)
            with pool.Fori(0, NG) as g:
                pool.wait_ge(S("m_var"), g + 1)
                nc.gpsimd.tensor_tensor(rstd[:, 0:G], var[:, 0:G], halves[:, 0, 0:G], ALU.pow).then_inc(S("m_rstd"), 1)

        @block.vector
        def _(dve):
            count = {"n": 0, "i": None, "per": 0, "c": 0}

            def enter(i, per):
                count.update(i=i, per=per, c=0)

            def leave(trips):
                assert count["c"] == count["per"], count
                count.update(n=count["n"] + trips * count["per"], i=None, c=0)

            def done(ins):
                ins.then_inc(S("dve_step"), 1)
                if count["i"] is None:
                    count["n"] += 1
                    dve.wait_ge(S("dve_step"), count["n"])
                else:
                    count["c"] += 1
                    dve.wait_ge(S("dve_step"), count["i"] * count["per"] + (count["n"] + count["c"]))

            stats = [0]
            norms = [0]

            def moments(P, n, eps, chain):
                chain(nc.vector.tensor_tensor(msum[0:P, 0:n], st[0:P, 0:n, 1], st[0:P, 0:n, 4], ALU.add))
                chain(nc.vector.tensor_tensor(mdif[0:P, 0:n], st[0:P, 0:n, 1], st[0:P, 0:n, 4], ALU.subtract))
                chain(nc.vector.tensor_tensor(var[0:P, 0:n], st[0:P, 0:n, 2], st[0:P, 0:n, 5], ALU.add))
                chain(nc.vector.tensor_scalar(mean[0:P, 0:n], msum[0:P, 0:n], 0.5, None, ALU.mult))
                chain(nc.vector.scalar_tensor_tensor(mdif[0:P, 0:n], mdif[0:P, 0:n], 0.25, mdif[0:P, 0:n], ALU.mult, ALU.mult))
                chain(nc.vector.scalar_tensor_tensor(var[0:P, 0:n], var[0:P, 0:n], 1.0 / D, mdif[0:P, 0:n], ALU.mult, ALU.add))
                return nc.vector.tensor_scalar(var[0:P, 0:n], var[0:P, 0:n], eps, None, ALU.add)

            def norm_stats(P, n, src, eps):
                for b in range(n):
                    nc.vector.bn_stats(st[0:P, b, :], src[0:P, b, :]).then_inc(S("stats"), 1)
                stats[0] += n
                norms[0] += 1
                dve.wait_ge(S("stats"), stats[0])
                moments(P, n, eps, done).then_inc(S("var_ready"), 1)
                dve.wait_ge(S("rstd_ready"), norms[0])

            def normalise(dst, src, P, b):
                return nc.vector.tensor_scalar(dst, src, mean[0:P, bass.ts(b, 1)], rstd[0:P, bass.ts(b, 1)],
                                               ALU.subtract, ALU.mult)

            nc.vector.memset(xt[KC:KC + 1], 1.0).then_inc(S("dve_const"), 1)
            nc.vector.memset(ot[KC:KC + 1], 1.0).then_inc(S("dve_const"), 1)
            nc.vector.memset(xtg[KC:KC + 1], 1.0).then_inc(S("dve_const"), 1)
            nc.vector.memset(xtn[KC:KC + 1], 1.0).then_inc(S("dve_const"), 1)
            nc.vector.memset(enct[R0:R0 + 1], 1.0).then_inc(S("dve_const"), 1)
            nc.vector.memset(va[:], 1.0).then_inc(S("dve_const"), 1)
            nc.vector.memset(cb[:], 0.0).then_inc(S("dve_const"), 1)
            nc.vector.memset(onehot[:], 0.0).then_inc(S("dve_const"), 1)
            dve.wait_ge(S("tokw_in"), 16)
            for shift, (c, lo, hi) in ((1, (0, 0, 128)), (1, (1, 0, 64)), (2, (1, 64, 128)), (2, (2, 0, 128)),
                                       (3, (3, 0, 128)), (3, (4, 0, 64)), (4, (4, 64, 128)), (4, (5, 0, 128))):
                w = tokw_sb[lo:hi, c, shift, :]
                nc.vector.tensor_tensor(w, w, tokw_sb[lo:hi, c, 0, :], ALU.add).then_inc(S("tokw_ready"), 1)
            dve.wait_ge(S("early_in"), 16 * len(early))

            def affine(x, P, n, g, b):
                done(nc.vector.tensor_tensor(x, x, vec[0:P, g, :].unsqueeze(1).to_broadcast([P, n, D]), ALU.mult))
                return nc.vector.tensor_tensor(x, x, vec[0:P, b, :].unsqueeze(1).to_broadcast([P, n, D]), ALU.add)

            dve.wait_ge(S("words_in"), 16 * 2 * B)
            done(nc.vector.tensor_tensor(txt[:], txt[:], stream[0:TT, :, :], ALU.add))
            done(nc.vector.tensor_tensor(txt[:], txt[:], pos[:].unsqueeze(1).to_broadcast([TT, B, D]), ALU.add))
            norm_stats(TT, B, txt, 1e-12)
            for b in range(B):
                ins = normalise(txt[:, b, :], txt[:, b, :], TT, b)
            done(ins)
            affine(txt[:], TT, B, V_TXTG, V_TXTB).then_inc(S("txt_ready"), 1)

            for i in range(2):
                dve.wait_ge(S("tok_mm"), 4 * i + 4)
                nc.vector.tensor_tensor(x1[0:TW, 4 * i:4 * i + 4, :], bank[0:TW, 4 * i:4 * i + 4, 0:D],
                                        vec[0:TW, V_TOKB, :].unsqueeze(1).to_broadcast([TW, 4, D]), ALU.add).then_inc(S("tok_sum"), 1)
            dve.wait_ge(S("tok_sum"), 2)
            norm_stats(TW, B // 2, x1, 1e-5)
            for b in range(B // 2):
                ins = normalise(x1[0:TW, b, :], x1[0:TW, b, :], TW, b)
            done(ins)
            affine(x1[0:TW, 0:B // 2, :], TW, B // 2, V_TOKG, V_TOKBETA).then_inc(S("tok_ready"), 1)
            dve.wait_ge(S("weights_in"), 16 * NW)
            nc.vector.tensor_scalar(w_bd[:], w_bd[:], HD ** -0.25, None, ALU.mult).then_inc(S("bd_ready"), 1)
            done(nc.vector.tensor_scalar(gneg[:], gamma_sb[:], -1.0, None, ALU.mult))
            done(nc.vector.tensor_tensor(gabs[:], gamma_sb[:], gneg[:], ALU.max))
            done(nc.vector.tensor_scalar(gsign[:], gamma_sb[:], 0.0, None, ALU.is_ge))
            done(nc.vector.tensor_scalar(gsign[:], gsign[:], 2.0, -1.0, ALU.mult, ALU.add))

            dve.wait_ge(S("stream_in"), 16 * 15)

            norm_stats(T, B, stream, 1e-5)
            for b in range(B):
                normalise(x1[:, b, :], stream[:, b, :], T, b).then_inc(S("f_x1"), 1)
            dve.wait_ge(S("f_x1"), B)
            norm_stats(T, B, x1, 1e-5)
            with dve.Fori(0, B // 2) as i:
                enter(i, 2 * 10)
                for u in range(2):
                    b = 2 * i + u
                    done(normalise(xs[:, u, :], x1[:, b, :], T, b))
                    done(nc.vector.tensor_tensor(xs[:, u, :], xs[:, u, :], vec[:, V_L1G, :], ALU.mult))
                    nc.vector.tensor_tensor(xs[:, u, :], xs[:, u, :], vec[:, V_L1B, :], ALU.add).then_inc(S("f_xs"), 1)
                for u in range(2):
                    dve.wait_ge(S("f_sq"), pair(i, u))
                    done(nc.vector.tensor_reduce(ssum[:, u, :], sq[:, u, :].rearrange("p (h d) -> p h d", h=HEADS), AX.X, ALU.add))
                for u in range(2):
                    feats = bank[0:T, 4 * u + 1:4 * u + 3, 0:HPC * M].rearrange("p k (h m) -> p k h m", m=M)
                    dve.wait_ge(S("f_u"), pair(i, u))
                    nc.vector.tensor_reduce(mq[:, u, :].rearrange("p (k h) -> p k h", k=2), feats, AX.X, ALU.max).then_inc(S("f_mq"), 1)
                    dve.wait_ge(S("f_mq"), pair(i, u))
                    done(nc.vector.scalar_tensor_tensor(qsub[:, u, :], ssum[:, u, :], 0.125, mq[:, u, :], ALU.mult, ALU.add))
                    nc.vector.tensor_tensor(eq[:, u, :].rearrange("p (k h m) -> p k h m", k=2, m=M), feats,
                                            qsub[:, u, :].rearrange("p (k h) -> p k h", k=2).unsqueeze(3).to_broadcast([T, 2, HPC, M]),
                                            ALU.subtract).then_inc(S("f_eq"), 1)
                for u in range(2):
                    dve.wait_ge(S("f_mqt"), pair(i, u))
                    done(nc.vector.tensor_reduce(kmax[:, u:u + 1], bank[0:HEADS, 4 * u, 256:256 + T], AX.X, ALU.max))
                    nc.vector.tensor_scalar(kdiag[:, u, :], ident[0:HEADS, 0:HEADS], kmax[:, u:u + 1], None, ALU.mult).then_inc(S("f_kd"), 1)
                for u in range(2):
                    feats = bank[0:T, 4 * u + 1:4 * u + 3, 0:HPC * M].rearrange("p k (h m) -> p k h m", m=M)
                    dve.wait_ge(S("f_kb"), pair(i, u))
                    done(nc.vector.scalar_tensor_tensor(ksub[:, u, :], ssum[:, u, :], 0.125, bank[0:T, 4 * u, 384:384 + HEADS], ALU.mult, ALU.add))
                    nc.vector.tensor_tensor(ek[:, u, :].rearrange("p (k h m) -> p k h m", k=2, m=M), feats,
                                            ksub[:, u, :].rearrange("p (k h) -> p k h", k=2).unsqueeze(3).to_broadcast([T, 2, HPC, M]),
                                            ALU.subtract).then_inc(S("f_eksub"), 1)
                for u in range(2):
                    dve.wait_ge(S("f_ctx"), pair(i, u))
                    ctxs = bank[:, 4 * u + 3, 0:6 * 34].rearrange("p (j n) -> p j n", n=34)
                    nc.vector.tensor_copy(cb[0:64, u, :, 0:17], ctxs[0:64, :, 0:17])
                    nc.vector.tensor_copy(cb[64:128, u, :, 17:34], ctxs[64:128, :, 17:34]).then_inc(S("f_cb"), 1)
                for u in range(2):
                    dve.wait_ge(S("f_qt"), pair(i, u))
                    nc.vector.tensor_scalar(qt_f[:, u, :].rearrange("p (k n) -> p k n", k=2), bank[:, 4 * u + 1:4 * u + 3, 0:3 * T],
                                            1e-4, None, ALU.add).then_inc(S("f_qts"), 1)
                for u in range(2):
                    b = 2 * i + u
                    dve.wait_ge(S("f_att"), pair(i, u))
                    att = bank[0:T, 4 * u + 3, 256:256 + 6 * 34].rearrange("p (h n) -> p h n", n=17)
                    done(nc.vector.reciprocal(rden[:, u, :], att[:, :, HD]))
                    done(nc.vector.tensor_tensor(at[:, u, :].rearrange("p (h d) -> p h d", h=HEADS), att[:, :, 0:HD],
                                                 rden[:, u, :].unsqueeze(2).to_broadcast([T, HEADS, HD]), ALU.mult))
                    done(nc.vector.tensor_tensor(x1[:, b, :], x1[:, b, :], at[:, u, :], ALU.add))
                    done(nc.vector.tensor_tensor(stream[:, b, :], stream[:, b, :], x1[:, b, :], ALU.add))
                leave(B // 2)

            norm_stats(T, B, x1, 1e-5)

            def group_tokens(n, g):
                if n == "x":
                    src, scale = stream, None
                else:
                    src, scale = x1, (V_L2G, V_L2B) if n == "n" else (V_N1G, V_N1B)
                for t in range(G):
                    ins = normalise(xs[:, t, :], src[:, 4 * g + t, :], T, 4 * g + t)
                if scale:
                    done(ins)
                    ins = affine(xs[:], T, G, *scale)
                ins.then_inc(S(n + "_xs"), 1)

            def gelu_slot(g, more):
                if more:
                    enter(g, 2 + 4)
                    dve.wait_ge(S("n_xtmm"), g + 1)
                    group_tokens("n", g + 1)
                for t in range(G):
                    b = 4 * g + t
                    dve.wait_ge(S("n_y"), b + 1)
                    done(nc.vector.tensor_tensor(at[:, t % 2, :], bank[0:T, 4 + t, 0:D], vec[:, V_FB2, :], ALU.add))
                    nc.vector.tensor_tensor(stream[:, b, :], stream[:, b, :], at[:, t % 2, :], ALU.add).then_inc(S("n_sum"), 1)
                    dve.wait_ge(S("n_sum"), b + 1)
                if more:
                    leave(NG - 1)

            group_loop(dve, group_tokens, gelu_slot, "n")

            def first_of(dst, values, top):
                n = values.shape[2]
                dve_top = gstat[:, top, :].unsqueeze(2).to_broadcast([T, G, n])
                done(nc.vector.tensor_reduce(gstat[:, top, :], values, AX.X, ALU.max))
                done(nc.vector.tensor_tensor(hit[:, :, 0:n], values, dve_top, ALU.is_ge))
                done(nc.vector.tensor_tensor(hit[:, :, 0:n], hit[:, :, 0:n], iota8[:, 0:n].unsqueeze(1).to_broadcast([T, G, n]), ALU.mult))
                done(nc.vector.tensor_reduce(gstat[:, 3, :], hit[:, :, 0:n], AX.X, ALU.min))
                return nc.vector.tensor_tensor(dst, hit[:, :, 0:n], gstat[:, 3, :].unsqueeze(2).to_broadcast([T, G, n]), ALU.is_equal)

            def softmax(n, logits, name, k):
                done(nc.vector.tensor_reduce(gstat[:, 0, :], logits, AX.X, ALU.max))
                nc.vector.tensor_tensor(lg[:, :, 0:n], logits, gstat[:, 0, :].unsqueeze(2).to_broadcast([T, G, n]),
                                        ALU.subtract).then_inc(S(name + "_lg"), 1)
                dve.wait_ge(S(name + "_exp"), k)
                done(nc.vector.tensor_reduce(gstat[:, 1, :], lg[:, :, 0:n], AX.X, ALU.add))
                done(nc.vector.reciprocal(gstat[:, 1, :], gstat[:, 1, :]))
                done(nc.vector.tensor_tensor(pe_[:, :, 0:n], lg[:, :, 0:n], gstat[:, 1, :].unsqueeze(2).to_broadcast([T, G, n]), ALU.mult))

            norm_stats(T, B, stream, 1e-5)

            def route_top(k):
                dve.wait_ge(S("x_logits"), k + 1)
                softmax(E0, bank[0:T, 1, 0:G * E0].rearrange("p (t e) -> p t e", e=E0), "x", k + 1)
                first_of(onehot[:], pe_[:], 2).then_inc(S("x_onehot"), 1)

            def take_routes(k):
                nc.vector.tensor_copy(pmax[:], gstat[:, 2, :])
                dve.wait_ge(S("x_oht"), k + 1)
                nc.vector.tensor_copy(oht[:], bank[0:E0, 0, 0:GT])
                nc.vector.tensor_copy(ohtb[:], bank[0:E0, 0, 0:GT]).then_inc(S("x_ohts"), 1)

            def routed_front(n, k):
                group_tokens(n, k)
                route_top(k)
                take_routes(k)

            def routed_slot(g, more):
                if more:
                    enter(g, 4 + 4)
                    dve.wait_ge(S("x_xtmm"), g + 1)
                    group_tokens("x", g + 1)
                for c in range(C0):
                    dve.wait_ge(S("x_hid"), C0 * g + (c + 1))
                    dve.wait_ge(S("x_mask"), C0 * g + (c + 1))
                    nc.vector.tensor_tensor(hid[:, c, :], hid[:, c, :], bank[:, 6 + c % 2, 0:GT], ALU.mult).then_inc(S("x_masked"), 1)
                if more:
                    route_top(g + 1)
                dve.wait_ge(S("x_ohts"), g + 1)
                dve.wait_ge(S("x_y"), g + 1)
                for t in range(G):
                    b = 4 * g + t
                    nc.vector.scalar_tensor_tensor(stream[:, b, :], bank[0:T, 4 + t // 2, t % 2 * D:(t % 2 + 1) * D], pmax[:, t:t + 1],
                                                   stream[:, b, :], ALU.mult, ALU.add).then_inc(S("x_sum"), 1)
                dve.wait_ge(S("x_sum"), G * g + G)
                if more:
                    take_routes(g + 1)
                    leave(NG - 1)

            group_loop(dve, routed_front, routed_slot, "x")

            norm_stats(T, B, stream, 1e-5)

            def front_tokens(n, k):
                if n == "g":
                    normalise(x1[:, k, :], stream[:, k, :], T, k)
                normalise(xs[:, 0, :], stream[:, k, :], T, k).then_inc(S(n + "_xs"), 1)

            def front_queries(n, k):
                dve.wait_ge(S(n + "_qkv"), k + 1)
                raw = bank[0:T, 1, 0:2 * D]
                if n == "g":
                    nc.vector.tensor_scalar(qk[:, 0:D], raw[:, 0:D], gsign[:, 0:1], None, ALU.mult)
                    nc.vector.tensor_copy(qk[:, D:2 * D], raw[:, D:2 * D]).then_inc(S("g_qk"), 1)
                    return
                raw2 = raw.rearrange("p (n r) -> p n r", r=2)
                cos, sin = (ropes[:, j, :].unsqueeze(1).to_broadcast([T, 2, D]) for j in range(2))
                sin2 = ropes[:, 1, :].rearrange("p (n r) -> p n r", r=2)
                swapped = qk2.rearrange("p (a n r) -> p a n r", a=2, r=2)
                raw4 = raw.rearrange("p (a n r) -> p a n r", a=2, r=2)
                for r in range(2):
                    nc.vector.tensor_tensor(swapped[:, :, :, r], raw4[:, :, :, 1 - r],
                                            sin2[:, :, r].unsqueeze(1).to_broadcast([T, 2, D // 2]), ALU.mult)
                done(nc.vector.tensor_tensor(qk.rearrange("p (a d) -> p a d", a=2), raw.rearrange("p (a d) -> p a d", a=2), cos, ALU.mult))
                nc.vector.tensor_tensor(qk, qk, qk2, ALU.add).then_inc(S("a_qk"), 1)

            def unit_scores(q):
                return bank[0:T, 4 + q, 0:3 * T].rearrange("p (h t) -> p h t", t=T)

            def unit_max(q):
                return nc.vector.tensor_reduce(smax[:, 3 * q:3 * q + 3], unit_scores(q), AX.X, ALU.max)

            def causal_bias(b, q):
                dve.wait_ge(S("a_s"), UNITS * b + (q + 1))
                done(unit_max(q))
                nc.vector.tensor_scalar(nbias[:, 3 * q:3 * q + 3], smax[:, 3 * q:3 * q + 3], -HD ** -0.5, None, ALU.mult).then_inc(S("a_bias"), 1)

            def row_moments(b, c):
                for q in (2 * c, 2 * c + 1):
                    dve.wait_ge(S("g_s"), UNITS * b + (q + 1))
                    for h in range(3):
                        nc.vector.bn_stats(st6[:, q % 2 * 3 + h, :], bank[0:T, 4 + q, h * T:(h + 1) * T])
                    ins = unit_max(q)
                done(ins)
                nc.vector.tensor_tensor(zdif[:], st6[:, :, 1], st6[:, :, 4], ALU.subtract)
                done(nc.vector.tensor_tensor(zvar[:], st6[:, :, 2], st6[:, :, 5], ALU.add))
                done(nc.vector.scalar_tensor_tensor(zdif[:], zdif[:], T / 4.0, zdif[:], ALU.mult, ALU.mult))
                done(nc.vector.tensor_tensor(zvar[:], zvar[:], zdif[:], ALU.add))
                nc.vector.tensor_scalar(zvar[:], zvar[:], 1.0 / (HD * (T - 1)), None, ALU.mult).then_inc(S("g_var"), 1)

            def row_scales(b, c):
                dve.wait_ge(S("g_std"), 2 * b + (c + 1))
                done(nc.vector.tensor_scalar(zstd[:], zstd[:], 1e-5, None, ALU.add))
                done(nc.vector.reciprocal(zscales[:, c, :], zstd[:]))
                done(nc.vector.tensor_scalar(zscales[:, c, :], zscales[:, c, :], gabs[:, 0:1], HD ** -0.5, ALU.mult, ALU.mult))
                nc.vector.scalar_tensor_tensor(nbias[:, HPC * c:HPC * c + HPC], smax[:, HPC * c:HPC * c + HPC], -1.0,
                                               zscales[:, c, :], ALU.mult, ALU.mult).then_inc(S("g_bias"), 1)

            def copy_probs(n, b, q):
                dve.wait_ge(S(n + "_pt"), UNITS * b + (q + 1))
                nc.vector.tensor_copy(pt[:, q, :], bank[0:T, 4 + q, 0:3 * T]).then_inc(S(n + "_pts"), 1)

            def attended(n, b):
                dve.wait_ge(S(n + "_pv"), b + 1)
                done(nc.vector.reciprocal(rden[:, 0, :], psums[:]))
                nc.vector.tensor_tensor(at[:, 0, :].rearrange("p (h d) -> p h d", h=HEADS),
                                        bank[0:T, 2, 0:D].rearrange("p (h d) -> p h d", h=HEADS),
                                        rden[:, 0, :].unsqueeze(2).to_broadcast([T, HEADS, HD]), ALU.mult).then_inc(S(n + "_at"), 1)
                dve.wait_ge(S(n + "_o"), b + 1)
                res = stream if n == "a" else x1
                nc.vector.tensor_tensor(res[:, b, :], res[:, b, :], bank[0:T, 3, 256:256 + D], ALU.add).then_inc(S(n + "_sum"), 1)

            def causal_slot(b, more):
                if more:
                    enter(b, UNITS + 1 + 1)
                    front_tokens("a", b + 1)
                for q in range(UNITS):
                    causal_bias(b, q)
                copy_probs("a", b, 0)
                if more:
                    front_queries("a", b + 1)
                for q in range(1, UNITS):
                    copy_probs("a", b, q)
                attended("a", b)
                if more:
                    leave(B - 1)

            def front(n, k):
                front_tokens(n, k)
                front_queries(n, k)

            attention_loop(dve, front, causal_slot, "a")
            dve.wait_ge(S("a_sum"), B)

            norm_stats(T, B, stream, 1e-5)

            def standard_slot(b, more):
                if more:
                    enter(b, 2 * 7 + 1)
                    front_tokens("g", b + 1)
                row_moments(b, 0)
                row_scales(b, 0)
                row_moments(b, 1)
                row_scales(b, 1)
                copy_probs("g", b, 0)
                if more:
                    front_queries("g", b + 1)
                for q in range(1, UNITS):
                    copy_probs("g", b, q)
                attended("g", b)
                if more:
                    leave(B - 1)

            attention_loop(dve, front, standard_slot, "g")
            dve.wait_ge(S("g_sum"), B)

            norm_stats(T, B, x1, 1e-5)

            def expert_sums(g, e, start):
                for t in range(G):
                    dve.wait_ge(S("m_y"), 16 * g + (4 * e + t + 1))
                    if e == 2:
                        dve.wait_ge(S("m_bsum"), 4 * g + (t + 1))
                    elif e > 0:
                        dve.wait_ge(S("m_acc"), 16 * g + (4 * e + t - 3))
                    nc.vector.scalar_tensor_tensor(acc[:, t, :], bank[0:T, 4 + t, 0:D], pe_[:, t, E1 + e:E1 + e + 1],
                                                   start[:, t, :], ALU.mult, ALU.add).then_inc(S("m_acc"), 1)

            def mixture_slot(g, more):
                if more:
                    enter(g, 16 + 2 + 1 + 6 + 1 + 2)
                dve.wait_ge(S("m_logits"), g + 1)
                softmax(E1, bank[0:T, 1, 0:G * E1].rearrange("p (t e) -> p t e", e=E1), "m", g + 1)
                p4, o1, o2 = pe_[:, :, 0:E1], onehot[:, :, 0:E1], one2[:, :, 0:E1]
                done(first_of(o1, p4, 2))
                done(nc.vector.scalar_tensor_tensor(lg[:, :, 0:E1], o1, -2.0, p4, ALU.mult, ALU.add))
                done(first_of(o2, lg[:, :, 0:E1], 2))
                done(nc.vector.tensor_tensor(o1, o1, o2, ALU.add))
                nc.vector.tensor_tensor(pe_[:, :, E1:2 * E1], o1, p4, ALU.mult).then_inc(S("m_comb"), 1)
                dve.wait_ge(S("m_comb"), g + 1)
                expert_sums(g, 0, xs)
                dve.wait_ge(S("m_combt"), g + 1)
                nc.vector.tensor_copy(oht[0:E1, :], bank[0:E1, 0, 0:GT]).then_inc(S("m_combts"), 1)
                expert_sums(g, 1, acc)
                for t in range(G):
                    dve.wait_ge(S("m_acc"), 16 * g + (4 + t + 1))
                    nc.vector.tensor_tensor(acc[:, t, :], acc[:, t, :], bank[0:T, 4 + t, 256:256 + D], ALU.add).then_inc(S("m_bsum"), 1)
                if more:
                    group_tokens("m", g + 1)
                expert_sums(g, 2, acc)
                expert_sums(g, 3, acc)
                dve.wait_ge(S("m_acc"), 16 * g + 16)
                for t in range(G):
                    ins = nc.vector.bn_stats(st[:, t, :], acc[:, t, :])
                done(ins)
                moments(T, G, 1e-5, done).then_inc(S("m_var"), 1)
                dve.wait_ge(S("m_rstd"), g + 1)
                for t in range(G):
                    ins = nc.vector.tensor_scalar(acc[:, t, :], acc[:, t, :], mean[:, t:t + 1], rstd[:, t:t + 1], ALU.subtract, ALU.mult)
                done(ins)
                done(affine(acc, T, G, V_N2G, V_N2B))
                for t in range(G):
                    nc.vector.tensor_tensor(stream[:, 4 * g + t, :], stream[:, 4 * g + t, :], acc[:, t, :], ALU.add).then_inc(S("final"), 1)
                dve.wait_ge(S("final"), G * g + G)
                if more:
                    leave(NG - 1)

            group_loop(dve, group_tokens, mixture_slot, "m")

        @block.scalar
        def _(act):
            act.wait_ge(S("early_in"), 16 * len(early))
            for dst, src in weights:
                act.dma_start(dst, src).then_inc(S("weights_in"), 16)
            act.wait_ge(S("weights_in"), 16 * NW)
            act.wait_ge(S("dve_const"), 8)

            def pair_tokens(xs_ready, xt_mm, xt_ready, i):
                for u in range(2):
                    act.wait_ge(S(xt_mm), pair(i, u))
                    nc.scalar.copy(xt[0:KC, u, :, :], bank[0:KC, 4 * u, 0:NK * T].rearrange("p (c t) -> p c t", c=NK)).then_inc(S(xt_ready), 1)

            def group_tokens(name, g):
                act.wait_ge(S(name + "_xtmm"), g + 1)
                nc.scalar.copy(xtg[0:KC, :, :], bank[0:KC, 0:2, 0:GT]).then_inc(S(name + "_xt"), 1)

            with act.Fori(0, B // 2) as i:
                for u in range(2):
                    act.wait_ge(S("f_xtmm"), pair(i, u))
                    nc.scalar.copy(xt[0:KC, u, :, :], bank[0:KC, 4 * u, 0:NK * T].rearrange("p (c t) -> p c t", c=NK)).then_inc(S("f_xt"), 1)
                for u in range(2):
                    act.wait_ge(S("f_xs"), pair(i, u))
                    nc.scalar.copy(va[:, u, :, 0:HD], xs[:, u, :].rearrange("p (h d) -> p h d", h=HEADS)).then_inc(S("f_va"), 1)
                for u in range(2):
                    act.wait_ge(S("f_eq"), pair(i, u))
                    nc.scalar.activation(eq[:, u, :], eq[:, u, :], ACT.Exp).then_inc(S("f_eqexp"), 1)
                for u in range(2):
                    act.wait_ge(S("f_eksub"), pair(i, u))
                    nc.scalar.activation(ek[:, u, :], ek[:, u, :], ACT.Exp).then_inc(S("f_ekexp"), 1)

            def gelu_slot(g, more):
                for f in range(FC):
                    act.wait_ge(S("n_hmm"), FC * g + (f + 1))
                    nc.scalar.activation(hid[:, f, :], bank[:, 2 + f % 2, 0:GT], ACT.Gelu, bias=w_fb1[:, f:f + 1]).then_inc(S("n_hid"), 1)
                if more:
                    group_tokens("n", g + 1)

            group_loop(act, group_tokens, gelu_slot, "n")

            def next_tokens(k):
                act.wait_ge(S("x_xtmm"), k + 1)
                nc.scalar.copy(xtn[0:KC, :, :], bank[0:KC, 0:2, 0:GT]).then_inc(S("x_xt"), 1)

            def encoded(k):
                act.wait_ge(S("x_encmm"), k + 1)
                nc.scalar.copy(enct[0:R0, :], bank[0:R0, 0, 0:GT]).then_inc(S("x_enc"), 1)

            def take_tokens(k):
                act.wait_ge(S("x_lg"), k + 1)
                nc.scalar.activation(lg[:], lg[:], ACT.Exp).then_inc(S("x_exp"), 1)
                act.wait_ge(S("x_xt"), k + 1)
                nc.scalar.copy(xtg[0:KC, :, :], xtn[0:KC, :, :]).then_inc(S("x_xtg"), 1)
                act.wait_ge(S("x_xtg"), k + 1)

            def routed_front(n, k):
                next_tokens(k)
                encoded(k)
                take_tokens(k)

            def routed_slot(g, more):
                for c in range(C0):
                    act.wait_ge(S("x_hmm"), C0 * g + (c + 1))
                    nc.scalar.activation(hid[:, c, :], bank[:, 2 + c % 2, 0:GT], ACT.Gelu, bias=w_xb1[:, c:c + 1]).then_inc(S("x_hid"), 1)
                    if more and c == 0:
                        next_tokens(g + 1)
                    if more and c == 1:
                        encoded(g + 1)
                if more:
                    take_tokens(g + 1)

            group_loop(act, routed_front, routed_slot, "x")

            def front_tokens(n, k):
                act.wait_ge(S(n + "_xtmm"), k + 1)
                nc.scalar.copy(xt[0:KC, 0, :, :], bank[0:KC, 0, 0:NK * T].rearrange("p (c t) -> p c t", c=NK)).then_inc(S(n + "_xt"), 1)

            def front_queries(n, k):
                act.wait_ge(S(n + "_qktmm"), k + 1)
                nc.scalar.copy(qkt[:], bank[0:KC, 1, 0:2 * NK * T]).then_inc(S(n + "_qkt"), 1)

            def front_values(n, k):
                nc.scalar.copy(vals[:], bank[0:T, 0, 256:256 + D]).then_inc(S(n + "_v"), 1)

            def front(n, k):
                front_tokens(n, k)
                act.wait_ge(S(n + "_qkv"), k + 1)
                front_values(n, k)
                front_queries(n, k)

            def unit_exp(n, b, q):
                act.wait_ge(S(n + "_bias"), UNITS * b + (q + 1) if n == "a" else 2 * b + (q // 2 + 1))
                for h in range(3):
                    head = 3 * q + h
                    scale = HD ** -0.5 if n == "a" else zscales[:, head // HPC, head % HPC:head % HPC + 1]
                    ins = nc.scalar.activation(pr[:, q, h * T:(h + 1) * T], bank[0:T, 4 + q, h * T:(h + 1) * T],
                                               ACT.Exp, bias=nbias[:, head:head + 1], scale=scale, accum_out=psums[:, head:head + 1])
                ins.then_inc(S(n + "_p"), 1)

            def attention(n):
                def slot(b, more):
                    unit_exp(n, b, 0)
                    if more:
                        front_tokens(n, b + 1)
                    for q in range(1, UNITS):
                        unit_exp(n, b, q)
                    if more:
                        front_queries(n, b + 1)
                    act.wait_ge(S(n + "_pv"), b + 1)
                    if more:
                        front_values(n, b + 1)
                    act.wait_ge(S(n + "_otmm"), b + 1)
                    nc.scalar.copy(ot[0:KC, 0, :, :], bank[0:KC, 3, 0:NK * T].rearrange("p (c t) -> p c t", c=NK)).then_inc(S(n + "_ot"), 1)

                attention_loop(act, front, slot, n)

            attention("a")
            attention("g")

            def mixture_slot(g, more):
                for e in range(E1):
                    if e == 1:
                        act.wait_ge(S("m_lg"), g + 1)
                        nc.scalar.activation(lg[:, :, 0:E1], lg[:, :, 0:E1], ACT.Exp).then_inc(S("m_exp"), 1)
                    for f in range(FC):
                        act.wait_ge(S("m_hmm"), E1 * FC * g + (FC * e + f + 1))
                        nc.scalar.activation(hid[:, f, :], bank[:, 2 + f % 2, 0:GT], ACT.Relu, bias=w_mb1[:, e, f:f + 1]).then_inc(S("m_hid"), 1)
                if more:
                    group_tokens("m", g + 1)

            group_loop(act, group_tokens, mixture_slot, "m")

        @block.tensor
        def _(pe):
            mm = nc.tensor.matmul
            pe.wait_ge(S("tokw_ready"), 8)

            with pe.Fori(0, B // 4) as i:
                for u in range(2):
                    pe.wait_ge(S(f"p1_in{u}"), 16 * i + 16)
                    grid = p1_sb[:, u, :].rearrange("p (c n) -> p c n", c=PF)
                    n = 0
                    for c in range(PF):
                        for shift, (dy, dx) in enumerate(((1, 1), (1, 0), (0, 1), (0, 0))):
                            at_ = 8 * dy + dx
                            ins = mm(bank[0:TW, 2 * i + u, 0:D], grid[:, c, at_:at_ + TW], tokw_sb[:, c, 1 + shift, :],
                                     start=(n == 0), stop=(n == PF * 4 - 1))
                            n += 1
                    ins.then_inc(S("tok_mm"), 1)
            pe.wait_ge(S("weights_in"), 16 * NW)
            pe.wait_ge(S("dve_const"), 8)
            pe.wait_ge(S("pool_const"), 4)
            pe.wait_ge(S("cast_in"), 48)

            def transpose_pair(name, ready, i, src):
                for u in range(2):
                    pe.wait_ge(S(ready), pair(i, u))
                    for c in range(NK):
                        ins = nc.tensor.transpose(bank[0:KC, 4 * u, c * T:(c + 1) * T], src[:, u, c * KC:(c + 1) * KC], ident[0:T, 0:T])
                    ins.then_inc(S(name), 1)

            def transpose_group(name, g):
                pe.wait_ge(S(name + "_xs"), g + 1)
                for c in range(NK):
                    for t in range(G):
                        ins = nc.tensor.transpose(bank[0:KC, c, t * T:(t + 1) * T], xs[:, t, c * KC:(c + 1) * KC], ident[0:T, 0:T])
                ins.then_inc(S(name + "_xtmm"), 1)

            pe.wait_ge(S("bd_ready"), 1)
            with pe.Fori(0, B // 2) as i:
                transpose_pair("f_xtmm", "f_xs", i, xs)
                for u in range(2):
                    pe.wait_ge(S("f_xt"), pair(i, u))
                    for c in range(NK):
                        ins = mm(bank[0:T, 4 * u + 1 + c, 0:HPC * M], xt[0:KC, u, c, :], w_bd[:], start=True, stop=True)
                    ins.then_inc(S("f_u"), 1)
                for u in range(2):
                    pe.wait_ge(S("f_mq"), pair(i, u))
                    nc.tensor.transpose(bank[0:HEADS, 4 * u, 256:256 + T], mq[:, u, :], ident[0:T, 0:T]).then_inc(S("f_mqt"), 1)
                for u in range(2):
                    pe.wait_ge(S("f_kd"), pair(i, u))
                    mm(bank[0:T, 4 * u, 384:384 + HEADS], ones[:], kdiag[:, u, :], start=True, stop=True).then_inc(S("f_kb"), 1)
                for u in range(2):
                    pe.wait_ge(S("f_ek"), pair(i, u))
                    pe.wait_ge(S("f_va"), pair(i, u))
                    for j in range(6):
                        ins = mm(bank[:, 4 * u + 3, j * 34:(j + 1) * 34], ek[:, u, j * 128:(j + 1) * 128],
                                 va[:, u, 2 * j:2 * j + 2, :].rearrange("p a b -> p (a b)"), start=True, stop=True)
                    ins.then_inc(S("f_ctx"), 1)
                for u in range(2):
                    pe.wait_ge(S("f_eqexp"), pair(i, u))
                    for j in range(6):
                        ins = nc.tensor.transpose(bank[:, 4 * u + 1 + j // 3, (j % 3) * T:(j % 3 + 1) * T], eq[:, u, j * 128:(j + 1) * 128], ident[0:T, 0:T])
                    ins.then_inc(S("f_qt"), 1)
                for u in range(2):
                    pe.wait_ge(S("f_cb"), pair(i, u))
                    pe.wait_ge(S("f_qts"), pair(i, u))
                    for j in range(6):
                        ins = mm(bank[0:T, 4 * u + 3, 256 + j * 34:256 + (j + 1) * 34], qt_f[:, u, j * T:(j + 1) * T], cb[:, u, j, :], start=True, stop=True)
                    ins.then_inc(S("f_att"), 1)

            def hidden_chunk(n, w, g, f, count):
                if f >= 2:
                    pe.wait_ge(S(n + "_hid"), count - 1)
                for c in range(NK):
                    ins = mm(bank[:, 2 + f % 2, 0:GT], w[:, c, f * 128:(f + 1) * 128], xtg[0:KC, c, :], start=(c == 0), stop=(c == NK - 1))
                ins.then_inc(S(n + "_hmm"), 1)

            def gelu_slot(g, more):
                pe.wait_ge(S("n_xt"), g + 1)
                for f in range(FC):
                    hidden_chunk("n", w_f1, g, f, FC * g + f)
                if more:
                    transpose_group("n", g + 1)
                else:
                    pe.wait_ge(S("n_sum"), G * g)
                pe.wait_ge(S("n_hid"), FC * g + FC)
                for t in range(G):
                    for f in range(FC):
                        ins = mm(bank[0:T, 4 + t, 0:D], hid[:, f, t * T:(t + 1) * T], w_f2[:, f, :], start=(f == 0), stop=(f == FC - 1))
                    ins.then_inc(S("n_y"), 1)

            group_loop(pe, transpose_group, gelu_slot, "n")

            def encode(k):
                pe.wait_ge(S("x_xt"), k + 1)
                for c in range(NK):
                    kc = KC + (c == NK - 1)
                    ins = mm(bank[0:R0, 0, 0:GT], w_enc[0:kc, c, :], xtn[0:kc, c, :], start=(c == 0), stop=(c == NK - 1))
                ins.then_inc(S("x_encmm"), 1)

            def logits(k):
                pe.wait_ge(S("x_enc"), k + 1)
                for t in range(G):
                    ins = mm(bank[0:T, 1, t * E0:(t + 1) * E0], enct[:, t * T:(t + 1) * T], w_sw[:], start=True, stop=True)
                ins.then_inc(S("x_logits"), 1)

            def routes(k):
                pe.wait_ge(S("x_onehot"), k + 1)
                for t in range(G):
                    ins = nc.tensor.transpose(bank[0:E0, 0, t * T:(t + 1) * T], onehot[:, t, :], ident[0:T, 0:T])
                ins.then_inc(S("x_oht"), 1)

            def routed_front(n, k):
                transpose_group(n, k)
                encode(k)
                logits(k)
                routes(k)

            def routed_slot(g, more):
                pe.wait_ge(S("x_xtg"), g + 1)
                for k in range(C0):
                    hidden_chunk("x", w_x1, g, k, C0 * g + k)
                    if k == 0:
                        pe.wait_ge(S("x_ohts"), g + 1)
                    if k >= 2:
                        pe.wait_ge(S("x_masked"), C0 * g + (k - 1))
                    mm(bank[:, 6 + k % 2, 0:GT], expand[:, k * 128:(k + 1) * 128], ohtb[:], start=True, stop=True).then_inc(S("x_mask"), 1)
                    if more and k < 3:
                        if k == 0:
                            transpose_group("x", g + 1)
                        elif k == 1:
                            encode(g + 1)
                        else:
                            logits(g + 1)
                pe.wait_ge(S("x_masked"), C0 * g + C0)
                for t in range(G):
                    y = bank[0:T, 4 + t // 2, t % 2 * D:(t % 2 + 1) * D]
                    for k in range(C0):
                        mm(y, hid[:, k, t * T:(t + 1) * T], w_x2[:, k, :], start=(k == 0), stop=False)
                    ins = mm(y, oht[:, t * T:(t + 1) * T], w_xb2[:], start=False, stop=True)
                ins.then_inc(S("x_y"), 1)
                if more:
                    routes(g + 1)

            group_loop(pe, routed_front, routed_slot, "x")

            def front_tokens(n, k):
                pe.wait_ge(S(n + "_xs"), k + 1)
                for c in range(NK):
                    ins = nc.tensor.transpose(bank[0:KC, 0, c * T:(c + 1) * T], xs[:, 0, c * KC:(c + 1) * KC], ident[0:T, 0:T])
                ins.then_inc(S(n + "_xtmm"), 1)

            def front_qkv(n, w, k):
                pe.wait_ge(S(n + "_xt"), k + 1)
                for out_, col, width in ((bank[0:T, 1, 0:2 * D], 0, 2 * D), (bank[0:T, 0, 256:256 + D], 2 * D, D)):
                    for c in range(NK):
                        kc = KC + (c == NK - 1 and n == "g")
                        ins = mm(out_, xt[0:kc, 0, c, :], w[0:kc, c, col:col + width], start=(c == 0), stop=(c == NK - 1))
                ins.then_inc(S(n + "_qkv"), 1)

            def front_queries(n, k):
                pe.wait_ge(S(n + "_qk"), k + 1)
                for j in range(2 * NK):
                    ins = nc.tensor.transpose(bank[0:KC, 1, j * T:(j + 1) * T], qk[:, j * KC:(j + 1) * KC], ident[0:T, 0:T])
                ins.then_inc(S(n + "_qktmm"), 1)

            def unit_scores(n, b, q):
                pe.wait_ge(S(n + "_kbd"), UNITS * b + (q + 1))
                c = q // 2
                ins = mm(bank[0:T, 4 + q, 0:3 * T], qkt[:, c * T:(c + 1) * T], kbd[:, q, :], start=True, stop=(n == "g"))
                if n == "a":
                    ins = mm(bank[0:T, 4 + q, 0:3 * T], identb[0:T, 0:T], causal[:], start=False, stop=True)
                ins.then_inc(S(n + "_s"), 1)

            def transpose_probs(n, b, q):
                pe.wait_ge(S(n + "_p"), UNITS * b + (q + 1))
                for h in range(3):
                    ins = nc.tensor.transpose(bank[0:T, 4 + q, h * T:(h + 1) * T], pr[:, q, h * T:(h + 1) * T], ident[0:T, 0:T])
                ins.then_inc(S(n + "_pt"), 1)

            def unit_values(n, b, q):
                pe.wait_ge(S(n + "_pts"), UNITS * b + (q + 1))
                for h in range(3):
                    col = (3 * q + h) * HD
                    ins = mm(bank[0:T, 2, col:col + HD], pt[:, q, h * T:(h + 1) * T], vals[:, col:col + HD], start=True, stop=True)
                if q == UNITS - 1:
                    ins.then_inc(S(n + "_pv"), 1)

            def attention(n, w):
                def front(n, k):
                    front_tokens(n, k)
                    front_qkv(n, w, k)
                    front_queries(n, k)
                    unit_scores(n, k, 0)

                def slot(b, more):
                    pe.wait_ge(S(n + "_v"), b + 1)
                    unit_scores(n, b, 1)
                    if more:
                        front_tokens(n, b + 1)
                    unit_scores(n, b, 2)
                    unit_scores(n, b, 3)
                    if more:
                        front_qkv(n, w, b + 1)
                    transpose_probs(n, b, 0)
                    transpose_probs(n, b, 1)
                    unit_values(n, b, 0)
                    transpose_probs(n, b, 2)
                    unit_values(n, b, 1)
                    if more:
                        front_queries(n, b + 1)
                    transpose_probs(n, b, 3)
                    unit_values(n, b, 2)
                    unit_values(n, b, 3)
                    pe.wait_ge(S(n + "_at"), b + 1)
                    for c in range(NK):
                        ins = nc.tensor.transpose(bank[0:KC, 3, c * T:(c + 1) * T], at[:, 0, c * KC:(c + 1) * KC], ident[0:T, 0:T])
                    ins.then_inc(S(n + "_otmm"), 1)
                    if more:
                        unit_scores(n, b + 1, 0)
                    pe.wait_ge(S(n + "_ot"), b + 1)
                    for c in range(NK):
                        kc = KC + (c == NK - 1 and n == "g")
                        ins = mm(bank[0:T, 3, 256:256 + D], ot[0:kc, 0, c, :], w[0:kc, c, 3 * D:4 * D], start=(c == 0), stop=(c == NK - 1))
                    ins.then_inc(S(n + "_o"), 1)

                attention_loop(pe, front, slot, n)

            attention("a", w_a)
            attention("g", w_g)

            def mixture_slot(g, more):
                pe.wait_ge(S("m_xt"), g + 1)
                for t in range(G):
                    for c in range(NK):
                        kc = KC + (c == NK - 1)
                        ins = mm(bank[0:T, 1, t * E1:(t + 1) * E1], xtg[0:kc, c, t * T:(t + 1) * T], w_gate[0:kc, c, :],
                                 start=(c == 0), stop=(c == NK - 1))
                ins.then_inc(S("m_logits"), 1)
                for e in range(E1):
                    for f in range(FC):
                        if e == 1 and f == FC - 1:
                            pe.wait_ge(S("m_comb"), g + 1)
                            for t in range(G):
                                ins = nc.tensor.transpose(bank[0:E1, 0, t * T:(t + 1) * T], pe_[:, t, E1:2 * E1], ident[0:T, 0:T])
                            ins.then_inc(S("m_combt"), 1)
                        hidden_chunk("m", w_m1[:, e], g, f, E1 * FC * g + (FC * e + f))
                    if more and e == 2:
                        transpose_group("m", g + 1)
                    pe.wait_ge(S("m_hid"), E1 * FC * g + (FC * e + FC))
                    if e == 1:
                        pe.wait_ge(S("m_combts"), g + 1)
                    for t in range(G):
                        if e == 2:
                            pe.wait_ge(S("m_bsum"), 4 * g + (t + 1))
                        elif e > 0:
                            pe.wait_ge(S("m_acc"), 16 * g + (4 * e + t - 3))
                        for f in range(FC):
                            ins = mm(bank[0:T, 4 + t, 0:D], hid[:, f, t * T:(t + 1) * T], w_m2[:, e, f, :], start=(f == 0), stop=(f == FC - 1))
                        if e == 1:
                            ins = mm(bank[0:T, 4 + t, 256:256 + D], oht[0:E1, t * T:(t + 1) * T], w_mb2[:], start=True, stop=True)
                        ins.then_inc(S("m_y"), 1)
                pe.wait_ge(S("m_acc"), 16 * g + 16)

            group_loop(pe, transpose_group, mixture_slot, "m")


def kernel(**inputs):
    import numpy as np
    import concourse.bacc as bacc
    from concourse.bass_utils import run_bass_kernel_spmd

    a = {k: np.asarray(x) for k, x in inputs.items()}
    nc = bacc.Bacc("TRN2", target_bir_lowering=False, num_devices=1)
    half = 8

    def quadrant_rows(w):
        n = w.shape[0]
        w = w.reshape(n, 2, half, 2, half, 3).transpose(0, 1, 3, 2, 4, 5)
        return w.reshape(n, 2, 2, half * half * 3)

    x = a["x"].reshape(B, 3, 14, half, 14, half)
    blocks = np.arange(-1, 15) % 14
    x = x[:, :, blocks][:, :, :, :, blocks]
    x = x.reshape(B, 3, 8, 2, half, 8, 2, half).transpose(3, 6, 4, 7, 1, 0, 2, 5)
    p1 = x.reshape(PF, 128, B // 2, 2, 8, 8).transpose(2, 1, 0, 3, 4, 5).reshape(B // 2, 128, PF * 128)
    wt = quadrant_rows(a["L0_tok_W"].reshape(D * 5, 16, 16, 3)).reshape(D, 5, 2, 2, D)
    wt = np.stack([wt[:, 0, ::-1, ::-1]] + [wt[:, k] for k in range(1, 5)])
    tokw = wt.reshape(5, D, PF, 128).transpose(3, 2, 0, 1)

    def chunks(w, k=KC):
        return w.reshape(w.shape[0] // k, k, w.shape[1]).transpose(1, 0, 2)

    def with_bias(w, b):
        row = np.zeros((1, NK, w.shape[1]), w.dtype)
        row[0, NK - 1] = b
        return np.concatenate([chunks(w), row])

    vecs = np.stack([a[k] for k in (
        "L0_tok_b", "L0_tok_gamma", "L0_tok_beta", "L0_txt_ln_gamma", "L0_txt_ln_beta", "L0_attn_ln1_g",
        "L0_attn_ln1_b", "L0_attn_ln2_g", "L0_attn_ln2_b", "L0_attn_b2", "L1_ffn_ln1_g", "L1_ffn_ln1_b",
        "L1_ffn_ln2_g", "L1_ffn_ln2_b")])
    bd = np.zeros((KC, HPC * M), np.float32)
    for h in range(HPC):
        bd[h * HD:(h + 1) * HD, h * M:(h + 1) * M] = a["L0_attn_proj"].T
    angle = np.repeat(np.arange(1, T + 1)[:, None] * 10000.0 ** (-2.0 * np.arange(D // 2) / D), 2, axis=-1)
    sign = np.tile([-1.0, 1.0], D // 2)
    rope = np.stack([np.cos(angle), np.sin(angle) * sign], axis=1).astype(np.float32)
    eye = np.eye(128, dtype=np.float32)[None]
    above = np.triu(np.ones((T, T)), k=1) * -1e30
    causal = np.tile(above, (1, 3)).astype(np.float32)
    headmask = np.repeat((np.arange(KC)[:, None] // HD == np.arange(HPC))[:, :, None], T, axis=2).astype(np.float32)
    expand = np.repeat(np.eye(E0, dtype=np.float32), R0, axis=1)
    iota = np.tile(np.arange(E0, dtype=np.float32) - E0, (T, 1))
    qkvo = np.concatenate([a[f"L1_attn_W_{k}"].T for k in "qkvo"], axis=1)
    qkvo_g = np.concatenate([a[f"L1_ffn_W{k}"].T for k in "qkvo"], axis=1)
    bias_g = np.concatenate([a[f"L1_ffn_b{k}"] for k in "qkvo"])
    arrays = {
        "p1": p1, "tokw": tokw, "ids": a["x_txt"].T, "types": a["mask_BS_i1_0"].T,
        "word_emb": a["L0_txt_word_emb"], "pos_emb": a["L0_txt_pos_emb"][:TT], "type_emb": a["L0_txt_type_emb"],
        "vecs": vecs, "favor_bd": bd, "f_w1": chunks(a["L0_attn_W1"]), "f_b1": a["L0_attn_b1"].reshape(FC, 128).T,
        "f_w2": chunks(a["L0_attn_W2"], 128), "enc_w": with_bias(a["L0_ffn_enc_w"], a["L0_ffn_enc_b"]),
        "sw_w": np.concatenate([a["L0_ffn_sw_w"], a["L0_ffn_sw_b"][None]]),
        "x_w1": chunks(a["L0_ffn_w1"].transpose(1, 0, 2).reshape(D, E0 * R0)),
        "x_b1": a["L0_ffn_b1"].reshape(C0, 128).T, "x_w2": chunks(a["L0_ffn_w2"].reshape(E0 * R0, D), 128),
        "x_b2": a["L0_ffn_b2"], "a_w": chunks(qkvo), "g_w": with_bias(qkvo_g, bias_g),
        "gate_w": with_bias(a["L1_ffn_Wg"].T, a["L1_ffn_bg"]),
        "m_w1": a["L1_ffn_W1"].reshape(E1, NK, KC, F).transpose(2, 0, 1, 3),
        "m_b1": a["L1_ffn_b1"].reshape(E1, FC, 128).transpose(2, 0, 1),
        "m_w2": a["L1_ffn_W2"].reshape(E1, FC, 128, D).transpose(2, 0, 1, 3), "m_b2": a["L1_ffn_b2"],
        "gamma": a["L1_ffn_gamma"].reshape(1), "rope": rope, "ident_in": eye, "causal_in": causal,
        "headmask_in": headmask, "expand_in": expand, "iota_in": iota,
    }
    arrays = {k: np.ascontiguousarray(x) for k, x in arrays.items()}
    handles = {k: nc.dram_tensor(k, x.shape, mybir.dt.from_np(x.dtype), kind="ExternalInput").ap()
               for k, x in arrays.items()}
    out = nc.dram_tensor("out", (B, T, D), F32, kind="ExternalOutput").ap()
    program(nc, out=out, **handles)
    result = run_bass_kernel_spmd(nc, [arrays], core_ids=[0])
    return result.results[0]["out"]
```

```python
from contextlib import ExitStack

import concourse.bass as bass
from concourse import mybir

F32 = mybir.dt.float32
BF16 = mybir.dt.bfloat16
I32 = mybir.dt.int32
ALU = mybir.AluOpType
ACT = mybir.ActivationFunctionType
AX = mybir.AxisListType

B = 16
TI = 49
TW = 64 + 55
TT = 77
T = TI + TT
D = 192
KC = 96
NK = D // KC
HEADS = 12
HD = D // HEADS
HPC = KC // HD
M = 64
F = 768
FC = F // 128
G = 4
GT = G * T
NG = B // G
E0 = 8
R0 = 64
UNITS = 4
C0 = E0 * R0 // 128
E1 = 4
PF = 6
P1B = 4

(V_TOKB, V_TOKG, V_TOKBETA, V_TXTG, V_TXTB, V_L1G, V_L1B, V_L2G, V_L2B, V_FB2,
 V_N1G, V_N1B, V_N2G, V_N2B) = range(14)


def program(nc, p1, tokw, ids, types, word_emb, pos_emb, type_emb, vecs, favor_bd, f_w1, f_b1, f_w2,
            enc_w, sw_w, x_w1, x_b1, x_w2, x_b2, a_w, g_w, gate_w, m_w1, m_b1, m_w2, m_b2, gamma,
            rope, ident_in, causal_in, headmask_in, expand_in, iota_in, out):
    with ExitStack() as ctx:
        def sb(name, shape, dt=F32):
            return ctx.enter_context(nc.sbuf_tensor(name, shape, dt))

        def sem(name):
            return ctx.enter_context(nc.semaphore(name))

        bank = ctx.enter_context(nc.psum_tensor("bank", [128, 8, 512], F32))

        stream = sb("stream", [T, B, D])
        x1 = sb("x1", [T, B, D])
        vec = sb("vec", [T, 14, D])
        ident = sb("ident", [128, 128])
        identb = sb("identb", [128, 128], BF16)
        causal = sb("causal", [T, 3 * T], BF16)
        headmask = sb("headmask", [KC, HPC, T])
        ropes = sb("ropes", [T, 2, D])
        iota8 = sb("iota8", [T, E0])
        expand = sb("expand", [E0, E0 * R0], BF16)
        ones = sb("ones", [HEADS, T])
        halves = sb("halves", [T, 2, B])
        xs = sb("xs", [T, G, D])
        xt = sb("xt", [KC + 1, 2, NK, T])
        ot = sb("ot", [KC + 1, 2, NK, T])
        xtg = sb("xtg", [KC + 1, NK, GT])
        xtn = sb("xtn", [KC + 1, NK, GT])
        gamma_sb = sb("gamma_sb", [T, 1])
        gsign = sb("gsign", [T, 1])
        gabs = sb("gabs", [T, 1])
        gneg = sb("gneg", [T, 1])
        w_bd = sb("w_bd", [KC, HPC * M])
        w_f1 = sb("w_f1", [KC, NK, F])
        w_fb1 = sb("w_fb1", [128, FC])
        w_f2 = sb("w_f2", [128, FC, D])
        w_enc = sb("w_enc", [KC + 1, NK, R0])
        w_sw = sb("w_sw", [R0 + 1, E0])
        w_x1 = sb("w_x1", [KC, NK, E0 * R0])
        w_xb1 = sb("w_xb1", [128, C0])
        w_x2 = sb("w_x2", [128, C0, D])
        w_xb2 = sb("w_xb2", [E0, D])
        w_a = sb("w_a", [KC, NK, 4 * D])
        w_g = sb("w_g", [KC + 1, NK, 4 * D])
        w_gate = sb("w_gate", [KC + 1, NK, E1])
        w_mb1 = sb("w_mb1", [128, E1, FC])
        w_mb2 = sb("w_mb2", [E1, D])
        w_m1 = sb("w_m1", [KC, E1, NK, F])
        w_m2 = sb("w_m2", [128, E1, FC, D])
        work = sb("work", [128, PF * 5 * D])
        tokw_sb = work[:].rearrange("p (c s d) -> p c s d", c=PF, s=5)
        p1_sb = sb("p1_sb", [128, P1B, PF * 128])
        txt = sb("txt", [TT, B, D])
        ids_sb = sb("ids_sb", [TT, B], I32)
        types_sb = sb("types_sb", [TT, B], I32)
        pos = sb("pos", [TT, D])
        hid = work[:, 0:FC * GT].rearrange("p (f t) -> p f t", f=FC)
        acc = work[0:T, FC * GT:FC * GT + G * D].rearrange("p (t d) -> p t d", t=G)

        st = sb("st", [T, B, 6])
        mean = sb("mean", [T, B])
        rstd = sb("rstd", [T, B])
        var = sb("var", [T, B])
        msum = sb("msum", [T, B])
        mdif = sb("mdif", [T, B])

        sq = sb("sq", [T, 2, D])
        ssum = sb("ssum", [T, 2, HEADS])
        mq = sb("mq", [T, HEADS])
        qsub = sb("qsub", [T, HEADS])
        ksub = sb("ksub", [T, HEADS])
        kmax = sb("kmax", [HEADS, 1])
        kdiag = sb("kdiag", [HEADS, HEADS])
        eq = work[0:T, 0:2 * F].rearrange("p (u m) -> p u m", u=2)
        ek = work[0:T, 2 * F:4 * F].rearrange("p (u m) -> p u m", u=2)
        va = sb("va", [T, 2, HEADS, HD + 1])
        cb = sb("cb", [128, HEADS // 2, 2 * (HD + 1)])
        qt_f = work[:, 4 * F:4 * F + 6 * T]
        rden = sb("rden", [T, 2, HEADS])
        at = sb("at", [T, 2, D])

        qk = work[0:T, 0:2 * D]
        qk2 = work[0:T, 2 * D:4 * D]
        qkt = sb("qkt", [KC, 2 * NK * T])
        kbd = sb("kbd", [KC, UNITS, 3 * T])
        vals = sb("vals", [T, 2, D])
        pr = work[0:T, 1536:1536 + UNITS * 3 * T].rearrange("p (q n) -> p q n", q=UNITS)
        pt = work[0:T, 3072:3072 + UNITS * 3 * T].rearrange("p (q n) -> p q n", q=UNITS)
        st6 = sb("st6", [T, HEADS, 6])
        smax = sb("smax", [T, HEADS])
        nbias = sb("nbias", [T, HEADS])
        zscales = sb("zscales", [T, NK, HPC])
        zvar = sb("zvar", [T, NK, HPC])
        zdif = sb("zdif", [T, NK, HPC])
        zstd = sb("zstd", [T, NK, HPC])
        psums = sb("psums", [T, 2, HEADS])

        enct = sb("enct", [R0 + 1, GT])
        lg = sb("lg", [T, G, E0])
        pe_ = sb("pe_", [T, G, E0])
        hit = sb("hit", [T, G, E0])
        onehot = sb("onehot", [T, G, E0])
        one2 = sb("one2", [T, G, E0])
        gstat = sb("gstat", [T, 4, G])
        pmax = sb("pmax", [T, G])
        oht = sb("oht", [E0, GT])
        ohtb = sb("ohtb", [E0, GT], BF16)

        feps = sb("feps", [128, 1])
        mark = sb("mark", [1, 32])
        sems = {}

        def S(name):
            if name not in sems:
                sems[name] = sem(name)
            return sems[name]

        early = [(pos[:], pos_emb), (vec[:], vecs.partition_broadcast(T))]
        weights = [(ident[:], ident_in[0]), (w_bd[:], favor_bd), (w_f1[:], f_w1), (w_fb1[:], f_b1),
                   (w_f2[:], f_w2), (w_enc[:], enc_w), (w_sw[:], sw_w), (w_x1[:], x_w1), (w_xb1[:], x_b1),
                   (w_x2[:], x_w2), (w_xb2[:], x_b2), (iota8[:], iota_in), (w_a[:], a_w), (ropes[:], rope),
                   (headmask[:], headmask_in), (w_g[:], g_w), (gamma_sb[:], gamma.partition_broadcast(T)),
                   (w_gate[:], gate_w), (w_mb1[:], m_b1), (w_mb2[:], m_b2)]
        late = [(w_m1[:], m_w1), (w_m2[:], m_w2)]
        NW = len(weights)

        block = ctx.enter_context(nc.Block())

        def place_images(eng, h, j):
            eng.wait_ge(S("tok_ready"), h + 1)
            for y in range(7):
                row = 64 * j + 8 * y
                eng.dma_start(stream[7 * y:7 * y + 7, 8 * h:8 * h + 8, :].rearrange("p (n j) d -> p n j d", j=2)[:, :, j, :],
                              x1[row:row + 7, 8 * h:8 * h + 4, :]).then_inc(S(f"images_in{h}"), 16)

        @block.sync
        def _(sp):
            sp.dma_start(ids_sb[:], ids).then_inc(S("ids_in"), 16)
            sp.dma_start(types_sb[:], types).then_inc(S("ids_in"), 16)
            sp.dma_start(tokw_sb, tokw).then_inc(S("tokw_in"), 16)
            for u in range(P1B):
                sp.dma_start(p1_sb[:, u, :], p1[u]).then_inc(S(f"p1_in{u}"), 16)
                if u == 1:
                    for dst, src in early:
                        sp.dma_start(dst, src).then_inc(S("early_in"), 16)
            for k in range(P1B, B // 2):
                sp.wait_ge(S("tok_mm"), k - P1B + 1)
                sp.dma_start(p1_sb[:, k % P1B, :], p1[k]).then_inc(S(f"p1_in{k % P1B}"), 16)
            sp.wait_ge(S("txt_ready"), 1)
            sp.dma_start(stream[TI:T, :, :], txt[:]).then_inc(S("text_in"), 16)
            for h in range(2):
                place_images(sp, h, 0)
            for g in range(NG):
                sp.wait_ge(S("final"), G * g + G)
                sp.dma_start(out[G * g:G * g + G].rearrange("b t d -> t b d"), stream[:, G * g:G * g + G, :]).then_inc(S("out_done"), 16)
            sp.wait_ge(S("out_done"), 16 * NG)

        def group_loop(eng, front, slot, n):
            front(n, 0)
            with eng.Fori(0, NG - 1) as g:
                slot(g, True)
            slot(NG - 1, False)

        def inside(k):
            return not isinstance(k, int) or 0 <= k < B

        def attention_loop(eng, slot, enter=None, leave=None):
            for b in range(-3, 1):
                slot(b, b % 2)
            with eng.Fori(0, (B - 4) // 2) as i:
                if enter:
                    enter(i)
                for u in range(2):
                    slot(2 * i + (u + 1), (u + 1) % 2)
                if leave:
                    leave()
            for b in range(B - 3, B + 1):
                slot(b, b % 2)

        @block.gpsimd
        def _(pool):
            nc.gpsimd.memset(ones[:], 1.0).then_inc(S("pool_const"), 1)
            nc.gpsimd.memset(feps[:], 1e-4).then_inc(S("pool_const"), 1)
            nc.gpsimd.memset(halves[:, 0, :], -0.5).then_inc(S("pool_const"), 1)
            nc.gpsimd.memset(halves[:, 1, :], 0.5).then_inc(S("pool_const"), 1)
            pool.wait_ge(S("ids_in"), 32)
            for b in range(B):
                pool.indirect_dma_start(txt[:, b, :], None, word_emb, bass.IndirectOffsetOnAxis(ids_sb[:, b:b + 1], 0)).then_inc(S(f"words_in{b // 8}"), 16)
                pool.indirect_dma_start(stream[0:TT, b, :], None, type_emb, bass.IndirectOffsetOnAxis(types_sb[:, b:b + 1], 0)).then_inc(S(f"words_in{b // 8}"), 16)
            pool.dma_start(identb[:], ident_in[0]).then_inc(S("cast_in"), 16)
            pool.dma_start(causal[:], causal_in).then_inc(S("cast_in"), 16)
            pool.dma_start(expand[:], expand_in).then_inc(S("cast_in"), 16)
            pool.wait_ge(S("pool_const"), 4)
            rs = [0]

            def inverse_deviation(P, n, lo=0):
                rs[0] += 1
                pool.wait_ge(S("var_ready"), rs[0])
                nc.gpsimd.tensor_tensor(rstd[0:P, lo:lo + n], var[0:P, lo:lo + n], halves[0:P, 0, 0:n], ALU.pow).then_inc(S("rstd_ready"), 1)

            def unit_keys(n, k, q):
                if q == 0:
                    pool.wait_ge(S(n + "_qkt"), k + 1)
                c, half = q // 2, q % 2
                nc.gpsimd.tensor_tensor(kbd[:, q, :].rearrange("p (h t) -> p h t", t=T),
                                        qkt[:, (2 + c) * T:(3 + c) * T].unsqueeze(1).to_broadcast([KC, 3, T]),
                                        headmask[:, 3 * half:3 * half + 3, :], ALU.mult).then_inc(S(n + "_kbd"), 1)

            def deviations(b, c):
                pool.wait_ge(S("g_var"), 2 * b + (c + 1))
                nc.gpsimd.tensor_tensor(zstd[:, c, :], zvar[:, c, :], halves[:, 1, 0:HPC], ALU.pow).then_inc(S("g_std"), 1)

            def causal_slot(b, u):
                if inside(b + 1):
                    for q in range(UNITS):
                        unit_keys("a", b + 1, q)

            def standard_slot(b, u):
                if inside(b):
                    deviations(b, 1)
                if inside(b + 1):
                    unit_keys("g", b + 1, 0)
                    unit_keys("g", b + 1, 1)
                    unit_keys("g", b + 1, 2)
                    unit_keys("g", b + 1, 3)
                    deviations(b + 1, 0)

            inverse_deviation(TT, B)
            inverse_deviation(TW, B // 4)
            inverse_deviation(T, B // 2)
            inverse_deviation(TW, B // 4, 8)
            inverse_deviation(T, B // 2)
            inverse_deviation(T, B // 2, 8)
            inverse_deviation(T, B // 2, 8)

            def kernel_slot(b, u):
                if inside(b - 1):
                    pool.wait_ge(S("f_at"), b)
                    nc.gpsimd.tensor_tensor(x1[:, b - 1, :], x1[:, b - 1, :], at[:, 0, :], ALU.add).then_inc(S("f_x1sum"), 1)
                    pool.wait_ge(S("f_x1sum"), b)
                    nc.gpsimd.tensor_tensor(stream[:, b - 1, :], stream[:, b - 1, :], x1[:, b - 1, :], ALU.add).then_inc(S("f_sum"), 1)
                if inside(b + 2):
                    pool.wait_ge(S("f_xs"), b + 3)
                    nc.gpsimd.tensor_tensor(sq[:, u, :], xs[:, u, :], xs[:, u, :], ALU.mult).then_inc(S("f_sq"), 1)
                if inside(b + 1):
                    pool.wait_ge(S("f_ekexp"), b + 2)
                    nc.gpsimd.tensor_tensor(ek[:, 1 - u, :], ek[:, 1 - u, :], feps[0:T].to_broadcast([T, F]), ALU.add).then_inc(S("f_ek"), 1)

            attention_loop(pool, kernel_slot)
            inverse_deviation(T, B)
            inverse_deviation(T, B)
            inverse_deviation(T, B)
            attention_loop(pool, causal_slot)
            inverse_deviation(T, B)
            attention_loop(pool, standard_slot)
            inverse_deviation(T, B)
            with pool.Fori(0, NG) as g:
                pool.wait_ge(S("m_var"), g + 1)
                nc.gpsimd.tensor_tensor(rstd[:, 0:G], var[:, 0:G], halves[:, 0, 0:G], ALU.pow).then_inc(S("m_rstd"), 1)

        @block.vector
        def _(dve):
            count = {"n": 0, "i": None, "per": 0, "c": 0}

            def enter(i, per):
                count.update(i=i, per=per, c=0)

            def leave(trips):
                assert count["c"] == count["per"], count
                count.update(n=count["n"] + trips * count["per"], i=None, c=0)

            def done(ins):
                ins.then_inc(S("dve_step"), 1)
                if count["i"] is None:
                    count["n"] += 1
                    dve.wait_ge(S("dve_step"), count["n"])
                else:
                    count["c"] += 1
                    dve.wait_ge(S("dve_step"), count["i"] * count["per"] + (count["n"] + count["c"]))

            stats = [0]
            norms = [0]

            def moments(P, n, eps, chain, lo=0):
                st_, mean_, var_, msum_, mdif_ = (x[0:P, lo:lo + n] for x in (st, mean, var, msum, mdif))
                nc.vector.tensor_tensor(msum_, st_[:, :, 1], st_[:, :, 4], ALU.add)
                nc.vector.tensor_tensor(mdif_, st_[:, :, 1], st_[:, :, 4], ALU.subtract)
                chain(nc.vector.tensor_tensor(var_, st_[:, :, 2], st_[:, :, 5], ALU.add))
                nc.vector.tensor_scalar(mean_, msum_, 0.5, None, ALU.mult)
                chain(nc.vector.scalar_tensor_tensor(mdif_, mdif_, 0.25, mdif_, ALU.mult, ALU.mult))
                chain(nc.vector.scalar_tensor_tensor(var_, var_, 1.0 / D, mdif_, ALU.mult, ALU.add))
                return nc.vector.tensor_scalar(var_, var_, eps, None, ALU.add)

            def count_row(P, src, b):
                nc.vector.bn_stats(st[0:P, b, :], src[0:P, b, :]).then_inc(S("stats"), 1)

            def count_rows(P, n, src, lo):
                for b in range(n):
                    count_row(P, src, lo + b)
                stats[0] += n

            def deviations(P, n, eps, lo=0):
                norms[0] += 1
                dve.wait_ge(S("stats"), stats[0])
                moments(P, n, eps, done, lo).then_inc(S("var_ready"), 1)
                return norms[0]

            def norm_stats(P, n, src, eps, lo=0):
                count_rows(P, n, src, lo)
                dve.wait_ge(S("rstd_ready"), deviations(P, n, eps, lo))

            def counted_norms():
                stats[0] += B
                dve.wait_ge(S("rstd_ready"), deviations(T, B, 1e-5))

            def normalise(dst, src, P, b):
                return nc.vector.tensor_scalar(dst, src, mean[0:P, bass.ts(b, 1)], rstd[0:P, bass.ts(b, 1)],
                                               ALU.subtract, ALU.mult)

            nc.vector.memset(xt[KC:KC + 1], 1.0).then_inc(S("dve_const"), 1)
            nc.vector.memset(ot[KC:KC + 1], 1.0).then_inc(S("dve_const"), 1)
            nc.vector.memset(xtg[KC:KC + 1], 1.0).then_inc(S("dve_const"), 1)
            nc.vector.memset(xtn[KC:KC + 1], 1.0).then_inc(S("dve_const"), 1)
            nc.vector.memset(enct[R0:R0 + 1], 1.0).then_inc(S("dve_const"), 1)
            nc.vector.memset(va[:], 1.0).then_inc(S("dve_const"), 1)
            nc.vector.memset(cb[:], 0.0).then_inc(S("dve_const"), 1)
            nc.vector.memset(onehot[:], 0.0).then_inc(S("dve_const"), 1)
            dve.wait_ge(S("tokw_in"), 16)
            for shift, (c, lo, hi) in ((1, (0, 0, 128)), (1, (1, 0, 64)), (2, (1, 64, 128)), (2, (2, 0, 128)),
                                       (3, (3, 0, 128)), (3, (4, 0, 64)), (4, (4, 64, 128)), (4, (5, 0, 128))):
                w = tokw_sb[lo:hi, c, shift, :]
                nc.vector.tensor_tensor(w, w, tokw_sb[lo:hi, c, 0, :], ALU.add).then_inc(S("tokw_ready"), 1)
            dve.wait_ge(S("early_in"), 16 * len(early))

            def affine(x, P, n, g, b):
                done(nc.vector.tensor_tensor(x, x, vec[0:P, g, :].unsqueeze(1).to_broadcast([P, n, D]), ALU.mult))
                return nc.vector.tensor_tensor(x, x, vec[0:P, b, :].unsqueeze(1).to_broadcast([P, n, D]), ALU.add)

            for h in range(2):
                half = txt[:, 8 * h:8 * h + 8, :]
                dve.wait_ge(S(f"words_in{h}"), 16 * B)
                done(nc.vector.tensor_tensor(half, half, stream[0:TT, 8 * h:8 * h + 8, :], ALU.add))
                done(nc.vector.tensor_tensor(half, half, pos[:].unsqueeze(1).to_broadcast([TT, B // 2, D]), ALU.add))
                count_rows(TT, B // 2, txt, 8 * h)
            dve.wait_ge(S("rstd_ready"), deviations(TT, B, 1e-12))
            for b in range(B):
                ins = normalise(txt[:, b, :], txt[:, b, :], TT, b)
            done(ins)
            affine(txt[:], TT, B, V_TXTG, V_TXTB).then_inc(S("txt_ready"), 1)

            def images(h):
                dve.wait_ge(S("tok_mm"), 4 * h + 4)
                grids = x1[0:TW, 8 * h:8 * h + 4, :]
                done(nc.vector.tensor_tensor(grids, bank[0:TW, 4 * h:4 * h + 4, 0:D],
                                             vec[0:TW, V_TOKB, :].unsqueeze(1).to_broadcast([TW, 4, D]), ALU.add))
                norm_stats(TW, B // 4, x1, 1e-5, 8 * h)
                for b in range(8 * h, 8 * h + 4):
                    ins = normalise(x1[0:TW, b, :], x1[0:TW, b, :], TW, b)
                done(ins)
                affine(grids, TW, B // 4, V_TOKG, V_TOKBETA).then_inc(S("tok_ready"), 1)
            def first_norm(h):
                dve.wait_ge(S(f"images_in{h}"), 16 * 14)
                norm_stats(T, B // 2, stream, 1e-5, 8 * h)
                for b in range(8 * h, 8 * h + 8):
                    normalise(x1[:, b, :], stream[:, b, :], T, b).then_inc(S("f_x1"), 1)
                dve.wait_ge(S("f_x1"), 8 * h + 8)

            images(0)
            dve.wait_ge(S("text_in"), 16)
            first_norm(0)
            images(1)
            norm_stats(T, B // 2, x1, 1e-5)
            dve.wait_ge(S("weights_in"), 16 * NW)
            nc.vector.tensor_scalar(w_bd[:], w_bd[:], HD ** -0.25, None, ALU.mult).then_inc(S("bd_ready"), 1)
            done(nc.vector.tensor_scalar(gneg[:], gamma_sb[:], -1.0, None, ALU.mult))
            done(nc.vector.tensor_tensor(gabs[:], gamma_sb[:], gneg[:], ALU.max))
            done(nc.vector.tensor_scalar(gsign[:], gamma_sb[:], 0.0, None, ALU.is_ge))
            done(nc.vector.tensor_scalar(gsign[:], gsign[:], 2.0, -1.0, ALU.mult, ALU.add))


            first_norm(1)
            norm_stats(T, B // 2, x1, 1e-5, 8)

            def tokens(k, u):
                done(normalise(xs[:, u, :], x1[:, k, :], T, k))
                done(nc.vector.tensor_tensor(xs[:, u, :], xs[:, u, :], vec[:, V_L1G, :], ALU.mult))
                nc.vector.tensor_tensor(xs[:, u, :], xs[:, u, :], vec[:, V_L1B, :], ALU.add).then_inc(S("f_xs"), 1)

            def norms_of(k, u):
                dve.wait_ge(S("f_sq"), k + 1)
                done(nc.vector.tensor_reduce(ssum[:, u, :], sq[:, u, :].rearrange("p (h d) -> p h d", h=HEADS), AX.X, ALU.add))

            def per_head(x):
                return x.rearrange("p (k h) -> p k h", k=2).unsqueeze(3).to_broadcast([T, 2, HPC, M])

            feats = bank[0:T, 1:3, 0:HPC * M].rearrange("p k (h m) -> p k h m", m=M)

            def by_heads(x):
                return x.rearrange("p (k h m) -> p k h m", k=2, m=M)

            def kernel_slot(b, u):
                v = 1 - u
                if inside(b + 1):
                    dve.wait_ge(S("f_u"), b + 2)
                    nc.vector.tensor_reduce(mq[:].rearrange("p (k h) -> p k h", k=2), feats, AX.X, ALU.max).then_inc(S("f_mq"), 1)
                    dve.wait_ge(S("f_mq"), b + 2)
                    done(nc.vector.scalar_tensor_tensor(qsub[:], ssum[:, v, :], 0.125, mq[:], ALU.mult, ALU.add))
                    nc.vector.tensor_tensor(by_heads(eq[:, v, :]), feats, per_head(qsub[:]), ALU.subtract).then_inc(S("f_eq"), 1)
                if inside(b - 1):
                    dve.wait_ge(S("f_att"), b)
                    att = bank[0:T, 6, 0:6 * 34].rearrange("p (h n) -> p h n", n=17)
                    done(nc.vector.reciprocal(rden[:, 0, :], att[:, :, HD]))
                    if not inside(b + 1):
                        dve.wait_ge(S("f_x1sum"), b - 1)
                    nc.vector.tensor_tensor(at[:, 0, :].rearrange("p (h d) -> p h d", h=HEADS), att[:, :, 0:HD],
                                            rden[:, 0, :].unsqueeze(2).to_broadcast([T, HEADS, HD]), ALU.mult).then_inc(S("f_at"), 1)
                if inside(b + 1):
                    dve.wait_ge(S("f_mqt"), b + 2)
                    done(nc.vector.tensor_reduce(kmax[:], bank[0:HEADS, 0, 0:T], AX.X, ALU.max))
                    nc.vector.tensor_scalar(kdiag[:], ident[0:HEADS, 0:HEADS], kmax[:], None, ALU.mult).then_inc(S("f_kd"), 1)
                if inside(b + 2):
                    if inside(b):
                        dve.wait_ge(S("f_va"), b + 1)
                    tokens(b + 2, u)
                if inside(b + 1):
                    dve.wait_ge(S("f_kb"), b + 2)
                    done(nc.vector.scalar_tensor_tensor(ksub[:], ssum[:, v, :], 0.125, bank[0:T, 0, 384:384 + HEADS], ALU.mult, ALU.add))
                    nc.vector.tensor_tensor(by_heads(ek[:, v, :]), feats, per_head(ksub[:]), ALU.subtract).then_inc(S("f_eksub"), 1)
                if inside(b):
                    dve.wait_ge(S("f_ctx"), b + 1)
                    ctxs = bank[:, 5, 0:6 * 34].rearrange("p (j n) -> p j n", n=34)
                    nc.vector.tensor_copy(cb[0:64, :, 0:17], ctxs[0:64, :, 0:17])
                    nc.vector.tensor_copy(cb[64:128, :, 17:34], ctxs[64:128, :, 17:34]).then_inc(S("f_cb"), 1)
                if inside(b + 2):
                    norms_of(b + 2, u)
                if inside(b - 1):
                    dve.wait_ge(S("f_x1sum"), b)
                    count_row(T, x1, b - 1)

            attention_loop(dve, kernel_slot, lambda i: enter(i, 2 * 7), lambda: leave((B - 4) // 2))
            dve.wait_ge(S("f_sum"), B)

            counted_norms()

            def group_tokens(n, g):
                if n == "x":
                    src, scale = stream, None
                else:
                    src, scale = x1, (V_L2G, V_L2B) if n == "n" else (V_N1G, V_N1B)
                for t in range(G):
                    ins = normalise(xs[:, t, :], src[:, 4 * g + t, :], T, 4 * g + t)
                if scale:
                    done(ins)
                    ins = affine(xs[:], T, G, *scale)
                ins.then_inc(S(n + "_xs"), 1)

            def gelu_slot(g, more):
                if more:
                    enter(g, 2 + 4)
                    dve.wait_ge(S("n_xtmm"), g + 1)
                    group_tokens("n", g + 1)
                for t in range(G):
                    b = 4 * g + t
                    dve.wait_ge(S("n_y"), b + 1)
                    done(nc.vector.tensor_tensor(at[:, t % 2, :], bank[0:T, 4 + t, 0:D], vec[:, V_FB2, :], ALU.add))
                    nc.vector.tensor_tensor(stream[:, b, :], stream[:, b, :], at[:, t % 2, :], ALU.add).then_inc(S("n_sum"), 1)
                    dve.wait_ge(S("n_sum"), b + 1)
                    count_row(T, stream, b)
                if more:
                    leave(NG - 1)

            group_loop(dve, group_tokens, gelu_slot, "n")

            def first_of(dst, values, top):
                n = values.shape[2]
                dve_top = gstat[:, top, :].unsqueeze(2).to_broadcast([T, G, n])
                done(nc.vector.tensor_reduce(gstat[:, top, :], values, AX.X, ALU.max))
                done(nc.vector.tensor_tensor(hit[:, :, 0:n], values, dve_top, ALU.is_ge))
                done(nc.vector.tensor_tensor(hit[:, :, 0:n], hit[:, :, 0:n], iota8[:, 0:n].unsqueeze(1).to_broadcast([T, G, n]), ALU.mult))
                done(nc.vector.tensor_reduce(gstat[:, 3, :], hit[:, :, 0:n], AX.X, ALU.min))
                return nc.vector.tensor_tensor(dst, hit[:, :, 0:n], gstat[:, 3, :].unsqueeze(2).to_broadcast([T, G, n]), ALU.is_equal)

            def softmax(n, logits, name, k):
                done(nc.vector.tensor_reduce(gstat[:, 0, :], logits, AX.X, ALU.max))
                nc.vector.tensor_tensor(lg[:, :, 0:n], logits, gstat[:, 0, :].unsqueeze(2).to_broadcast([T, G, n]),
                                        ALU.subtract).then_inc(S(name + "_lg"), 1)
                dve.wait_ge(S(name + "_exp"), k)
                done(nc.vector.tensor_reduce(gstat[:, 1, :], lg[:, :, 0:n], AX.X, ALU.add))
                done(nc.vector.reciprocal(gstat[:, 1, :], gstat[:, 1, :]))
                done(nc.vector.tensor_tensor(pe_[:, :, 0:n], lg[:, :, 0:n], gstat[:, 1, :].unsqueeze(2).to_broadcast([T, G, n]), ALU.mult))

            counted_norms()

            def route_top(k):
                dve.wait_ge(S("x_logits"), k + 1)
                softmax(E0, bank[0:T, 1, 0:G * E0].rearrange("p (t e) -> p t e", e=E0), "x", k + 1)
                first_of(onehot[:], pe_[:], 2).then_inc(S("x_onehot"), 1)

            def take_routes(k):
                nc.vector.tensor_copy(pmax[:], gstat[:, 2, :])
                dve.wait_ge(S("x_oht"), k + 1)
                nc.vector.tensor_copy(oht[:], bank[0:E0, 0, 0:GT])
                nc.vector.tensor_copy(ohtb[:], bank[0:E0, 0, 0:GT]).then_inc(S("x_ohts"), 1)

            def routed_front(n, k):
                group_tokens(n, k)
                route_top(k)
                take_routes(k)

            def routed_slot(g, more):
                if more:
                    enter(g, 4 + 4)
                    dve.wait_ge(S("x_xtmm"), g + 1)
                    group_tokens("x", g + 1)
                for c in range(C0):
                    dve.wait_ge(S("x_hid"), C0 * g + (c + 1))
                    dve.wait_ge(S("x_mask"), C0 * g + (c + 1))
                    nc.vector.tensor_tensor(hid[:, c, :], hid[:, c, :], bank[:, 6 + c % 2, 0:GT], ALU.mult).then_inc(S("x_masked"), 1)
                if more:
                    route_top(g + 1)
                dve.wait_ge(S("x_ohts"), g + 1)
                dve.wait_ge(S("x_y"), g + 1)
                for t in range(G):
                    b = 4 * g + t
                    nc.vector.scalar_tensor_tensor(stream[:, b, :], bank[0:T, 4 + t // 2, t % 2 * D:(t % 2 + 1) * D], pmax[:, t:t + 1],
                                                   stream[:, b, :], ALU.mult, ALU.add).then_inc(S("x_sum"), 1)
                dve.wait_ge(S("x_sum"), G * g + G)
                if more:
                    take_routes(g + 1)
                for t in range(G):
                    count_row(T, stream, 4 * g + t)
                if more:
                    leave(NG - 1)

            group_loop(dve, routed_front, routed_slot, "x")

            counted_norms()

            def tokens(n, k):
                if n == "g":
                    normalise(x1[:, k, :], stream[:, k, :], T, k)
                normalise(xs[:, 0, :], stream[:, k, :], T, k).then_inc(S(n + "_xs"), 1)

            def queries(n, k):
                dve.wait_ge(S(n + "_qkv"), k + 1)
                raw = bank[0:T, 1, 0:2 * D]
                if n == "g":
                    nc.vector.tensor_scalar(qk[:, 0:D], raw[:, 0:D], gsign[:, 0:1], None, ALU.mult)
                    nc.vector.tensor_copy(qk[:, D:2 * D], raw[:, D:2 * D]).then_inc(S("g_qk"), 1)
                    return
                raw2 = raw.rearrange("p (n r) -> p n r", r=2)
                cos, sin = (ropes[:, j, :].unsqueeze(1).to_broadcast([T, 2, D]) for j in range(2))
                sin2 = ropes[:, 1, :].rearrange("p (n r) -> p n r", r=2)
                swapped = qk2.rearrange("p (a n r) -> p a n r", a=2, r=2)
                raw4 = raw.rearrange("p (a n r) -> p a n r", a=2, r=2)
                for r in range(2):
                    nc.vector.tensor_tensor(swapped[:, :, :, r], raw4[:, :, :, 1 - r],
                                            sin2[:, :, r].unsqueeze(1).to_broadcast([T, 2, D // 2]), ALU.mult)
                done(nc.vector.tensor_tensor(qk.rearrange("p (a d) -> p a d", a=2), raw.rearrange("p (a d) -> p a d", a=2), cos, ALU.mult))
                nc.vector.tensor_tensor(qk, qk, qk2, ALU.add).then_inc(S("a_qk"), 1)

            def unit_scores(q):
                return bank[0:T, 4 + q, 0:3 * T].rearrange("p (h t) -> p h t", t=T)

            def unit_max(q):
                return nc.vector.tensor_reduce(smax[:, 3 * q:3 * q + 3], unit_scores(q), AX.X, ALU.max)

            def causal_bias(b, q):
                dve.wait_ge(S("a_s"), UNITS * b + (q + 1))
                done(unit_max(q))
                nc.vector.tensor_scalar(nbias[:, 3 * q:3 * q + 3], smax[:, 3 * q:3 * q + 3], -HD ** -0.5, None, ALU.mult).then_inc(S("a_bias"), 1)

            def row_stats(b, q):
                dve.wait_ge(S("g_s"), UNITS * b + (q + 1))
                for h in range(3):
                    nc.vector.bn_stats(st6[:, 3 * q + h, :], bank[0:T, 4 + q, h * T:(h + 1) * T])
                return unit_max(q)

            def row_variances(c):
                rows = st6[:, HPC * c:HPC * c + HPC, :]
                nc.vector.tensor_tensor(zdif[:, c, :], rows[:, :, 1], rows[:, :, 4], ALU.subtract)
                done(nc.vector.tensor_tensor(zvar[:, c, :], rows[:, :, 2], rows[:, :, 5], ALU.add))
                done(nc.vector.scalar_tensor_tensor(zdif[:, c, :], zdif[:, c, :], T / 4.0, zdif[:, c, :], ALU.mult, ALU.mult))
                done(nc.vector.tensor_tensor(zvar[:, c, :], zvar[:, c, :], zdif[:, c, :], ALU.add))
                nc.vector.tensor_scalar(zvar[:, c, :], zvar[:, c, :], 1.0 / (HD * (T - 1)), None, ALU.mult).then_inc(S("g_var"), 1)

            def row_scales(b, c):
                dve.wait_ge(S("g_std"), 2 * b + (c + 1))
                done(nc.vector.tensor_scalar(zstd[:, c, :], zstd[:, c, :], 1e-5, None, ALU.add))
                done(nc.vector.reciprocal(zscales[:, c, :], zstd[:, c, :]))
                done(nc.vector.tensor_scalar(zscales[:, c, :], zscales[:, c, :], gabs[:, 0:1], HD ** -0.5, ALU.mult, ALU.mult))
                nc.vector.scalar_tensor_tensor(nbias[:, HPC * c:HPC * c + HPC], smax[:, HPC * c:HPC * c + HPC], -1.0,
                                               zscales[:, c, :], ALU.mult, ALU.mult).then_inc(S("g_bias"), 1)

            def copy_probs(n, b, q):
                dve.wait_ge(S(n + "_pt"), UNITS * b + (q + 1))
                nc.vector.tensor_copy(pt[:, q, :], bank[0:T, 4 + q, 0:3 * T]).then_inc(S(n + "_pts"), 1)

            def attended(n, b, u):
                dve.wait_ge(S(n + "_pv"), b + 1)
                done(nc.vector.reciprocal(rden[:, 0, :], psums[:, u, :]))
                nc.vector.tensor_tensor(at[:, 0, :].rearrange("p (h d) -> p h d", h=HEADS),
                                        bank[0:T, 2, 0:D].rearrange("p (h d) -> p h d", h=HEADS),
                                        rden[:, 0, :].unsqueeze(2).to_broadcast([T, HEADS, HD]), ALU.mult).then_inc(S(n + "_at"), 1)

            def residual(n, b):
                dve.wait_ge(S(n + "_o"), b + 1)
                res = stream if n == "a" else x1
                nc.vector.tensor_tensor(res[:, b, :], res[:, b, :], bank[0:T, 3, 256:256 + D], ALU.add).then_inc(S(n + "_sum"), 1)

            def causal_slot(b, u):
                if inside(b):
                    causal_bias(b, 2)
                    causal_bias(b, 3)
                if inside(b - 1):
                    residual("a", b - 1)
                if inside(b):
                    copy_probs("a", b, 0)
                    copy_probs("a", b, 1)
                if inside(b + 2):
                    queries("a", b + 2)
                if inside(b):
                    copy_probs("a", b, 2)
                    copy_probs("a", b, 3)
                if inside(b + 1):
                    causal_bias(b + 1, 0)
                if inside(b):
                    attended("a", b, u)
                if inside(b + 1):
                    causal_bias(b + 1, 1)
                if inside(b + 3):
                    tokens("a", b + 3)
                if inside(b - 1):
                    dve.wait_ge(S("a_sum"), b)
                    count_row(T, stream, b - 1)

            attention_loop(dve, causal_slot, lambda i: enter(i, 2 * (UNITS + 1 + 1)), lambda: leave((B - 4) // 2))
            dve.wait_ge(S("a_sum"), B)

            counted_norms()

            def standard_slot(b, u):
                if inside(b - 1):
                    residual("g", b - 1)
                if inside(b):
                    row_scales(b, 1)
                    copy_probs("g", b, 0)
                    copy_probs("g", b, 1)
                if inside(b + 2):
                    queries("g", b + 2)
                if inside(b + 3):
                    tokens("g", b + 3)
                if inside(b - 1):
                    dve.wait_ge(S("g_sum"), b)
                    count_row(T, x1, b - 1)
                if inside(b + 1):
                    row_stats(b + 1, 0)
                if inside(b):
                    copy_probs("g", b, 2)
                if inside(b + 1):
                    done(row_stats(b + 1, 1))
                if inside(b):
                    copy_probs("g", b, 3)
                if inside(b + 1):
                    row_variances(0)
                if inside(b):
                    attended("g", b, u)
                if inside(b + 1):
                    row_stats(b + 1, 2)
                    row_scales(b + 1, 0)
                    done(row_stats(b + 1, 3))
                    row_variances(1)

            attention_loop(dve, standard_slot, lambda i: enter(i, 2 * (2 * 7 + 1)), lambda: leave((B - 4) // 2))
            dve.wait_ge(S("g_sum"), B)

            counted_norms()

            def expert_sums(g, e, start):
                for t in range(G):
                    dve.wait_ge(S("m_y"), 16 * g + (4 * e + t + 1))
                    if e == 2:
                        dve.wait_ge(S("m_bsum"), 4 * g + (t + 1))
                    elif e > 0:
                        dve.wait_ge(S("m_acc"), 16 * g + (4 * e + t - 3))
                    nc.vector.scalar_tensor_tensor(acc[:, t, :], bank[0:T, 4 + t, 0:D], pe_[:, t, E1 + e:E1 + e + 1],
                                                   start[:, t, :], ALU.mult, ALU.add).then_inc(S("m_acc"), 1)

            def mixture_slot(g, more):
                if more:
                    enter(g, 16 + 2 + 1 + 3 + 1 + 2)
                dve.wait_ge(S("m_logits"), g + 1)
                softmax(E1, bank[0:T, 1, 0:G * E1].rearrange("p (t e) -> p t e", e=E1), "m", g + 1)
                p4, o1, o2 = pe_[:, :, 0:E1], onehot[:, :, 0:E1], one2[:, :, 0:E1]
                done(first_of(o1, p4, 2))
                done(nc.vector.scalar_tensor_tensor(lg[:, :, 0:E1], o1, -2.0, p4, ALU.mult, ALU.add))
                done(first_of(o2, lg[:, :, 0:E1], 2))
                done(nc.vector.tensor_tensor(o1, o1, o2, ALU.add))
                nc.vector.tensor_tensor(pe_[:, :, E1:2 * E1], o1, p4, ALU.mult).then_inc(S("m_comb"), 1)
                dve.wait_ge(S("m_comb"), g + 1)
                expert_sums(g, 0, xs)
                dve.wait_ge(S("m_combt"), g + 1)
                nc.vector.tensor_copy(oht[0:E1, :], bank[0:E1, 0, 0:GT]).then_inc(S("m_combts"), 1)
                expert_sums(g, 1, acc)
                for t in range(G):
                    dve.wait_ge(S("m_acc"), 16 * g + (4 + t + 1))
                    nc.vector.tensor_tensor(acc[:, t, :], acc[:, t, :], bank[0:T, 4 + t, 256:256 + D], ALU.add).then_inc(S("m_bsum"), 1)
                if more:
                    group_tokens("m", g + 1)
                expert_sums(g, 2, acc)
                expert_sums(g, 3, acc)
                dve.wait_ge(S("m_acc"), 16 * g + 16)
                for t in range(G):
                    ins = nc.vector.bn_stats(st[:, t, :], acc[:, t, :])
                done(ins)
                moments(T, G, 1e-5, done).then_inc(S("m_var"), 1)
                dve.wait_ge(S("m_rstd"), g + 1)
                for t in range(G):
                    ins = nc.vector.tensor_scalar(acc[:, t, :], acc[:, t, :], mean[:, t:t + 1], rstd[:, t:t + 1], ALU.subtract, ALU.mult)
                done(ins)
                done(affine(acc, T, G, V_N2G, V_N2B))
                for t in range(G):
                    nc.vector.tensor_tensor(stream[:, 4 * g + t, :], stream[:, 4 * g + t, :], acc[:, t, :], ALU.add).then_inc(S("final"), 1)
                dve.wait_ge(S("final"), G * g + G)
                if more:
                    leave(NG - 1)

            group_loop(dve, group_tokens, mixture_slot, "m")

        @block.scalar
        def _(act):
            act.wait_ge(S("early_in"), 16 * len(early))
            for dst, src in weights:
                act.dma_start(dst, src).then_inc(S("weights_in"), 16)
            act.wait_ge(S("words_in1"), 16 * B)
            act.wait_ge(S("tok_mm"), P1B)
            for dst, src in late:
                act.dma_start(dst, src).then_inc(S("late_in"), 16)
            for h in range(2):
                place_images(act, h, 1)
            act.wait_ge(S("weights_in"), 16 * NW)
            act.wait_ge(S("dve_const"), 8)
            act.wait_ge(S("pool_const"), 4)

            def group_tokens(name, g):
                act.wait_ge(S(name + "_xtmm"), g + 1)
                nc.scalar.copy(xtg[0:KC, :, :], bank[0:KC, 0:2, 0:GT]).then_inc(S(name + "_xt"), 1)

            def kernel_slot(b, u):
                if inside(b + 1):
                    act.wait_ge(S("f_eq"), b + 2)
                    nc.scalar.activation(eq[:, 1 - u, :], eq[:, 1 - u, :], ACT.Exp).then_inc(S("f_eqexp"), 1)
                if inside(b):
                    act.wait_ge(S("f_qt"), b + 1)
                    nc.scalar.activation(qt_f.rearrange("p (k n) -> p k n", k=2), bank[:, 3:5, 0:3 * T], ACT.Identity,
                                         bias=feps[:]).then_inc(S("f_qts"), 1)
                if inside(b + 2):
                    act.wait_ge(S("f_xtmm"), b + 3)
                    nc.scalar.copy(xt[0:KC, u, :, :], bank[0:KC, 7, 0:NK * T].rearrange("p (c t) -> p c t", c=NK)).then_inc(S("f_xt"), 1)
                    act.wait_ge(S("f_xs"), b + 3)
                    if inside(b):
                        act.wait_ge(S("f_ctx"), b + 1)
                    nc.scalar.copy(va[:, u, :, 0:HD], xs[:, u, :].rearrange("p (h d) -> p h d", h=HEADS)).then_inc(S("f_va"), 1)
                if inside(b + 1):
                    act.wait_ge(S("f_eksub"), b + 2)
                    nc.scalar.activation(ek[:, 1 - u, :], ek[:, 1 - u, :], ACT.Exp).then_inc(S("f_ekexp"), 1)

            attention_loop(act, kernel_slot)

            def gelu_slot(g, more):
                for f in range(FC):
                    act.wait_ge(S("n_hmm"), FC * g + (f + 1))
                    nc.scalar.activation(hid[:, f, :], bank[:, 2 + f % 2, 0:GT], ACT.Gelu, bias=w_fb1[:, f:f + 1]).then_inc(S("n_hid"), 1)
                if more:
                    group_tokens("n", g + 1)

            group_loop(act, group_tokens, gelu_slot, "n")

            def next_tokens(k):
                act.wait_ge(S("x_xtmm"), k + 1)
                nc.scalar.copy(xtn[0:KC, :, :], bank[0:KC, 0:2, 0:GT]).then_inc(S("x_xt"), 1)

            def encoded(k):
                act.wait_ge(S("x_encmm"), k + 1)
                nc.scalar.copy(enct[0:R0, :], bank[0:R0, 0, 0:GT]).then_inc(S("x_enc"), 1)

            def take_tokens(k):
                act.wait_ge(S("x_lg"), k + 1)
                nc.scalar.activation(lg[:], lg[:], ACT.Exp).then_inc(S("x_exp"), 1)
                act.wait_ge(S("x_xt"), k + 1)
                nc.scalar.copy(xtg[0:KC, :, :], xtn[0:KC, :, :]).then_inc(S("x_xtg"), 1)
                act.wait_ge(S("x_xtg"), k + 1)

            def routed_front(n, k):
                next_tokens(k)
                encoded(k)
                take_tokens(k)

            def routed_slot(g, more):
                for c in range(C0):
                    act.wait_ge(S("x_hmm"), C0 * g + (c + 1))
                    nc.scalar.activation(hid[:, c, :], bank[:, 2 + c % 2, 0:GT], ACT.Gelu, bias=w_xb1[:, c:c + 1]).then_inc(S("x_hid"), 1)
                    if more and c == 1:
                        next_tokens(g + 1)
                    if more and c == 2:
                        encoded(g + 1)
                if more:
                    take_tokens(g + 1)

            group_loop(act, routed_front, routed_slot, "x")

            def unit_exp(n, b, u, q):
                act.wait_ge(S(n + "_bias"), UNITS * b + (q + 1) if n == "a" else 2 * b + (q // 2 + 1))
                for h in range(3):
                    head = 3 * q + h
                    scale = HD ** -0.5 if n == "a" else zscales[:, head // HPC, head % HPC:head % HPC + 1]
                    ins = nc.scalar.activation(pr[:, q, h * T:(h + 1) * T], bank[0:T, 4 + q, h * T:(h + 1) * T],
                                               ACT.Exp, bias=nbias[:, head:head + 1], scale=scale, accum_out=psums[:, u, head:head + 1])
                ins.then_inc(S(n + "_p"), 1)

            def attention(n):
                def slot(b, u):
                    if inside(b + 1):
                        act.wait_ge(S(n + "_qkv"), b + 2)
                        if inside(b - 1):
                            act.wait_ge(S(n + "_pv"), b)
                        nc.scalar.copy(vals[:, 1 - u, :], bank[0:T, 0, 256:256 + D]).then_inc(S(n + "_v"), 1)
                    if inside(b) and n == "a":
                        unit_exp(n, b, u, 0)
                    if inside(b - 1):
                        act.wait_ge(S(n + "_otmm"), b)
                        nc.scalar.copy(ot[0:KC, 0, :, :], bank[0:KC, 3, 0:NK * T].rearrange("p (c t) -> p c t", c=NK)).then_inc(S(n + "_ot"), 1)
                    if inside(b + 2):
                        act.wait_ge(S(n + "_xtmm"), b + 3)
                        nc.scalar.copy(xt[0:KC, 0, :, :], bank[0:KC, 0, 0:NK * T].rearrange("p (c t) -> p c t", c=NK)).then_inc(S(n + "_xt"), 1)
                    if inside(b + 1):
                        act.wait_ge(S(n + "_qktmm"), b + 2)
                        nc.scalar.copy(qkt[:], bank[0:KC, 1, 0:2 * NK * T]).then_inc(S(n + "_qkt"), 1)
                    if inside(b):
                        for q in range(n == "a", UNITS):
                            unit_exp(n, b, u, q)

                attention_loop(act, slot)

            attention("a")
            attention("g")

            def mixture_slot(g, more):
                for e in range(E1):
                    if e == 1:
                        act.wait_ge(S("m_lg"), g + 1)
                        nc.scalar.activation(lg[:, :, 0:E1], lg[:, :, 0:E1], ACT.Exp).then_inc(S("m_exp"), 1)
                    for f in range(FC):
                        act.wait_ge(S("m_hmm"), E1 * FC * g + (FC * e + f + 1))
                        nc.scalar.activation(hid[:, f, :], bank[:, 2 + f % 2, 0:GT], ACT.Relu, bias=w_mb1[:, e, f:f + 1]).then_inc(S("m_hid"), 1)
                if more:
                    group_tokens("m", g + 1)

            group_loop(act, group_tokens, mixture_slot, "m")

        @block.tensor
        def _(pe):
            mm = nc.tensor.matmul
            pe.wait_ge(S("tokw_ready"), 8)

            with pe.Fori(0, B // 2 // P1B) as i:
                for u in range(P1B):
                    pe.wait_ge(S(f"p1_in{u}"), 16 * i + 16)
                    grid = p1_sb[:, u, :].rearrange("p (c n) -> p c n", c=PF)
                    n = 0
                    for c in range(PF):
                        for shift, (dy, dx) in enumerate(((1, 1), (1, 0), (0, 1), (0, 0))):
                            at_ = 8 * dy + dx
                            ins = mm(bank[0:TW, P1B * i + u, 0:D], grid[:, c, at_:at_ + TW], tokw_sb[:, c, 1 + shift, :],
                                     start=(n == 0), stop=(n == PF * 4 - 1))
                            n += 1
                    ins.then_inc(S("tok_mm"), 1)
            pe.wait_ge(S("weights_in"), 16 * NW)
            pe.wait_ge(S("dve_const"), 8)
            pe.wait_ge(S("pool_const"), 4)
            pe.wait_ge(S("cast_in"), 48)

            def transpose_group(name, g):
                pe.wait_ge(S(name + "_xs"), g + 1)
                for c in range(NK):
                    for t in range(G):
                        ins = nc.tensor.transpose(bank[0:KC, c, t * T:(t + 1) * T], xs[:, t, c * KC:(c + 1) * KC], ident[0:T, 0:T])
                ins.then_inc(S(name + "_xtmm"), 1)

            pe.wait_ge(S("bd_ready"), 1)
            def kernel_slot(b, u):
                v = 1 - u
                if inside(b - 1):
                    pe.wait_ge(S("f_cb"), b)
                    pe.wait_ge(S("f_qts"), b)
                    if not inside(b):
                        pe.wait_ge(S("f_at"), b - 1)
                    for j in range(6):
                        ins = mm(bank[0:T, 6, j * 34:(j + 1) * 34], qt_f[:, j * T:(j + 1) * T], cb[:, j, :], start=True, stop=True)
                    ins.then_inc(S("f_att"), 1)
                if inside(b + 1):
                    pe.wait_ge(S("f_mq"), b + 2)
                    nc.tensor.transpose(bank[0:HEADS, 0, 0:T], mq[:], ident[0:T, 0:T]).then_inc(S("f_mqt"), 1)
                if inside(b):
                    pe.wait_ge(S("f_eqexp"), b + 1)
                    for j in range(6):
                        ins = nc.tensor.transpose(bank[:, 3 + j // 3, (j % 3) * T:(j % 3 + 1) * T], eq[:, u, j * 128:(j + 1) * 128], ident[0:T, 0:T])
                    ins.then_inc(S("f_qt"), 1)
                if inside(b + 1):
                    pe.wait_ge(S("f_kd"), b + 2)
                    mm(bank[0:T, 0, 384:384 + HEADS], ones[:], kdiag[:], start=True, stop=True).then_inc(S("f_kb"), 1)
                def contexts(heads):
                    for j in heads:
                        ins = mm(bank[:, 5, j * 34:(j + 1) * 34], ek[:, u, j * 128:(j + 1) * 128],
                                 va[:, u, 2 * j:2 * j + 2, :].rearrange("p a b -> p (a b)"), start=True, stop=True)
                    return ins

                if inside(b):
                    pe.wait_ge(S("f_ek"), b + 1)
                    pe.wait_ge(S("f_va"), b + 1)
                    contexts(range(4))
                if inside(b + 2):
                    pe.wait_ge(S("f_xs"), b + 3)
                    for c in range(NK):
                        ins = nc.tensor.transpose(bank[0:KC, 7, c * T:(c + 1) * T], xs[:, u, c * KC:(c + 1) * KC], ident[0:T, 0:T])
                    ins.then_inc(S("f_xtmm"), 1)
                if inside(b):
                    contexts(range(4, 6)).then_inc(S("f_ctx"), 1)
                if inside(b + 2):
                    pe.wait_ge(S("f_xt"), b + 3)
                    if inside(b + 1):
                        pe.wait_ge(S("f_eksub"), b + 2)
                    for c in range(NK):
                        ins = mm(bank[0:T, 1 + c, 0:HPC * M], xt[0:KC, u, c, :], w_bd[:], start=True, stop=True)
                    ins.then_inc(S("f_u"), 1)

            attention_loop(pe, kernel_slot)

            def hidden_chunk(n, w, g, f, count):
                if f >= 2:
                    pe.wait_ge(S(n + "_hid"), count - 1)
                for c in range(NK):
                    ins = mm(bank[:, 2 + f % 2, 0:GT], w[:, c, f * 128:(f + 1) * 128], xtg[0:KC, c, :], start=(c == 0), stop=(c == NK - 1))
                ins.then_inc(S(n + "_hmm"), 1)

            def gelu_slot(g, more):
                pe.wait_ge(S("n_xt"), g + 1)
                for f in range(FC):
                    hidden_chunk("n", w_f1, g, f, FC * g + f)
                if more:
                    transpose_group("n", g + 1)
                else:
                    pe.wait_ge(S("n_sum"), G * g)
                pe.wait_ge(S("n_hid"), FC * g + (FC - 1))
                for t in range(G):
                    for f in range(FC):
                        if t == 0 and f == FC - 1:
                            pe.wait_ge(S("n_hid"), FC * g + FC)
                        ins = mm(bank[0:T, 4 + t, 0:D], hid[:, f, t * T:(t + 1) * T], w_f2[:, f, :], start=(f == 0), stop=(f == FC - 1))
                    ins.then_inc(S("n_y"), 1)

            group_loop(pe, transpose_group, gelu_slot, "n")

            def encode(k):
                pe.wait_ge(S("x_xt"), k + 1)
                for c in range(NK):
                    kc = KC + (c == NK - 1)
                    ins = mm(bank[0:R0, 0, 0:GT], w_enc[0:kc, c, :], xtn[0:kc, c, :], start=(c == 0), stop=(c == NK - 1))
                ins.then_inc(S("x_encmm"), 1)

            def logits(k):
                pe.wait_ge(S("x_enc"), k + 1)
                for t in range(G):
                    ins = mm(bank[0:T, 1, t * E0:(t + 1) * E0], enct[:, t * T:(t + 1) * T], w_sw[:], start=True, stop=True)
                ins.then_inc(S("x_logits"), 1)

            def routes(k):
                pe.wait_ge(S("x_onehot"), k + 1)
                for t in range(G):
                    ins = nc.tensor.transpose(bank[0:E0, 0, t * T:(t + 1) * T], onehot[:, t, :], ident[0:T, 0:T])
                ins.then_inc(S("x_oht"), 1)

            def routed_front(n, k):
                transpose_group(n, k)
                encode(k)
                logits(k)
                routes(k)

            def routed_slot(g, more):
                pe.wait_ge(S("x_xtg"), g + 1)
                for k in range(C0):
                    hidden_chunk("x", w_x1, g, k, C0 * g + k)
                    if k == 0:
                        pe.wait_ge(S("x_ohts"), g + 1)
                    if k >= 2:
                        pe.wait_ge(S("x_masked"), C0 * g + (k - 1))
                    mm(bank[:, 6 + k % 2, 0:GT], expand[:, k * 128:(k + 1) * 128], ohtb[:], start=True, stop=True).then_inc(S("x_mask"), 1)
                    if more and k == 1:
                        transpose_group("x", g + 1)
                    if more and k == 2:
                        encode(g + 1)
                pe.wait_ge(S("x_masked"), C0 * g + (C0 - 1))
                for t in range(G):
                    y = bank[0:T, 4 + t // 2, t % 2 * D:(t % 2 + 1) * D]
                    for k in range(C0):
                        if t == 0 and k == C0 - 1:
                            pe.wait_ge(S("x_masked"), C0 * g + C0)
                        mm(y, hid[:, k, t * T:(t + 1) * T], w_x2[:, k, :], start=(k == 0), stop=False)
                    ins = mm(y, oht[:, t * T:(t + 1) * T], w_xb2[:], start=False, stop=True)
                    if t == G - 1:
                        ins.then_inc(S("x_y"), 1)
                    if more and t == 0:
                        logits(g + 1)
                if more:
                    routes(g + 1)

            group_loop(pe, routed_front, routed_slot, "x")

            def tokens(n, k):
                pe.wait_ge(S(n + "_xs"), k + 1)
                if inside(k - 1):
                    pe.wait_ge(S(n + "_v"), k)
                for c in range(NK):
                    ins = nc.tensor.transpose(bank[0:KC, 0, c * T:(c + 1) * T], xs[:, 0, c * KC:(c + 1) * KC], ident[0:T, 0:T])
                ins.then_inc(S(n + "_xtmm"), 1)

            def projections(n, w, k):
                pe.wait_ge(S(n + "_xt"), k + 1)
                if inside(k - 1):
                    pe.wait_ge(S(n + "_qkt"), k)
                for out_, col, width in ((bank[0:T, 1, 0:2 * D], 0, 2 * D), (bank[0:T, 0, 256:256 + D], 2 * D, D)):
                    for c in range(NK):
                        kc = KC + (c == NK - 1 and n == "g")
                        ins = mm(out_, xt[0:kc, 0, c, :], w[0:kc, c, col:col + width], start=(c == 0), stop=(c == NK - 1))
                ins.then_inc(S(n + "_qkv"), 1)

            def queries(n, k):
                pe.wait_ge(S(n + "_qk"), k + 1)
                for j in range(2 * NK):
                    ins = nc.tensor.transpose(bank[0:KC, 1, j * T:(j + 1) * T], qk[:, j * KC:(j + 1) * KC], ident[0:T, 0:T])
                ins.then_inc(S(n + "_qktmm"), 1)

            def unit_scores(n, b, q):
                pe.wait_ge(S(n + "_kbd"), UNITS * b + (q + 1))
                c = q // 2
                ins = mm(bank[0:T, 4 + q, 0:3 * T], qkt[:, c * T:(c + 1) * T], kbd[:, q, :], start=True, stop=(n == "g"))
                if n == "a":
                    ins = mm(bank[0:T, 4 + q, 0:3 * T], identb[0:T, 0:T], causal[:], start=False, stop=True)
                ins.then_inc(S(n + "_s"), 1)

            def transpose_probs(n, b, q):
                pe.wait_ge(S(n + "_p"), UNITS * b + (q + 1))
                for h in range(3):
                    ins = nc.tensor.transpose(bank[0:T, 4 + q, h * T:(h + 1) * T], pr[:, q, h * T:(h + 1) * T], ident[0:T, 0:T])
                ins.then_inc(S(n + "_pt"), 1)

            def unit_values(n, b, u, q):
                pe.wait_ge(S(n + "_pts"), UNITS * b + (q + 1))
                for h in range(3):
                    col = (3 * q + h) * HD
                    ins = mm(bank[0:T, 2, col:col + HD], pt[:, q, h * T:(h + 1) * T], vals[:, u, col:col + HD], start=True, stop=True)
                if q == UNITS - 1:
                    ins.then_inc(S(n + "_pv"), 1)

            def attention(n, w):
                def slot(b, u):
                    if inside(b - 1):
                        pe.wait_ge(S(n + "_at"), b)
                        for c in range(NK):
                            ins = nc.tensor.transpose(bank[0:KC, 3, c * T:(c + 1) * T], at[:, 0, c * KC:(c + 1) * KC], ident[0:T, 0:T])
                        ins.then_inc(S(n + "_otmm"), 1)
                    if inside(b + 2):
                        tokens(n, b + 2)
                    if inside(b + 1):
                        queries(n, b + 1)
                    if inside(b - 1):
                        pe.wait_ge(S(n + "_ot"), b)
                        for c in range(NK):
                            kc = KC + (c == NK - 1 and n == "g")
                            ins = mm(bank[0:T, 3, 256:256 + D], ot[0:kc, 0, c, :], w[0:kc, c, 3 * D:4 * D], start=(c == 0), stop=(c == NK - 1))
                        ins.then_inc(S(n + "_o"), 1)
                    if inside(b + 2):
                        projections(n, w, b + 2)
                    if inside(b):
                        transpose_probs(n, b, 0)
                        transpose_probs(n, b, 1)
                        pe.wait_ge(S(n + "_v"), b + 1)
                        unit_values(n, b, u, 0)
                    if n == "a":
                        if inside(b):
                            transpose_probs(n, b, 2)
                            unit_values(n, b, u, 1)
                            transpose_probs(n, b, 3)
                        if inside(b + 1):
                            unit_scores(n, b + 1, 0)
                        if inside(b):
                            unit_values(n, b, u, 2)
                        if inside(b + 1):
                            unit_scores(n, b + 1, 1)
                    else:
                        if inside(b):
                            unit_values(n, b, u, 1)
                        if inside(b + 1):
                            unit_scores(n, b + 1, 0)
                            unit_scores(n, b + 1, 1)
                        if inside(b):
                            transpose_probs(n, b, 2)
                            transpose_probs(n, b, 3)
                            unit_values(n, b, u, 2)
                    if inside(b + 1) and n == "g":
                        unit_scores(n, b + 1, 2)
                    if inside(b):
                        unit_values(n, b, u, 3)
                    if inside(b + 1):
                        if n == "a":
                            unit_scores(n, b + 1, 2)
                        unit_scores(n, b + 1, 3)

                attention_loop(pe, slot)

            attention("a", w_a)
            attention("g", w_g)

            def mixture_slot(g, more):
                pe.wait_ge(S("m_xt"), g + 1)
                for t in range(G):
                    for c in range(NK):
                        kc = KC + (c == NK - 1)
                        ins = mm(bank[0:T, 1, t * E1:(t + 1) * E1], xtg[0:kc, c, t * T:(t + 1) * T], w_gate[0:kc, c, :],
                                 start=(c == 0), stop=(c == NK - 1))
                ins.then_inc(S("m_logits"), 1)
                for e in range(E1):
                    for f in range(FC):
                        if e == 1 and f == FC - 1:
                            pe.wait_ge(S("m_comb"), g + 1)
                            for t in range(G):
                                ins = nc.tensor.transpose(bank[0:E1, 0, t * T:(t + 1) * T], pe_[:, t, E1:2 * E1], ident[0:T, 0:T])
                            ins.then_inc(S("m_combt"), 1)
                        hidden_chunk("m", w_m1[:, e], g, f, E1 * FC * g + (FC * e + f))
                    if more and e == 2:
                        transpose_group("m", g + 1)
                    pe.wait_ge(S("m_hid"), E1 * FC * g + (FC * e + FC - 1))
                    if e == 1:
                        pe.wait_ge(S("m_combts"), g + 1)
                    for t in range(G):
                        if e == 2:
                            pe.wait_ge(S("m_bsum"), 4 * g + (t + 1))
                        elif e > 0:
                            pe.wait_ge(S("m_acc"), 16 * g + (4 * e + t - 3))
                        for f in range(FC):
                            if t == 0 and f == FC - 1:
                                pe.wait_ge(S("m_hid"), E1 * FC * g + (FC * e + FC))
                            ins = mm(bank[0:T, 4 + t, 0:D], hid[:, f, t * T:(t + 1) * T], w_m2[:, e, f, :], start=(f == 0), stop=(f == FC - 1))
                        if e == 1:
                            ins = mm(bank[0:T, 4 + t, 256:256 + D], oht[0:E1, t * T:(t + 1) * T], w_mb2[:], start=True, stop=True)
                        ins.then_inc(S("m_y"), 1)
                pe.wait_ge(S("m_acc"), 16 * g + 16)

            pe.wait_ge(S("late_in"), 16 * len(late))
            group_loop(pe, transpose_group, mixture_slot, "m")


def kernel(**inputs):
    import numpy as np
    import concourse.bacc as bacc
    from concourse.bass_utils import run_bass_kernel_spmd

    a = {k: np.asarray(x) for k, x in inputs.items()}
    nc = bacc.Bacc("TRN2", target_bir_lowering=False, num_devices=1)
    half = 8

    def quadrant_rows(w):
        n = w.shape[0]
        w = w.reshape(n, 2, half, 2, half, 3).transpose(0, 1, 3, 2, 4, 5)
        return w.reshape(n, 2, 2, half * half * 3)

    x = a["x"].reshape(B, 3, 14, half, 14, half)
    blocks = np.arange(-1, 15) % 14
    x = x[:, :, blocks][:, :, :, :, blocks]
    x = x.reshape(B, 3, 8, 2, half, 8, 2, half).transpose(3, 6, 4, 7, 1, 0, 2, 5)
    p1 = x.reshape(PF, 128, B // 2, 2, 8, 8).transpose(2, 1, 0, 3, 4, 5).reshape(B // 2, 128, PF * 128)
    wt = quadrant_rows(a["L0_tok_W"].reshape(D * 5, 16, 16, 3)).reshape(D, 5, 2, 2, D)
    wt = np.stack([wt[:, 0, ::-1, ::-1]] + [wt[:, k] for k in range(1, 5)])
    tokw = wt.reshape(5, D, PF, 128).transpose(3, 2, 0, 1)

    def chunks(w, k=KC):
        return w.reshape(w.shape[0] // k, k, w.shape[1]).transpose(1, 0, 2)

    def with_bias(w, b):
        row = np.zeros((1, NK, w.shape[1]), w.dtype)
        row[0, NK - 1] = b
        return np.concatenate([chunks(w), row])

    vecs = np.stack([a[k] for k in (
        "L0_tok_b", "L0_tok_gamma", "L0_tok_beta", "L0_txt_ln_gamma", "L0_txt_ln_beta", "L0_attn_ln1_g",
        "L0_attn_ln1_b", "L0_attn_ln2_g", "L0_attn_ln2_b", "L0_attn_b2", "L1_ffn_ln1_g", "L1_ffn_ln1_b",
        "L1_ffn_ln2_g", "L1_ffn_ln2_b")])
    bd = np.zeros((KC, HPC * M), np.float32)
    for h in range(HPC):
        bd[h * HD:(h + 1) * HD, h * M:(h + 1) * M] = a["L0_attn_proj"].T
    angle = np.repeat(np.arange(1, T + 1)[:, None] * 10000.0 ** (-2.0 * np.arange(D // 2) / D), 2, axis=-1)
    sign = np.tile([-1.0, 1.0], D // 2)
    rope = np.stack([np.cos(angle), np.sin(angle) * sign], axis=1).astype(np.float32)
    eye = np.eye(128, dtype=np.float32)[None]
    above = np.triu(np.ones((T, T)), k=1) * -1e30
    causal = np.tile(above, (1, 3)).astype(np.float32)
    headmask = np.repeat((np.arange(KC)[:, None] // HD == np.arange(HPC))[:, :, None], T, axis=2).astype(np.float32)
    expand = np.repeat(np.eye(E0, dtype=np.float32), R0, axis=1)
    iota = np.tile(np.arange(E0, dtype=np.float32) - E0, (T, 1))
    qkvo = np.concatenate([a[f"L1_attn_W_{k}"].T for k in "qkvo"], axis=1)
    qkvo_g = np.concatenate([a[f"L1_ffn_W{k}"].T for k in "qkvo"], axis=1)
    bias_g = np.concatenate([a[f"L1_ffn_b{k}"] for k in "qkvo"])
    arrays = {
        "p1": p1, "tokw": tokw, "ids": a["x_txt"].T, "types": a["mask_BS_i1_0"].T,
        "word_emb": a["L0_txt_word_emb"], "pos_emb": a["L0_txt_pos_emb"][:TT], "type_emb": a["L0_txt_type_emb"],
        "vecs": vecs, "favor_bd": bd, "f_w1": chunks(a["L0_attn_W1"]), "f_b1": a["L0_attn_b1"].reshape(FC, 128).T,
        "f_w2": chunks(a["L0_attn_W2"], 128), "enc_w": with_bias(a["L0_ffn_enc_w"], a["L0_ffn_enc_b"]),
        "sw_w": np.concatenate([a["L0_ffn_sw_w"], a["L0_ffn_sw_b"][None]]),
        "x_w1": chunks(a["L0_ffn_w1"].transpose(1, 0, 2).reshape(D, E0 * R0)),
        "x_b1": a["L0_ffn_b1"].reshape(C0, 128).T, "x_w2": chunks(a["L0_ffn_w2"].reshape(E0 * R0, D), 128),
        "x_b2": a["L0_ffn_b2"], "a_w": chunks(qkvo), "g_w": with_bias(qkvo_g, bias_g),
        "gate_w": with_bias(a["L1_ffn_Wg"].T, a["L1_ffn_bg"]),
        "m_w1": a["L1_ffn_W1"].reshape(E1, NK, KC, F).transpose(2, 0, 1, 3),
        "m_b1": a["L1_ffn_b1"].reshape(E1, FC, 128).transpose(2, 0, 1),
        "m_w2": a["L1_ffn_W2"].reshape(E1, FC, 128, D).transpose(2, 0, 1, 3), "m_b2": a["L1_ffn_b2"],
        "gamma": a["L1_ffn_gamma"].reshape(1), "rope": rope, "ident_in": eye, "causal_in": causal,
        "headmask_in": headmask, "expand_in": expand, "iota_in": iota,
    }
    arrays = {k: np.ascontiguousarray(x) for k, x in arrays.items()}
    handles = {k: nc.dram_tensor(k, x.shape, mybir.dt.from_np(x.dtype), kind="ExternalInput").ap()
               for k, x in arrays.items()}
    out = nc.dram_tensor("out", (B, T, D), F32, kind="ExternalOutput").ap()
    program(nc, out=out, **handles)
    result = run_bass_kernel_spmd(nc, [arrays], core_ids=[0])
    return result.results[0]["out"]
```
